# Optimizing a Trainium2 kernel written in Bass

```python
import numpy as np
import jax
import jax.numpy as jnp

def _softmax(x, axis=-1):
    return jax.nn.softmax(x, axis=axis)

def _gelu(x):
    return jax.nn.gelu(x, approximate=True)

def _silu(x):
    return jax.nn.silu(x)

def _sigmoid(x):
    return jax.nn.sigmoid(x)

def _layernorm(x, axis=-1, eps=1e-05):
    m = jnp.mean(x, axis=axis, keepdims=True)
    v = jnp.var(x, axis=axis, keepdims=True)
    return (x - m) / jnp.sqrt(v + eps)

def _scatter_add(tgt, idx, src, axis=0):
    return tgt.at[idx].add(src)

def _segment_sum(src, seg, n):
    return jax.ops.segment_sum(src, seg, n)
kernel_name = 'mk_gnn_ffn_d2_gnn_r32_9e827e'

def setup_inputs(seed: int=0):
    np.random.seed(seed)
    _w = jnp.asarray

    def _rec_inputs():
        import jax
        import jax.numpy as jnp
        _gk = jax.random.key(seed)
        x = -0.000125 + 0.9999 * jax.random.normal(jax.random.fold_in(_gk, 1), (2048, 512), jnp.float32)
        src = jax.random.randint(jax.random.fold_in(_gk, 2), (32768,), 0, 2048, jnp.int32)
        dst = jax.random.randint(jax.random.fold_in(_gk, 3), (32768,), 0, 2048, jnp.int32)
        _o = jnp.argsort(dst, stable=True)
        src = src[_o]
        dst = dst[_o]
        edge_attr_20 = 0.000389844 + 1.00025 * jax.random.normal(jax.random.fold_in(_gk, 12), (32768, 20), jnp.float32)
        edge_attr_4 = -0.00185629 + 0.998788 * jax.random.normal(jax.random.fold_in(_gk, 13), (32768, 4), jnp.float32)
        edge_weight = jax.random.uniform(jax.random.fold_in(_gk, 14), (32768,), jnp.float32, 0.0, 0.999998)
        return (x, src, dst, edge_attr_20, edge_attr_4, edge_weight)
    x, src, dst, edge_attr_20, edge_attr_4, edge_weight = _rec_inputs()

    def _L0_gnn_setup():
        import jax, jax.numpy as jnp
        import numpy as np
        N_NODES = 2048
        N_EDGES = 16384
        FEAT_DIM = 512
        EMBED_DIM = 512
        key = jax.random.key(seed)
        k1, k2, k3, k4, k5 = jax.random.split(key, 5)
        x = jax.random.normal(k1, (N_NODES, FEAT_DIM), dtype=jnp.float32)
        limit = float(np.sqrt(6.0 / (EMBED_DIM + FEAT_DIM)))
        weight = jax.random.uniform(k2, (EMBED_DIM, FEAT_DIM), dtype=jnp.float32, minval=-limit, maxval=limit)
        row = jax.random.randint(k3, (N_EDGES,), 0, N_NODES, dtype=jnp.int64)
        col = jax.random.randint(k4, (N_EDGES,), 0, N_NODES, dtype=jnp.int64)
        vals = jax.random.uniform(k5, (N_EDGES,), dtype=jnp.float32)
        return {'x': x, 'weight': weight, 'row': row, 'col': col, 'vals': vals}
    _L0_gnn_all = _L0_gnn_setup()
    _L0_gnn_in = {k: v for k, v in _L0_gnn_all.items() if k in ('weight',)}
    del _L0_gnn_all

    def _L0_ffn_setup():
        import jax, jax.numpy as jnp
        import numpy as np
        D, H, E, K = (512, 64, 8, 2)
        EPS = 1e-05

        def _ln(x, g, b):
            m = jnp.mean(x, axis=-1, keepdims=True)
            v = jnp.var(x, axis=-1, keepdims=True)
            return (x - m) * jax.lax.rsqrt(v + EPS) * g + b
        key = jax.random.key(seed)
        ks = jax.random.split(key, 12)
        s = 0.02
        return {'x': jax.random.normal(ks[0], (2, 64, D), jnp.float32), 'Wg1': jax.random.normal(ks[1], (D, 2 * E), jnp.float32) * s, 'bg1': jnp.zeros((2 * E,), jnp.float32), 'Wg2': jax.random.normal(ks[2], (2 * E, E), jnp.float32) * s, 'bg2': jnp.zeros((E,), jnp.float32), 'W1': jax.random.normal(ks[3], (E, D, H), jnp.float32) * s, 'b1': jnp.zeros((E, H), jnp.float32), 'g1': jnp.ones((E, H), jnp.float32), 'be1': jnp.zeros((E, H), jnp.float32), 'W2': jax.random.normal(ks[4], (E, H, H), jnp.float32) * s, 'b2': jnp.zeros((E, H), jnp.float32), 'g2': jnp.ones((E, H), jnp.float32), 'be2': jnp.zeros((E, H), jnp.float32), 'W3': jax.random.normal(ks[5], (E, H, D), jnp.float32) * s, 'b3': jnp.zeros((E, D), jnp.float32)}
    _L0_ffn_all = _L0_ffn_setup()
    _L0_ffn_in = {k: v for k, v in _L0_ffn_all.items() if k in ('Wg1', 'bg1', 'Wg2', 'bg2', 'W1', 'b1', 'g1', 'be1', 'W2', 'b2', 'g2', 'be2', 'W3', 'b3')}
    del _L0_ffn_all

    def _L1_gnn_setup():
        import jax, jax.numpy as jnp
        import numpy as np
        import math
        B = 128
        F = 32
        R = 20
        N = 512
        E = 8192
        LOG2 = 0.6931471805599453
        IS2 = 1.0 / math.sqrt(2.0)
        IS3 = 1.0 / math.sqrt(3.0)
        IS6 = 1.0 / math.sqrt(6.0)

        def ssp(x):
            return jax.nn.softplus(x) - LOG2
        key = jax.random.key(seed)
        ks = jax.random.split(key, 14)
        return dict(x=jax.random.normal(ks[0], (N, 4 * B), jnp.float32), idx_i=jax.random.randint(ks[1], (E,), 0, N), idx_j=jax.random.randint(ks[2], (E,), 0, N), f_ij=jax.random.normal(ks[3], (E, R), jnp.float32), rcut_ij=jax.random.uniform(ks[4], (E,), jnp.float32), Yr_ij=jax.random.normal(ks[5], (E, 4), jnp.float32), w_in2f_s=jax.random.normal(ks[6], (B, F), jnp.float32), w_in2f_v=jax.random.normal(ks[7], (B, F), jnp.float32), W1=jax.random.normal(ks[8], (R, F), jnp.float32) / math.sqrt(R), b1=jnp.zeros((F,), jnp.float32), W2=jax.random.normal(ks[9], (F, 6 * F), jnp.float32) / math.sqrt(F), b2=jnp.zeros((6 * F,), jnp.float32), w_f2o1_s=jax.random.normal(ks[10], (2 * F, B), jnp.float32), w_f2o1_v=jax.random.normal(ks[11], (2 * F, B), jnp.float32), w_f2o2_s=jax.random.normal(ks[12], (B, B), jnp.float32), w_f2o2_v=jax.random.normal(ks[13], (B, B), jnp.float32))
    _L1_gnn_all = _L1_gnn_setup()
    _L1_gnn_in = {k: v for k, v in _L1_gnn_all.items() if k in ('w_in2f_s', 'w_in2f_v', 'W1', 'b1', 'W2', 'b2', 'w_f2o1_s', 'w_f2o1_v', 'w_f2o2_s', 'w_f2o2_v')}
    del _L1_gnn_all

    def _L1_ffn_setup():
        import jax, jax.numpy as jnp
        import numpy as np
        K_ACTIVE = 2
        CAP_FACTOR = 4

        def _route(x, hash_proj, k):
            logits = jnp.einsum('td,hde->hte', x, hash_proj)
            cand = jnp.argmax(logits, axis=-1)
            scores = jnp.take_along_axis(logits, cand[..., None], axis=-1)[..., 0]
            cand_t = cand.T
            scores_t = scores.T
            top_s, top_i = jax.lax.top_k(scores_t, k)
            sel = jnp.take_along_axis(cand_t, top_i, axis=1)
            return sel

        def _moe(x, sel, W1, W2):
            T, d = x.shape
            E = W1.shape[0]
            k = sel.shape[1]
            C = CAP_FACTOR * T * k // E
            se = sel.reshape(-1)
            oh = jax.nn.one_hot(se, E, dtype=jnp.int32)
            pos = jnp.take_along_axis(jnp.cumsum(oh, axis=0) - 1, se[:, None], axis=1)[:, 0]
            keep = pos < C
            posc = jnp.where(keep, pos, 0)
            xr = jnp.repeat(x, k, axis=0)
            xr = jnp.where(keep[:, None], xr, 0.0)
            buf = jnp.zeros((E, C, d), x.dtype).at[se, posc].add(xr)
            h = jax.nn.gelu(jnp.einsum('ecd,edf->ecf', buf, W1), approximate=False)
            y = jnp.einsum('ecf,efd->ecd', h, W2)
            out = y[se, posc] * keep[:, None].astype(x.dtype)
            return out.reshape(T, k, d)
        key = jax.random.key(seed)
        k1, k2, k3, k4 = jax.random.split(key, 4)
        B, S, D, F, E, H = (4, 64, 512, 64, 64, 4)
        hidden_states = jax.random.normal(k1, (B, S, D), dtype=jnp.float32)
        hash_proj = jax.random.normal(k2, (H, D, E), dtype=jnp.float32)
        W1 = jax.random.normal(k3, (E, D, F), dtype=jnp.float32) * (1.0 / np.sqrt(D))
        W2 = jax.random.normal(k4, (E, F, D), dtype=jnp.float32) * (1.0 / np.sqrt(F))
        return {'hidden_states': hidden_states, 'hash_proj': hash_proj, 'W1': W1, 'W2': W2}
    _L1_ffn_all = _L1_ffn_setup()
    _L1_ffn_in = {k: v for k, v in _L1_ffn_all.items() if k in ('hash_proj', 'W1', 'W2')}
    del _L1_ffn_all
    return {'x': x, 'src': src, 'dst': dst, 'edge_attr_20': edge_attr_20, 'edge_attr_4': edge_attr_4, 'edge_weight': edge_weight, 'L0_gnn_weight': _L0_gnn_in['weight'], 'L0_ffn_Wg1': _L0_ffn_in['Wg1'], 'L0_ffn_bg1': _L0_ffn_in['bg1'], 'L0_ffn_Wg2': _L0_ffn_in['Wg2'], 'L0_ffn_bg2': _L0_ffn_in['bg2'], 'L0_ffn_W1': _L0_ffn_in['W1'], 'L0_ffn_b1': _L0_ffn_in['b1'], 'L0_ffn_g1': _L0_ffn_in['g1'], 'L0_ffn_be1': _L0_ffn_in['be1'], 'L0_ffn_W2': _L0_ffn_in['W2'], 'L0_ffn_b2': _L0_ffn_in['b2'], 'L0_ffn_g2': _L0_ffn_in['g2'], 'L0_ffn_be2': _L0_ffn_in['be2'], 'L0_ffn_W3': _L0_ffn_in['W3'], 'L0_ffn_b3': _L0_ffn_in['b3'], 'L1_gnn_w_in2f_s': _L1_gnn_in['w_in2f_s'], 'L1_gnn_w_in2f_v': _L1_gnn_in['w_in2f_v'], 'L1_gnn_W1': _L1_gnn_in['W1'], 'L1_gnn_b1': _L1_gnn_in['b1'], 'L1_gnn_W2': _L1_gnn_in['W2'], 'L1_gnn_b2': _L1_gnn_in['b2'], 'L1_gnn_w_f2o1_s': _L1_gnn_in['w_f2o1_s'], 'L1_gnn_w_f2o1_v': _L1_gnn_in['w_f2o1_v'], 'L1_gnn_w_f2o2_s': _L1_gnn_in['w_f2o2_s'], 'L1_gnn_w_f2o2_v': _L1_gnn_in['w_f2o2_v'], 'L1_ffn_hash_proj': _L1_ffn_in['hash_proj'], 'L1_ffn_W1': _L1_ffn_in['W1'], 'L1_ffn_W2': _L1_ffn_in['W2']}

def reference(x, src, dst, edge_attr_20, edge_attr_4, edge_weight, L0_gnn_weight, L0_ffn_Wg1, L0_ffn_bg1, L0_ffn_Wg2, L0_ffn_bg2, L0_ffn_W1, L0_ffn_b1, L0_ffn_g1, L0_ffn_be1, L0_ffn_W2, L0_ffn_b2, L0_ffn_g2, L0_ffn_be2, L0_ffn_W3, L0_ffn_b3, L1_gnn_w_in2f_s, L1_gnn_w_in2f_v, L1_gnn_W1, L1_gnn_b1, L1_gnn_W2, L1_gnn_b2, L1_gnn_w_f2o1_s, L1_gnn_w_f2o1_v, L1_gnn_w_f2o2_s, L1_gnn_w_f2o2_v, L1_ffn_hash_proj, L1_ffn_W1, L1_ffn_W2):
    import jax
    import jax.numpy as jnp

    def _L0_gnn_ref(x, weight, row, col, vals):
        import jax, jax.numpy as jnp
        import numpy as np
        N_NODES = 2048
        N_EDGES = 16384
        FEAT_DIM = 512
        EMBED_DIM = 512
        h = jnp.einsum('nf,ef->ne', x, weight)
        msgs = vals[:, None] * h[col]
        out = jax.ops.segment_sum(msgs, row, num_segments=N_NODES)
        return out

    def _L0_ffn_ref(x, Wg1, bg1, Wg2, bg2, W1, b1, g1, be1, W2, b2, g2, be2, W3, b3):
        import jax, jax.numpy as jnp
        import numpy as np
        D, H, E, K = (512, 64, 8, 2)
        EPS = 1e-05

        def _ln(x, g, b):
            m = jnp.mean(x, axis=-1, keepdims=True)
            v = jnp.var(x, axis=-1, keepdims=True)
            return (x - m) * jax.lax.rsqrt(v + EPS) * g + b
        B, S, d = x.shape
        t = x.reshape(-1, d)
        logits = jax.nn.gelu(t @ Wg1 + bg1, approximate=False) @ Wg2 + bg2
        gates_full = jax.nn.softmax(logits, axis=-1)
        topv, topi = jax.lax.top_k(gates_full, K)
        topv = topv / jnp.sum(topv, axis=-1, keepdims=True)
        cw = jnp.sum(jax.nn.one_hot(topi, E, dtype=t.dtype) * topv[..., None], axis=1)
        h = jnp.einsum('td,edh->eth', t, W1) + b1[:, None, :]
        h = jax.nn.gelu(_ln(h, g1[:, None, :], be1[:, None, :]), approximate=False)
        h = jnp.einsum('eth,ehg->etg', h, W2) + b2[:, None, :]
        h = jax.nn.gelu(_ln(h, g2[:, None, :], be2[:, None, :]), approximate=False)
        o = jnp.einsum('eth,eho->eto', h, W3) + b3[:, None, :]
        out = jnp.einsum('te,eto->to', cw, o)
        return out.reshape(B, S, -1)

    def _L1_gnn_ref(x, idx_i, idx_j, f_ij, rcut_ij, Yr_ij, w_in2f_s, w_in2f_v, W1, b1, W2, b2, w_f2o1_s, w_f2o1_v, w_f2o2_s, w_f2o2_v):
        import jax, jax.numpy as jnp
        import numpy as np
        import math
        B = 128
        F = 32
        R = 20
        N = 512
        E = 8192
        LOG2 = 0.6931471805599453
        IS2 = 1.0 / math.sqrt(2.0)
        IS3 = 1.0 / math.sqrt(3.0)
        IS6 = 1.0 / math.sqrt(6.0)

        def ssp(x):
            return jax.nn.softplus(x) - LOG2
        n = x.shape[0]
        xs = x[:, :B]
        xv = x[:, B:].reshape(n, B, 3)
        hs = xs @ w_in2f_s / math.sqrt(B)
        hv = jnp.einsum('nbc,bf->nfc', xv, w_in2f_v) / math.sqrt(B)
        s = hs[idx_j]
        v = hv[idx_j]
        ys = Yr_ij[:, 0]
        yv = Yr_ij[:, 1:4]
        t_s1 = s * ys[:, None]
        t_s2 = jnp.einsum('efc,ec->ef', v, yv) * IS3
        t_v1 = s[:, :, None] * yv[:, None, :]
        t_v2 = v * ys[:, None, None]
        t_pv = jnp.cross(v, yv[:, None, :]) * IS2
        ax, ay, az = (v[..., 0], v[..., 1], v[..., 2])
        bx, by, bz = (yv[:, None, 0:1], yv[:, None, 1:2], yv[:, None, 2:3])
        bx, by, bz = (bx[..., 0], by[..., 0], bz[..., 0])
        t_q = jnp.stack([(ax * by + ay * bx) * IS2, (ay * bz + az * by) * IS2, (2.0 * az * bz - ax * bx - ay * by) * IS6, (ax * bz + az * bx) * IS2, (ax * bx - ay * by) * IS2], axis=-1)
        h = ssp(f_ij @ W1 + b1)
        Wij = (h @ W2 + b2) * rcut_ij[:, None]
        Wf = Wij.reshape(-1, F, 6)
        edge = jnp.concatenate([(t_s1 * Wf[..., 0])[..., None], (t_s2 * Wf[..., 1])[..., None], t_v1 * Wf[..., 2:3], t_v2 * Wf[..., 3:4], t_pv * Wf[..., 4:5], t_q * Wf[..., 5:6]], axis=-1)
        agg = jax.ops.segment_sum(edge.reshape(edge.shape[0], -1), idx_i, num_segments=n).reshape(n, F, 16)
        s_in = jnp.concatenate([agg[..., 0], agg[..., 1]], axis=1)
        v_in = jnp.concatenate([agg[..., 2:5], agg[..., 5:8]], axis=1)
        os1 = s_in @ w_f2o1_s / math.sqrt(2 * F)
        ov1 = jnp.einsum('nmc,mb->nbc', v_in, w_f2o1_v) / math.sqrt(2 * F)
        os1 = ssp(os1)
        os2 = os1 @ w_f2o2_s / math.sqrt(B)
        ov2 = jnp.einsum('nbc,bd->ndc', ov1, w_f2o2_v) / math.sqrt(B)
        return jnp.concatenate([os2, ov2.reshape(n, -1)], axis=-1)

    def _L1_ffn_ref(hidden_states, hash_proj, W1, W2):
        import jax, jax.numpy as jnp
        import numpy as np
        K_ACTIVE = 2
        CAP_FACTOR = 4

        def _route(x, hash_proj, k):
            logits = jnp.einsum('td,hde->hte', x, hash_proj)
            cand = jnp.argmax(logits, axis=-1)
            scores = jnp.take_along_axis(logits, cand[..., None], axis=-1)[..., 0]
            cand_t = cand.T
            scores_t = scores.T
            top_s, top_i = jax.lax.top_k(scores_t, k)
            sel = jnp.take_along_axis(cand_t, top_i, axis=1)
            return sel

        def _moe(x, sel, W1, W2):
            T, d = x.shape
            E = W1.shape[0]
            k = sel.shape[1]
            C = CAP_FACTOR * T * k // E
            se = sel.reshape(-1)
            oh = jax.nn.one_hot(se, E, dtype=jnp.int32)
            pos = jnp.take_along_axis(jnp.cumsum(oh, axis=0) - 1, se[:, None], axis=1)[:, 0]
            keep = pos < C
            posc = jnp.where(keep, pos, 0)
            xr = jnp.repeat(x, k, axis=0)
            xr = jnp.where(keep[:, None], xr, 0.0)
            buf = jnp.zeros((E, C, d), x.dtype).at[se, posc].add(xr)
            h = jax.nn.gelu(jnp.einsum('ecd,edf->ecf', buf, W1), approximate=False)
            y = jnp.einsum('ecf,efd->ecd', h, W2)
            out = y[se, posc] * keep[:, None].astype(x.dtype)
            return out.reshape(T, k, d)
        B, S, D = hidden_states.shape
        x = hidden_states.reshape(B * S, D)
        sel = _route(x, hash_proj, K_ACTIVE)
        expert_outputs = _moe(x, sel, W1, W2)
        out = expert_outputs.mean(axis=1)
        return out.reshape(B, S, D)
    x = x + _L0_gnn_ref(_layernorm(x, axis=-1), L0_gnn_weight, src, dst, edge_weight)
    x = x + _L0_ffn_ref(_layernorm(x, axis=-1)[None], L0_ffn_Wg1, L0_ffn_bg1, L0_ffn_Wg2, L0_ffn_bg2, L0_ffn_W1, L0_ffn_b1, L0_ffn_g1, L0_ffn_be1, L0_ffn_W2, L0_ffn_b2, L0_ffn_g2, L0_ffn_be2, L0_ffn_W3, L0_ffn_b3)[0]
    x = x + _L1_gnn_ref(_layernorm(x, axis=-1), src, dst, edge_attr_20, edge_weight, edge_attr_4, L1_gnn_w_in2f_s, L1_gnn_w_in2f_v, L1_gnn_W1, L1_gnn_b1, L1_gnn_W2, L1_gnn_b2, L1_gnn_w_f2o1_s, L1_gnn_w_f2o1_v, L1_gnn_w_f2o2_s, L1_gnn_w_f2o2_v)
    x = x + _L1_ffn_ref(_layernorm(x, axis=-1)[None], L1_ffn_hash_proj, L1_ffn_W1, L1_ffn_W2)[0]
    return x

_drawn_inputs = setup_inputs


def setup_inputs(seed=0):
    import zlib

    import numpy as np

    out = dict(_drawn_inputs(seed))
    spreads = {'L0_ffn_bg1': (0.0, 0.303),
     'L0_ffn_bg2': (0.0, 0.1),
     'L0_ffn_b1': (0.0, 0.425),
     'L0_ffn_g1': (1.0, 0.6),
     'L0_ffn_be1': (0.0, 0.779),
     'L0_ffn_b2': (0.0, 0.1),
     'L0_ffn_g2': (1.0, 0.6),
     'L0_ffn_be2': (0.0, 0.494),
     'L0_ffn_b3': (0.0, 0.1),
     'L1_gnn_b1': (0.0, 0.1),
     'L1_gnn_b2': (0.0, 0.1)}
    factors = {}
    for name, (base, spread) in spreads.items():
        noise = np.random.default_rng([zlib.crc32(name.encode()), seed]).standard_normal(out[name].shape)
        drawn = base * np.exp(spread * noise) if base else spread * noise
        out[name] = jnp.asarray(drawn.astype(out[name].dtype))
    for name, factor in factors.items():
        out[name] = (out[name] * factor).astype(out[name].dtype)
    return out
```

```python
import numpy as np
import concourse.bass as bass
from concourse import mybir
from contextlib import ExitStack

FP32 = mybir.dt.float32
BF16 = mybir.dt.bfloat16
I32 = mybir.dt.int32
U32 = mybir.dt.uint32
ALU = mybir.AluOpType
ACT = mybir.ActivationFunctionType
AX = mybir.AxisListType

P = 128
N = 2048
D = 512
T = N // P
K = D // P
E = 32768
J = E // P
B = N // P
GE = 2 * P
G = E // GE + B
ET = 2 * G
REC = 28
R_W, R_Y, R_F, R_FROM, R_TO = 0, 1, 5, 25, 26
EPS = 1e-5


class Chain:

    def __init__(self, eng, sem):
        self.eng, self.sem, self.n, self.i, self.base, self.per = eng, sem, 0, None, 0, 0

    def enter(self, i, per, first=0):
        self.base, self.i, self.per, self.n = self.n, i - first, per, 0

    def leave(self, times):
        assert self.n == self.per, (self.n, self.per)
        self.n, self.i = self.base + self.per * times, None

    def step(self, ins):
        ins.then_inc(self.sem, 1)
        self.n += 1

    def wait(self):
        self.eng.wait_ge(self.sem, self.n if self.i is None else self.i * self.per + (self.base + self.n))

    def link(self, ins):
        self.step(ins)
        self.wait()


LEAD = 2


def made(eng, sem, n, lead=LEAD):
    eng.wait_ge(sem, n + 1 + lead)


def retired(eng, sem, n, ring=LEAD, lead=LEAD):
    eng.wait_ge(sem, n + 1 + lead - ring)


def allocators(nc, ctx, layer):
    def sb(name, shape, dt=FP32):
        return ctx.enter_context(nc.sbuf_tensor(f"{layer}_{name}", shape, dt))

    def sem(name):
        return nc.alloc_semaphore(f"{layer}_{name}")

    return sb, sem


def clear_semaphores(nc, before):
    nc.clear_and_free_semaphores(nc.allocated_since(before))
    nc.all_engine_barrier()


def norm_stats(nc, own, x, stats, mean, rstd, var_ready):
    V = nc.vector
    with nc.vector.Fori(0, T) as t:
        own.enter(t, 1)
        own.step(V.bn_stats(stats[:, bass.ds(t, 1), :], x[:, bass.ds(t, 1), :]))
        own.leave(T)
    own.wait()
    me, ve, mo, vo = stats[:, :, 1], stats[:, :, 2], stats[:, :, 4], stats[:, :, 5]
    own.step(V.tensor_tensor(mean, me, mo, ALU.add))
    own.link(V.tensor_tensor(rstd, me, mo, ALU.subtract))
    own.step(V.tensor_scalar(mean, mean, 0.5, None, ALU.mult))
    own.step(V.tensor_tensor(stats[:, :, 0], ve, vo, ALU.add))
    own.link(V.scalar_tensor_tensor(rstd, rstd, 0.25, rstd, ALU.mult, ALU.mult))
    own.link(V.scalar_tensor_tensor(rstd, stats[:, :, 0], 1.0 / D, rstd, ALU.mult, ALU.add))
    V.tensor_scalar(rstd, rstd, EPS, None, ALU.add).then_inc(var_ready, 1)


def build(nc, dram):
    with ExitStack() as ctx:
        sb, sem = allocators(nc, ctx, "all")
        rec_dram = nc.dram_tensor("rec_dram", [P * ET, REC], FP32, kind="Internal").ap()
        h_dram = nc.dram_tensor("h_dram", [N, D], FP32, kind="Internal").ap()
        feat_dram = nc.dram_tensor("feat_dram", [N, P], FP32, kind="Internal").ap()
        xn_dram = nc.dram_tensor("xn_dram", [N, D], FP32, kind="Internal").ap()
        tok_dram = nc.dram_tensor("tok_dram", [P * NB + 2 * N, 1], I32, kind="Internal").ap()
        y_dram = nc.dram_tensor("y_dram", [NB * P, D], FP32, kind="Internal").ap()

        x = sb("x", [P, T, D])
        ident = sb("ident", [P, P])
        iota = sb("iota", [P, P])
        edges = sb("edges", [P, ET, REC])
        from_idx = sb("from_idx", [P, ET + 16], I32)
        to_loc = sb("to_loc", [P, ET])
        group_tile = sb("group_tile", [P, G])
        group_tile_i = sb("group_tile_i", [P, G], I32)
        stats = sb("stats", [P, T, 6])
        mean = sb("mean", [P, T])
        rstd = sb("rstd", [P, T])
        shift = sb("shift", [P, T])
        neghalf = sb("neghalf", [P, P])
        bank = [ctx.enter_context(nc.psum_tensor(f"bank{k}", [P, 512], FP32)) for k in range(8)]

        v = {**dram, **locals()}
        before = nc.snapshot_sems()
        layer0_prepare(nc, v)
        layer0_edges(nc, v)
        layer0_ffn(nc, v)
        clear_semaphores(nc, before)
        with ExitStack() as layer1:
            v["hT"] = layer1.enter_context(nc.sbuf_tensor("hT", [P, F * ET], FP32))
            v["agg"] = layer1.enter_context(nc.sbuf_tensor("agg", [P, T, 8 * F], FP32))
            layer1_features(nc, v)
            layer1_edges(nc, v)
            layer1_nodes(nc, v)
        with ExitStack() as ffn1:
            def sb(name, shape, dt):
                return ffn1.enter_context(nc.sbuf_tensor(name, shape, dt))

            v["tok_idx"] = sb("tok_idx", [P, NB + 16], I32)
            v["y_idx"] = sb("y_idx", [P, 2 * T + 16], I32)
            v["gain"] = sb("gain", [P, 2 * T], FP32)
            v["block_expert"] = sb("block_expert", [P, NB], I32)
            layer1_route(nc, v)
            layer1_experts(nc, v)
            layer1_combine(nc, v)


def layer0_prepare(nc, v):
    x_in, to_in, from_in, rec_in, wg_in = (v[k] for k in ("x_in", "to_in", "from_in", "rec_in", "wg_in"))
    x, ident, iota, edges, from_idx, to_loc = (v[k] for k in ("x", "ident", "iota", "edges", "from_idx", "to_loc"))
    group_tile, group_tile_i = v["group_tile"], v["group_tile_i"]
    stats, mean, rstd, neghalf, bank = v["stats"], v["mean"], v["rstd"], v["neghalf"], v["bank"]
    rec_dram, h_dram = v["rec_dram"], v["h_dram"]
    with ExitStack() as ctx:
        sb, sem = allocators(nc, ctx, "prepare")
        rec = sb("rec", [P, J, REC])
        from_i, to_i, bkt_i = (sb(n, [P, J], I32) for n in ("from_i", "to_i", "bkt_i"))
        bkt = sb("bkt", [P, J])
        h = sb("h", [P, T, D])
        h_flat = h[:, :, :].rearrange("p t d -> p (t d)")
        mask = h_flat[:, 0:B * J].rearrange("p (b j) -> p b j", b=B)
        scan = h_flat[:, B * J:2 * B * J]
        ones_row = sb("ones_row", [P, B * J], BF16)
        pos = sb("pos", [P, J])
        pos_i, slot_i = (sb(n, [P, J], I32) for n in ("pos_i", "slot_i"))
        iota_b = sb("iota_b", [P, B])
        iota_g = sb("iota_g", [P, G])
        ones = sb("ones", [P, P])
        lower = sb("lower", [P, P])
        small = sb("small", [P, 7, B])
        cnt, lscan, pre, tot, adj, ng, gend = (small[:, k, :] for k in range(7))
        ng_i = sb("ng_i", [P, B], I32)
        gmask = sb("gmask", [P, G, B])
        STAGES = 4
        stage_rec = sb("stage_rec", [P, STAGES, 4, REC])
        stage_pos = sb("stage_pos", [P, STAGES, 4], I32)
        wg = sb("wg", [P, K, D])
        xn = [sb(f"xn{u}", [P, D]) for u in range(2)]
        xT = [sb(f"xT{u}", [P, K, P]) for u in range(2)]

        ends_in, rec_landed, x_landed, wg_landed = (sem(n) for n in ("ends_in", "rec_landed", "x_landed", "wg_landed"))
        consts_made, pool_own, dve_own = sem("consts_made"), sem("pool_own"), sem("dve_own")
        ends_filled, cnt_ready, sums_ready, pos_ready = (
            sem(n) for n in ("ends_filled", "cnt_ready", "sums_ready", "pos_ready"))
        pad_made, pad_written, stage_full, gate, rec_sorted = (
            sem(n) for n in ("pad_made", "pad_written", "stage_full", "gate", "rec_sorted"))
        stage_sent = [sem(f"stage_sent{q}") for q in range(STAGES)]
        edges_in, var_ready, rstd_ready = (sem(n) for n in ("edges_in", "var_ready", "rstd_ready"))
        xn_ready, xT_ps, xT_ready, h_ps, h_ready, h_stored = (
            sem(n) for n in ("xn_ready", "xT_ps", "xT_ready", "h_ps", "h_ready", "h_stored"))
        block = ctx.enter_context(nc.Block())

        @block.sync
        def _(sp):
            sp.dma_start(to_i[:, :], to_in.rearrange("(p j) -> p j", p=P)).then_inc(ends_in, 16)
            sp.dma_start(from_i[:, :], from_in.rearrange("(p j) -> p j", p=P)).then_inc(ends_in, 16)
            sp.dma_start(x[:, :, :], x_in.rearrange("(t p) d -> p t d", p=P)).then_inc(x_landed, 16)
            sp.dma_start(rec[:, :, :], rec_in.rearrange("(p j) c -> p j c", p=P)).then_inc(rec_landed, 16)
            sp.dma_start(wg[:, :, :], wg_in.rearrange("(k p) e -> p k e", p=P)).then_inc(wg_landed, 16)
            with sp.Fori(0, T) as t:
                made(sp, h_ready, t)
                sp.dma_start(h_dram[bass.ds(t * P, P), :], h[:, bass.ds(t, 1), :].rearrange("p a d -> p (a d)")).then_inc(h_stored, 16)
            sp.wait_ge(rec_sorted, 1)
            sp.dma_start(edges[:, :, :].rearrange("p t c -> p (t c)"), rec_dram.rearrange("(p t) c -> p (t c)", p=P)).then_inc(edges_in, 16)
            sp.wait_ge(h_stored, 16 * T)
            sp.wait_ge(edges_in, 16)

        @block.gpsimd
        def _(gp):
            own = Chain(gp, pool_own)
            nc.gpsimd.iota(iota[:, :], [[1, P]], base=0, channel_multiplier=0, allow_small_or_imprecise_dtypes=True).then_inc(consts_made, 1)
            nc.gpsimd.iota(iota_b[:, :], [[1, B]], base=0, channel_multiplier=0, allow_small_or_imprecise_dtypes=True).then_inc(consts_made, 1)
            nc.gpsimd.iota(iota_g[:, :], [[1, G]], base=0, channel_multiplier=0, allow_small_or_imprecise_dtypes=True).then_inc(consts_made, 1)
            nc.gpsimd.memset(ones_row[:, :], 1.0).then_inc(consts_made, 1)
            nc.gpsimd.memset(neghalf[:, :], -0.5).then_inc(consts_made, 1)
            own.step(nc.gpsimd.memset(ones[:, :], 1.0))
            own.step(nc.gpsimd.memset(ident[:, :], 0.0))
            own.link(nc.gpsimd.memset(edges[:, :, :], 0.0))
            nc.gpsimd.memset(edges[:, :, R_TO:R_TO + 1], -1.0).then_inc(pad_made, 1)
            nc.gpsimd.affine_select(out=lower[:, :], in_=ones[:, :], compare_op=ALU.is_gt, fill=0.0, base=0,
                                    pattern=[[1, P]], channel_multiplier=-1).then_inc(consts_made, 1)
            nc.gpsimd.affine_select(out=ident[:, :], in_=ident[:, :], compare_op=ALU.not_equal, fill=1.0, base=0,
                                    pattern=[[-1, P]], channel_multiplier=1).then_inc(consts_made, 1)
            gp.wait_ge(pad_made, 1)
            gp.dma_start(rec_dram.rearrange("(p t) c -> p (t c)", p=P), edges[:, :, :].rearrange("p t c -> p (t c)")).then_inc(pad_written, 16)
            gp.wait_ge(var_ready, 1)
            nc.gpsimd.tensor_tensor(rstd[:, :], rstd[:, :], neghalf[:, 0:T], ALU.pow).then_inc(rstd_ready, 1)
            gp.wait_ge(ends_filled, 2)
            gp.wait_ge(pos_ready, 1)
            def place(j, q, refill):
                if refill:
                    gp.wait_ge(stage_sent[q], j * 64)
                    gp.sem_inc(gate, 1)
                at = (j * STAGES + q) * 4
                nc.gpsimd.tensor_copy(stage_rec[:, q, :, :], rec[:, bass.ds(at, 4), :]).then_inc(stage_full, 1)
                nc.gpsimd.tensor_copy(stage_pos[:, q, :], pos_i[:, bass.ds(at, 4)]).then_inc(stage_full, 1)
                gp.wait_ge(stage_full, (j * STAGES + q) * 2 + 2)
                gp.sem_inc(gate, 1)
                for k in range(4):
                    gp.indirect_dma_start(out=rec_dram, in_=stage_rec[:, q, k, :], in_offset=None,
                                          out_offset=bass.IndirectOffsetOnAxis(ap=stage_pos[:, q, k:k + 1], axis=0)
                                          ).then_inc(stage_sent[q], 16)

            gp.wait_ge(pad_written, 16)
            for q in range(STAGES):
                place(0, q, False)
            with gp.Fori(1, J // 4 // STAGES) as j:
                for q in range(STAGES):
                    place(j, q, True)
            for q in range(STAGES):
                gp.wait_ge(stage_sent[q], 16 * J // STAGES)
            gp.sem_inc(rec_sorted, 1)

        @block.vector
        def _(dve):
            own = Chain(dve, dve_own)
            V = nc.vector
            dve.sem_inc(xn_ready, LEAD)
            dve.sem_inc(h_ready, LEAD)
            dve.wait_ge(ends_in, 32)
            own.link(V.tensor_scalar(bkt_i[:, :], to_i[:, :], 7, None, ALU.arith_shift_right))
            own.link(V.tensor_copy(bkt[:, :], bkt_i[:, :]))
            dve.wait_ge(consts_made, 7)
            own.link(V.tensor_tensor(mask, bkt[:, :].unsqueeze(1).broadcast_to([P, B, J]),
                                     iota_b[:, :].unsqueeze(2).broadcast_to([P, B, J]), ALU.is_equal))
            V.tensor_reduce(cnt, mask, AX.X, ALU.add).then_inc(cnt_ready, 1)
            own.link(V.tensor_tensor_scan(scan, ones_row[:, :], h_flat[:, 0:B * J], 0.0, ALU.mult, ALU.add))
            dve.wait_ge(cnt_ready, 1)
            own.step(V.tensor_tensor_scan(lscan, ones_row[:, 0:B], cnt, 0.0, ALU.mult, ALU.add))
            dve.wait_ge(sums_ready, 1)
            own.link(V.tensor_copy(small[:, 2:4, :], bank[7][:, 0:2 * B].rearrange("p (a b) -> p a b", a=2)))
            own.link(V.tensor_scalar(ng_i[:, :], tot, float(GE - 1), None, ALU.add))
            own.link(V.tensor_scalar(ng_i[:, :], ng_i[:, :], GE.bit_length() - 1, None, ALU.arith_shift_right))
            own.link(V.tensor_copy(ng, ng_i[:, :]))
            own.link(V.tensor_tensor_scan(gend, ones_row[:, 0:B], ng, 0.0, ALU.mult, ALU.add))
            own.link(V.tensor_tensor(adj, gend, ng, ALU.subtract))
            own.link(V.scalar_tensor_tensor(adj, adj, float(GE), pre, ALU.mult, ALU.add))
            own.link(V.tensor_tensor(adj, adj, cnt, ALU.add))
            own.link(V.scalar_tensor_tensor(adj, adj, -1.0, lscan, ALU.add, ALU.subtract))
            sc3 = scan.rearrange("p (b j) -> p b j", b=B)
            own.link(V.tensor_tensor(sc3, sc3, adj.unsqueeze(2).broadcast_to([P, B, J]), ALU.add))
            own.link(V.tensor_tensor(sc3, sc3, mask, ALU.mult))
            own.link(V.tensor_reduce(pos[:, :], scan.rearrange("p (b j) -> p j b", b=B), AX.X, ALU.add))
            own.link(V.tensor_copy(slot_i[:, :], pos[:, :]))
            own.step(V.tensor_scalar(pos_i[:, :], slot_i[:, :], P - 1, None, ALU.bitwise_and))
            own.link(V.tensor_scalar(slot_i[:, :], slot_i[:, :], P.bit_length() - 1, None, ALU.arith_shift_right))
            V.scalar_tensor_tensor(pos_i[:, :], pos_i[:, :], float(ET), slot_i[:, :], ALU.mult, ALU.add).then_inc(pos_ready, 1)
            own.link(V.tensor_tensor(gmask[:, :, :], iota_g[:, :].unsqueeze(2).broadcast_to([P, G, B]),
                                     gend.unsqueeze(1).broadcast_to([P, G, B]), ALU.is_ge))
            own.link(V.tensor_reduce(group_tile[:, :], gmask[:, :, :], AX.X, ALU.add))
            own.link(V.tensor_scalar(group_tile[:, :], group_tile[:, :], float(B - 1), None, ALU.min))
            own.link(V.tensor_copy(group_tile_i[:, :], group_tile[:, :]))
            dve.wait_ge(rec_landed, 16)
            V.tensor_copy(rec[:, :, R_FROM], from_i[:, :]).then_inc(ends_filled, 1)
            V.tensor_copy(rec[:, :, R_TO], to_i[:, :]).then_inc(ends_filled, 1)
            dve.wait_ge(x_landed, 16)
            norm_stats(nc, own, x, stats, mean[:, :], rstd[:, :], var_ready)
            dve.wait_ge(rstd_ready, 1)
            with dve.Fori(0, T // 2) as i:
                for u in range(2):
                    t = i * 2 + u
                    retired(dve, xT_ps, t)
                    V.tensor_scalar(xn[u][:, :], x[:, bass.ds(t, 1), :].rearrange("p a d -> p (a d)"),
                                    mean[:, bass.ds(t, 1)], rstd[:, bass.ds(t, 1)],
                                    ALU.subtract, ALU.mult).then_inc(xn_ready, 1)
                for u in range(2):
                    t = i * 2 + u
                    made(dve, h_ps, t)
                    V.tensor_copy(h[:, bass.ds(t, 1), :].rearrange("p a d -> p (a d)"), bank[2 + u][:, :]).then_inc(h_ready, 1)

        @block.scalar
        def _(act):
            act.sem_inc(xT_ready, LEAD)
            with act.Fori(0, T // 2) as i:
                for u in range(2):
                    t = i * 2 + u
                    made(act, xT_ps, t)
                    retired(act, h_ps, t)
                    nc.scalar.activation(xT[u][:, :, :].rearrange("p k n -> p (k n)"), bank[u][:, :], ACT.Copy).then_inc(xT_ready, 1)

        @block.tensor
        def _(pe):
            pe.sem_inc(xT_ps, LEAD)
            pe.sem_inc(h_ps, LEAD)
            pe.wait_ge(consts_made, 7)
            pe.wait_ge(cnt_ready, 1)
            nc.tensor.matmul(bank[7][:, 0:B], lower[:, :], cnt, start=True, stop=True)
            nc.tensor.matmul(bank[7][:, B:2 * B], ones[:, :], cnt, start=True, stop=True).then_inc(sums_ready, 1)
            pe.wait_ge(wg_landed, 16)
            with pe.Fori(0, T // 2) as i:
                for u in range(2):
                    t = i * 2 + u
                    made(pe, xn_ready, t)
                    retired(pe, xT_ready, t)
                    for k in range(K):
                        last = nc.tensor.transpose(bank[u][:, k * P:(k + 1) * P], xn[u][:, k * P:(k + 1) * P], ident[:, :])
                    last.then_inc(xT_ps, 1)
                for u in range(2):
                    t = i * 2 + u
                    made(pe, xT_ready, t)
                    retired(pe, h_ready, t)
                    for k in range(K):
                        last = nc.tensor.matmul(bank[2 + u][:, :], xT[u][:, k, :], wg[:, k, :], start=(k == 0), stop=(k == K - 1))
                    last.then_inc(h_ps, 1)


def gather_quads(nc, gp, s, gathered, quads, tiles, rows, idx, from_idx, table, used, per):
    def copy_idx(n, q):
        nc.gpsimd.tensor_copy(idx[q][:, :], from_idx[:, bass.ds(n * 4, 4)]).then_inc(s["idx_ready"], 1)

    def quad(i, q, first):
        n = i * quads + q
        gp.wait_ge(used, (n + 1) * per)
        gp.sem_inc(s["gate"], 1)
        gp.wait_ge(s["idx_ready"], n + 1)
        gp.sem_inc(s["gate"], 1)
        for r in range(4):
            gp.indirect_dma_start(out=rows[q][:, r, :], out_offset=None, in_=table,
                                  in_offset=bass.IndirectOffsetOnAxis(ap=idx[q][:, r:r + 1], axis=0)).then_inc(gathered[q], 16)
        if not (first and q < quads // 2):
            b = (q + quads // 2) % quads
            gp.wait_ge(gathered[b], i * 64 + (64 if q >= quads // 2 else 0))
            gp.sem_inc(s["gate"], 1)
            copy_idx(n + quads // 2, b)

    for q in range(quads):
        copy_idx(q, q)
    for q in range(quads):
        quad(0, q, True)
    with gp.Fori(1, tiles // 4 // quads) as i:
        for q in range(quads):
            quad(i, q, False)


def layer0_edges(nc, v):
    x, iota, edges, from_idx, to_loc = (v[k] for k in ("x", "iota", "edges", "from_idx", "to_loc"))
    group_tile, group_tile_i, bank, h_dram = v["group_tile"], v["group_tile_i"], v["bank"], v["h_dram"]
    QUADS = 4
    RING = 4 * QUADS
    with ExitStack() as ctx:
        sb, sem = allocators(nc, ctx, "edges0")
        rows = [sb(f"rows{q}", [P, 4, D]) for q in range(QUADS)]
        idx = [sb(f"idx{q}", [P, 4], I32) for q in range(QUADS)]
        S = [sb(f"S{r}", [P, P]) for r in range(4)]
        x_flat = x[:, :, :].rearrange("p t d -> p (t d)")
        prepared = sem("prepared")
        s = {n: sem(n) for n in ("idx_ready", "gate")}
        gathered = [sem(f"gathered{q}") for q in range(QUADS)]
        S_ready, sum_ready, sum_added = sem("S_ready"), sem("sum_ready"), sem("sum_added")
        block = ctx.enter_context(nc.Block())

        @block.vector
        def _(dve):
            V = nc.vector
            dve.sem_inc(S_ready, 4)
            dve.sem_inc(sum_added, LEAD)
            V.memset(from_idx[:, ET:], 0).then_inc(prepared, 1)
            V.tensor_copy(from_idx[:, 0:ET], edges[:, :, R_FROM]).then_inc(prepared, 1)
            e_to = edges[:, :, R_TO].rearrange("p (g k) -> p g k", k=2)
            V.scalar_tensor_tensor(to_loc[:, :].rearrange("p (g k) -> p g k", k=2),
                                   group_tile[:, :].unsqueeze(2).broadcast_to([P, G, 2]), -float(P), e_to,
                                   ALU.mult, ALU.add).then_inc(prepared, 1)
            dve.wait_ge(prepared, 3)
            with dve.Fori(0, G // 2) as i:
                for u in range(2):
                    g = i * 2 + u
                    for k in range(2):
                        if k == 0:
                            retired(dve, sum_ready, g, lead=RING // 2)
                        s = g * 2 + k
                        V.tensor_scalar(S[2 * u + k][:, :], iota[:, :], to_loc[:, bass.ds(s, 1)],
                                        edges[:, bass.ds(s, 1), R_W], ALU.is_equal, ALU.mult).then_inc(S_ready, 1)
                for u in range(2):
                    g = i * 2 + u
                    col = dve.value_load(group_tile_i[0:1, bass.ds(g, 1)], min_val=0, max_val=T - 1) * D
                    made(dve, sum_ready, g, lead=RING // 2)
                    retired(dve, sum_added, g + 1)
                    V.tensor_tensor(x_flat[:, bass.ds(col, D)], x_flat[:, bass.ds(col, D)],
                                    bank[u][:, :], ALU.add).then_inc(sum_added, 1)

        @block.gpsimd
        def _(gp):
            gp.wait_ge(prepared, 3)
            gather_quads(nc, gp, s, gathered, QUADS, ET, rows, idx, from_idx, h_dram, sum_ready, 2)

        @block.tensor
        def _(pe):
            pe.sem_inc(sum_ready, RING // 2)
            with pe.Fori(0, ET // RING) as i:
                for q in range(RING // 2):
                    g = i * (RING // 2) + q
                    retired(pe, sum_added, g)
                    for k in range(2):
                        r = 2 * q + k
                        pe.wait_ge(S_ready, g * 2 + k + 1 + 4)
                        pe.wait_ge(gathered[r // 4], i * 64 + 64)
                        last = nc.tensor.matmul(bank[q % 2][:, :], S[r % 4][:, :], rows[r // 4][:, r % 4, :], start=(k == 0), stop=(k == 1))
                    last.then_inc(sum_ready, 1)


def layer0_ffn(nc, v):
    x, ident, iota, stats, mean, rstd = (v[k] for k in ("x", "ident", "iota", "stats", "mean", "rstd"))
    neghalf, shift, bank = v["neghalf"], v["shift"], v["bank"]
    NE, H, GH = 8, 64, 16
    pairs = T // 2
    with ExitStack() as ctx:
        sb, sem = allocators(nc, ctx, "ffn0")
        w1, w3 = sb("w1", [P, K, D]), sb("w3", [P, K, D])
        wg1, wg2 = sb("wg1", [P, K, GH]), sb("wg2", [GH, NE])
        w2 = sb("w2", [P, K, P])
        b1, b2, g2, be2 = (sb(n, [P, D]) for n in ("b1", "b2", "g2", "be2"))
        gb1 = sb("gb1", [P, 2, K])
        bg1, bg2, b3 = sb("bg1", [GH, 1]), sb("bg2", [P, NE]), sb("b3", [NE, D])
        natural = sb("natural", [P, 2])
        two = range(2)
        xn, hb, hc = ([sb(f"{n}{u}", [P, D]) for u in two] for n in ("xn", "hb", "hc"))
        xT, aT, cT = ([sb(f"{n}{u}", [P, K, P]) for u in two] for n in ("xT", "aT", "cT"))
        gT = [sb(f"gT{u}", [GH, P]) for u in two]
        cwT = [sb(f"cwT{u}", [NE, P]) for u in two]
        lg, top = sb("lg", [P, 2, NE]), sb("top", [P, 2, NE])
        top_i, top_f = sb("top_i", [P, 2, NE], U32), sb("top_f", [P, 2, NE])
        share = sb("share", [P, 2, 4])
        cw, cw2 = sb("cw", [P, 2, NE]), sb("cw2", [P, 2, NE])
        st1, st2 = (sb(n, [P, 2, NE, 6]) for n in ("st1", "st2"))
        ms1, ms2 = (sb(n, [P, 2, 2, NE]) for n in ("ms1", "ms2"))

        names = ("weights_in", "w2_zero", "w2_in", "natural_made", "dve_own", "gate", "shift_ready", "pool_own", "var_ready", "rstd_ready",
                 "xn_ready", "xT_ps", "xT_ready", "h1_ps", "gate_ps", "gate_ready", "logit_ps", "logit_taken", "dist_ready", "exp_ready",
                 "cw_ready", "cwT_ps", "cwT_ready", "h1_taken", "var1_ready", "rstd1_ready", "a_ready", "aT_ps", "aT_ready",
                 "h2_ps", "h2_taken", "var2_ready", "rstd2_ready", "c_normed", "c_scaled", "c_active", "c_ready", "cT_ps", "cT_ready",
                 "o_ps", "x_done")
        s = {n: sem(n) for n in names}
        block = ctx.enter_context(nc.Block())

        @block.sync
        def _(sp):
            for dst, src in ((w1[:, :, :], v["w1_in"].rearrange("(k p) e -> p k e", p=P)),
                             (wg1[:, :, :], v["wg1_in"].rearrange("(k p) e -> p k e", p=P)),
                             (wg2[:, :], v["wg2_in"]), (w3[:, :, :], v["w3_in"].rearrange("(k p) e -> p k e", p=P)),
                             (b1[:, :], v["b1_in"].broadcast_to([P, D])), (b2[:, :], v["b2_in"].broadcast_to([P, D])),
                             (g2[:, :], v["g2_in"].broadcast_to([P, D])), (be2[:, :], v["be2_in"].broadcast_to([P, D])),
                             (gb1[:, :, :], v["gb1_in"]), (bg1[:, :], v["bg1_in"]), (bg2[:, :], v["bg2_in"].broadcast_to([P, NE])),
                             (b3[:, :], v["b3_in"])):
                sp.dma_start(dst, src).then_inc(s["weights_in"], 16)
            sp.wait_ge(s["w2_zero"], 1)
            for e in range(NE):
                q = H * (e % 2)
                sp.dma_start(w2[q:q + H, e // 2, q:q + H], v["w2_in"][e, :, :]).then_inc(s["w2_in"], 16)

        def weights(eng):
            eng.wait_ge(s["weights_in"], 12 * 16)

        def groups(ap):
            return ap.rearrange("p (e h) -> p e h", e=NE)

        @block.gpsimd
        def _(gp):
            G_ = nc.gpsimd
            G_.memset(w2[:, :, :], 0.0).then_inc(s["w2_zero"], 1)
            G_.memset(natural[:, :], float(np.e)).then_inc(s["natural_made"], 1)
            for n in ("c_scaled",):
                gp.sem_inc(s[n], LEAD)
            for n in ("rstd1_ready", "rstd2_ready", "exp_ready"):
                gp.sem_inc(s[n], 1)
            gp.wait_ge(s["var_ready"], 1)
            G_.tensor_tensor(rstd[:, :], rstd[:, :], neghalf[:, 0:T], ALU.pow).then_inc(s["rstd_ready"], 1)
            weights(gp)
            gp.wait_ge(s["natural_made"], 1)

            def gate_exp(i):
                made(gp, s["dist_ready"], i, lead=1)
                G_.tensor_tensor(share[:, :, 1], natural[:, :], share[:, :, 0], ALU.pow).then_inc(s["exp_ready"], 1)

            def rsqrt1(i):
                made(gp, s["var1_ready"], i, lead=1)
                G_.tensor_tensor(ms1[:, :, 1, :], ms1[:, :, 1, :], neghalf[:, 0:2 * NE].rearrange("p (a e) -> p a e", a=2), ALU.pow).then_inc(s["rstd1_ready"], 1)

            def rsqrt2(i):
                made(gp, s["var2_ready"], i, lead=1)
                G_.tensor_tensor(ms2[:, :, 1, :], ms2[:, :, 1, :], neghalf[:, 0:2 * NE].rearrange("p (a e) -> p a e", a=2), ALU.pow).then_inc(s["rstd2_ready"], 1)

            def affine2(own, i):
                for u in two:
                    made(gp, s["c_normed"], i * 2 + u)
                    own.step(G_.tensor_tensor(hc[u][:, :], hc[u][:, :], g2[:, :], ALU.mult))
                for u in two:
                    own.wait()
                    G_.tensor_tensor(hc[u][:, :], hc[u][:, :], be2[:, :], ALU.add).then_inc(s["c_scaled"], 1)

            own = Chain(gp, s["pool_own"])
            gate_exp(0)
            rsqrt1(0)
            with gp.Fori(0, pairs - 1) as i:
                own.enter(i, 2)
                rsqrt2(i)
                affine2(own, i)
                gate_exp(i + 1)
                rsqrt1(i + 1)
                own.leave(pairs - 1)
            rsqrt2(pairs - 1)
            affine2(own, pairs - 1)

        @block.vector
        def _(dve):
            V = nc.vector
            own = Chain(dve, s["dve_own"])
            for n in ("logit_taken", "h1_taken", "h2_taken", "a_ready", "c_normed", "c_ready", "x_done", "cT_ready"):
                dve.sem_inc(s[n], LEAD)
            for n in ("dist_ready", "cw_ready", "var1_ready", "var2_ready"):
                dve.sem_inc(s[n], 1)
            norm_stats(nc, own, x, stats, mean[:, :], rstd[:, :], s["var_ready"])
            dve.wait_ge(s["rstd_ready"], 1)
            V.scalar_tensor_tensor(shift[:, :], mean[:, :], -1.0, rstd[:, :], ALU.mult, ALU.mult).then_inc(s["shift_ready"], 1)
            weights(dve)

            def route(i):
                retired(dve, s["cwT_ps"], i * 2 + 1)
                for u in two:
                    made(dve, s["logit_ps"], i * 2 + u)
                    V.tensor_tensor(lg[:, u, :], bank[6 + u][:, P:P + NE], bg2[:, :], ALU.add).then_inc(s["logit_taken"], 1)
                made(dve, s["logit_taken"], i * 2 + 1)
                dve.sem_inc(s["gate"], 1)
                for u in two:
                    own.step(V.max(top[:, u, :], lg[:, u, :]))
                own.wait()
                dve.sem_inc(s["gate"], 1)
                for u in two:
                    own.step(V.max_index(top_i[:, u, :], top[:, u, :], lg[:, u, :]))
                V.tensor_tensor(share[:, :, 0], top[:, :, 1], top[:, :, 0], ALU.subtract).then_inc(s["dist_ready"], 1)
                own.wait()
                own.step(V.tensor_copy(top_f[:, :, :], top_i[:, :, :]))
                made(dve, s["exp_ready"], i, lead=1)
                own.link(V.tensor_scalar(share[:, :, 2], share[:, :, 1], 1.0, None, ALU.add))
                own.link(V.reciprocal(share[:, :, 2], share[:, :, 2]))
                own.link(V.tensor_tensor(share[:, :, 3], share[:, :, 2], share[:, :, 1], ALU.mult))
                for u in two:
                    own.step(V.tensor_scalar(cw[:, u, :], iota[:, 0:NE], top_f[:, u, 0:1], share[:, u, 2:3], ALU.is_equal, ALU.mult))
                    own.step(V.tensor_scalar(cw2[:, u, :], iota[:, 0:NE], top_f[:, u, 1:2], share[:, u, 3:4], ALU.is_equal, ALU.mult))
                own.wait()
                V.tensor_tensor(cw[:, :, :], cw[:, :, :], cw2[:, :, :], ALU.add).then_inc(s["cw_ready"], 1)

            def norm(i, h_ps, first, taken, bias, hx, read_by, st, ms, var, rst, out):
                for u in two:
                    retired(dve, read_by, i * 2 + u)
                    made(dve, h_ps, i * 2 + u)
                    V.tensor_tensor(hx[u][:, :], bank[first + u][:, :], bias[:, :], ALU.add).then_inc(taken, 1)
                for u in two:
                    made(dve, taken, i * 2 + u)
                    for e in range(NE):
                        own.step(V.bn_stats(st[:, u, e, :], hx[u][:, e * H:(e + 1) * H]))
                own.wait()
                me, ve, mo, vo = (st[:, :, :, c] for c in (1, 2, 4, 5))
                m, r = ms[:, :, 0, :], ms[:, :, 1, :]
                own.step(V.tensor_tensor(m, me, mo, ALU.add))
                own.step(V.tensor_tensor(r, me, mo, ALU.subtract))
                own.link(V.tensor_tensor(st[:, :, :, 0], ve, vo, ALU.add))
                own.step(V.tensor_scalar(m, m, 0.5, None, ALU.mult))
                own.link(V.scalar_tensor_tensor(r, r, 0.25, r, ALU.mult, ALU.mult))
                own.link(V.scalar_tensor_tensor(r, st[:, :, :, 0], 1.0 / H, r, ALU.mult, ALU.add))
                V.tensor_scalar(r, r, EPS, None, ALU.add).then_inc(var, 1)
                for u in two:
                    own.step(V.tensor_tensor(groups(hx[u][:, :]), groups(hx[u][:, :]), ms[:, u, 0, :].unsqueeze(2).broadcast_to([P, NE, H]), ALU.subtract))
                own.wait()
                made(dve, rst, i, lead=1)
                for u in two:
                    V.tensor_tensor(groups(hx[u][:, :]), groups(hx[u][:, :]), ms[:, u, 1, :].unsqueeze(2).broadcast_to([P, NE, H]), ALU.mult).then_inc(out, 1)

            def norm1(i):
                norm(i, s["h1_ps"], 2, s["h1_taken"], b1, hb, s["aT_ps"], st1, ms1, s["var1_ready"], s["rstd1_ready"], s["a_ready"])

            def norm2(i):
                norm(i, s["h2_ps"], 4, s["h2_taken"], b2, hc, s["cT_ps"], st2, ms2, s["var2_ready"], s["rstd2_ready"], s["c_normed"])

            def weigh(i):
                made(dve, s["cw_ready"], i, lead=1)
                for u in two:
                    made(dve, s["c_active"], i * 2 + u)
                    V.tensor_tensor(groups(hc[u][:, :]), groups(hc[u][:, :]), cw[:, u, :].unsqueeze(2).broadcast_to([P, NE, H]), ALU.mult).then_inc(s["c_ready"], 1)

            def add_out(i):
                for u in two:
                    xt = x[:, bass.ds(i * 2 + u, 1), :].rearrange("p a d -> p (a d)")
                    made(dve, s["o_ps"], i * 2 + u)
                    V.tensor_tensor(xt, xt, bank[4 + u][:, :], ALU.add).then_inc(s["x_done"], 1)

            route(0)
            norm1(0)
            with dve.Fori(0, pairs - 1) as i:
                own.enter(i, 60)
                norm2(i)
                weigh(i)
                route(i + 1)
                norm1(i + 1)
                add_out(i)
                own.leave(pairs - 1)
            norm2(pairs - 1)
            weigh(pairs - 1)
            add_out(pairs - 1)

        @block.scalar
        def _(act):
            A = nc.scalar
            for n in ("xn_ready", "xT_ready", "gate_ready", "cwT_ready", "aT_ready", "c_active"):
                act.sem_inc(s[n], LEAD)
            weights(act)
            act.wait_ge(s["shift_ready"], 1)

            def first(i):
                for u in two:
                    t = i * 2 + u
                    retired(act, s["xT_ps"], t)
                    A.activation(xn[u][:, :], x[:, bass.ds(t, 1), :].rearrange("p a d -> p (a d)"), ACT.Identity,
                                 bias=shift[:, bass.ds(t, 1)], scale=rstd[:, bass.ds(t, 1)]).then_inc(s["xn_ready"], 1)
                for u in two:
                    t = i * 2 + u
                    made(act, s["xT_ps"], t)
                    retired(act, s["gate_ps"], t)
                    A.activation(xT[u][:, :, :].rearrange("p k n -> p (k n)"), bank[u][:, :], ACT.Copy).then_inc(s["xT_ready"], 1)
                for u in two:
                    t = i * 2 + u
                    made(act, s["gate_ps"], t)
                    retired(act, s["logit_ps"], t)
                    A.activation(gT[u][:, :], bank[6 + u][0:GH, 0:P], ACT.Gelu, bias=bg1[:, 0:1]).then_inc(s["gate_ready"], 1)

            def second(i):
                for u in two:
                    t = i * 2 + u
                    made(act, s["cwT_ps"], t)
                    retired(act, s["o_ps"], t)
                    A.activation(cwT[u][:, :], bank[6 + u][0:NE, 256:256 + P], ACT.Copy).then_inc(s["cwT_ready"], 1)
                for u in two:
                    t = i * 2 + u
                    made(act, s["aT_ps"], t)
                    retired(act, s["h2_ps"], t)
                    for c in range(K):
                        last = A.activation(aT[u][:, c, :], bank[u][:, c * P:(c + 1) * P], ACT.Gelu, bias=gb1[:, 1, c:c + 1], scale=gb1[:, 0, c:c + 1])
                    last.then_inc(s["aT_ready"], 1)

            def third(i):
                for u in two:
                    t = i * 2 + u
                    made(act, s["c_scaled"], t)
                    A.activation(hc[u][:, :], hc[u][:, :], ACT.Gelu).then_inc(s["c_active"], 1)
                for u in two:
                    t = i * 2 + u
                    made(act, s["cT_ps"], t)
                    retired(act, s["o_ps"], t)
                    A.activation(cT[u][:, :, :].rearrange("p k n -> p (k n)"), bank[u][:, :], ACT.Copy).then_inc(s["cT_ready"], 1)

            first(0)
            with act.Fori(0, pairs - 1) as i:
                second(i)
                first(i + 1)
                third(i)
            second(pairs - 1)
            third(pairs - 1)

        @block.tensor
        def _(pe):
            M = nc.tensor
            for n in ("xT_ps", "h1_ps", "gate_ps", "logit_ps", "cwT_ps", "aT_ps", "h2_ps", "cT_ps", "o_ps"):
                pe.sem_inc(s[n], LEAD)
            weights(pe)
            pe.wait_ge(s["w2_in"], NE * 16)

            def turn(i, ready, src, done):
                for u in two:
                    made(pe, ready, i * 2 + u)
                    for k in range(K):
                        last = M.transpose(bank[u][:, k * P:(k + 1) * P], src[u][:, k * P:(k + 1) * P], ident[:, :])
                    last.then_inc(done, 1)

            def first(i):
                turn(i, s["xn_ready"], xn, s["xT_ps"])
                for u in two:
                    t = i * 2 + u
                    made(pe, s["xT_ready"], t)
                    retired(pe, s["h1_taken"], t)
                    for k in range(K):
                        last = M.matmul(bank[2 + u][:, :], xT[u][:, k, :], w1[:, k, :], start=(k == 0), stop=(k == K - 1))
                    last.then_inc(s["h1_ps"], 1)
                    retired(pe, s["logit_taken"], t)
                    retired(pe, s["cwT_ready"], t)
                    for k in range(K):
                        last = M.matmul(bank[6 + u][0:GH, 0:P], wg1[:, k, :], xT[u][:, k, :], start=(k == 0), stop=(k == K - 1))
                    last.then_inc(s["gate_ps"], 1)
                for u in two:
                    made(pe, s["gate_ready"], i * 2 + u)
                    M.matmul(bank[6 + u][:, P:P + NE], gT[u][:, :], wg2[:, :], start=True, stop=True).then_inc(s["logit_ps"], 1)

            def second(i):
                made(pe, s["cw_ready"], i, lead=1)
                for u in two:
                    M.transpose(bank[6 + u][0:NE, 256:256 + P], cw[:, u, :], ident[:, :]).then_inc(s["cwT_ps"], 1)
                turn(i, s["a_ready"], hb, s["aT_ps"])
                for u in two:
                    t = i * 2 + u
                    made(pe, s["aT_ready"], t)
                    retired(pe, s["x_done"], t)
                    for c in range(K):
                        last = M.matmul(bank[4 + u][:, c * P:(c + 1) * P], aT[u][:, c, :], w2[:, c, :], start=True, stop=True)
                    last.then_inc(s["h2_ps"], 1)

            def third(i):
                turn(i, s["c_ready"], hc, s["cT_ps"])
                for u in two:
                    t = i * 2 + u
                    made(pe, s["cwT_ready"], t)
                    M.matmul(bank[4 + u][:, :], cwT[u][:, :], b3[:, :], start=True, stop=False)
                    made(pe, s["cT_ready"], t)
                    for c in range(K):
                        last = M.matmul(bank[4 + u][:, :], cT[u][:, c, :], w3[:, c, :], start=False, stop=(c == K - 1))
                    last.then_inc(s["o_ps"], 1)

            first(0)
            with pe.Fori(0, pairs - 1) as i:
                second(i)
                first(i + 1)
                third(i)
            second(pairs - 1)
            third(pairs - 1)


F = 32
AT, RT = 4, 20
LOG2 = float(np.log(2.0))


def softplus_less_log2(nc, act, own, out, tmp, in_, scale=1.0):
    own.link(nc.scalar.activation(tmp, in_, ACT.Abs, scale=scale))
    own.link(nc.scalar.activation(tmp, tmp, ACT.Exp, scale=-1.0))
    return nc.scalar.activation(out, tmp, ACT.Ln, scale=0.5, bias=0.5)


def layer1_features(nc, v):
    x, ident, edges, stats, mean, rstd = (v[k] for k in ("x", "ident", "edges", "stats", "mean", "rstd"))
    neghalf, shift, bank, hT, feat_dram = v["neghalf"], v["shift"], v["bank"], v["hT"], v["feat_dram"]
    two = range(2)
    EB = 16
    with ExitStack() as ctx:
        sb, sem = allocators(nc, ctx, "feat1")
        w_in = sb("w_in", [P, 2, F])
        wr = sb("wr", [4 * RT, P])
        br = sb("br", [P, 1])
        xn = [sb(f"xn{u}", [P, D]) for u in two]
        xT = [sb(f"xT{u}", [P, K, P]) for u in two]
        feat = sb("feat", [P, T, P])
        fr = [sb(f"fr{u}", [P, EB, RT]) for u in two]
        fT = [sb(f"fT{u}", [4 * RT, 4 * P]) for u in two]
        pre, soft = ([sb(f"{n}{u}", [P, 4 * P]) for u in two] for n in ("pre", "soft"))
        names = ("weights_in", "wr_zero", "wr_in", "dve_own", "act_own", "var_ready", "rstd_ready", "shift_ready", "xn_ready", "xT_ps",
                 "xT_ready", "feat_ps", "feat_ready", "feat_stored", "fr_ready", "fT_ps", "fT_ready", "pre_ps", "pre_ready",
                 "soft_ready", "hT_ready")
        s = {n: sem(n) for n in names}
        block = ctx.enter_context(nc.Block())

        @block.sync
        def _(sp):
            sp.dma_start(w_in[:, :, :], v["w_in_in"]).then_inc(s["weights_in"], 16)
            sp.dma_start(br[:, :], v["br_in"]).then_inc(s["weights_in"], 16)
            sp.wait_ge(s["wr_zero"], 1)
            for k in range(4):
                sp.dma_start(wr[RT * k:RT * k + RT, F * k:F * k + F], v["wr_in"]).then_inc(s["wr_in"], 16)
            with sp.Fori(0, T) as t:
                made(sp, s["feat_ready"], t)
                sp.dma_start(feat_dram[bass.ds(t * P, P), :], feat[:, bass.ds(t, 1), :].rearrange("p a d -> p (a d)")).then_inc(s["feat_stored"], 16)
            sp.wait_ge(s["feat_stored"], 16 * T)

        @block.gpsimd
        def _(gp):
            nc.gpsimd.memset(wr[:, :], 0.0).then_inc(s["wr_zero"], 1)
            gp.wait_ge(s["var_ready"], 1)
            nc.gpsimd.tensor_tensor(rstd[:, :], rstd[:, :], neghalf[:, 0:T], ALU.pow).then_inc(s["rstd_ready"], 1)

        @block.vector
        def _(dve):
            V = nc.vector
            own = Chain(dve, s["dve_own"])
            for n in ("feat_ready", "fr_ready", "pre_ready", "hT_ready"):
                dve.sem_inc(s[n], LEAD)
            norm_stats(nc, own, x, stats, mean[:, :], rstd[:, :], s["var_ready"])
            dve.wait_ge(s["weights_in"], 32)
            dve.wait_ge(s["rstd_ready"], 1)
            V.scalar_tensor_tensor(shift[:, :], mean[:, :], -1.0, rstd[:, :], ALU.mult, ALU.mult).then_inc(s["shift_ready"], 1)
            with dve.Fori(0, T // 2) as i:
                for u in two:
                    t = i * 2 + u
                    made(dve, s["feat_ps"], t)
                    V.tensor_scalar(feat[:, bass.ds(t, 1), :].rearrange("p a d -> p (a d)"), bank[2 + u][:, 0:P],
                                    float(P) ** -0.5, None, ALU.mult).then_inc(s["feat_ready"], 1)
            with dve.Fori(0, ET // EB // 2) as i:
                for u in two:
                    t = i * 2 + u
                    retired(dve, s["fT_ps"], t)
                    V.tensor_copy(fr[u][:, :, :], edges[:, bass.ds(t * EB, EB), R_F:R_F + RT]).then_inc(s["fr_ready"], 1)
                for u in two:
                    t = i * 2 + u
                    made(dve, s["pre_ps"], t)
                    retired(dve, s["hT_ready"], t)
                    V.tensor_scalar(pre[u][:, :], bank[6 + u][:, :], br[:, 0:1], None, ALU.add).then_inc(s["pre_ready"], 1)
                for u in two:
                    t = i * 2 + u
                    made(dve, s["soft_ready"], t)
                    V.scalar_tensor_tensor(hT[:, bass.ds(t * 4 * P, 4 * P)], pre[u][:, :], 0.0, soft[u][:, :],
                                           ALU.max, ALU.add).then_inc(s["hT_ready"], 1)

        @block.scalar
        def _(act):
            A = nc.scalar
            own = Chain(act, s["act_own"])
            for n in ("xn_ready", "xT_ready", "fT_ready", "soft_ready"):
                act.sem_inc(s[n], LEAD)
            act.wait_ge(s["shift_ready"], 1)
            with act.Fori(0, T // 2) as i:
                for u in two:
                    t = i * 2 + u
                    retired(act, s["xT_ps"], t)
                    A.activation(xn[u][:, :], x[:, bass.ds(t, 1), :].rearrange("p a d -> p (a d)"), ACT.Identity,
                                 bias=shift[:, bass.ds(t, 1)], scale=rstd[:, bass.ds(t, 1)]).then_inc(s["xn_ready"], 1)
                for u in two:
                    t = i * 2 + u
                    made(act, s["xT_ps"], t)
                    retired(act, s["feat_ps"], t)
                    A.activation(xT[u][:, :, :].rearrange("p k n -> p (k n)"), bank[u][:, :], ACT.Copy).then_inc(s["xT_ready"], 1)
            with act.Fori(0, ET // EB // 2) as i:
                own.enter(i, 4)
                for u in two:
                    t = i * 2 + u
                    made(act, s["fT_ps"], t)
                    retired(act, s["pre_ps"], t)
                    A.activation(fT[u][:, :], bank[4 + u][0:4 * RT, :], ACT.Copy).then_inc(s["fT_ready"], 1)
                for u in two:
                    t = i * 2 + u
                    made(act, s["pre_ready"], t)
                    softplus_less_log2(nc, act, own, soft[u][:, :], soft[u][:, :], pre[u][:, :]).then_inc(s["soft_ready"], 1)
                own.leave(ET // EB // 2)

        @block.tensor
        def _(pe):
            M = nc.tensor
            for n in ("xT_ps", "feat_ps", "fT_ps", "pre_ps"):
                pe.sem_inc(s[n], LEAD)
            pe.wait_ge(s["weights_in"], 32)
            pe.wait_ge(s["wr_in"], 64)
            with pe.Fori(0, T // 2) as i:
                for u in two:
                    t = i * 2 + u
                    made(pe, s["xn_ready"], t)
                    for k in range(K):
                        src = xn[u][:, 0:P] if k == 0 else xn[u][:, P + k - 1:D:3]
                        last = M.transpose(bank[u][:, k * P:(k + 1) * P], src, ident[:, :])
                    last.then_inc(s["xT_ps"], 1)
                for u in two:
                    t = i * 2 + u
                    made(pe, s["xT_ready"], t)
                    retired(pe, s["feat_ready"], t)
                    for k in range(K):
                        last = M.matmul(bank[2 + u][:, k * F:(k + 1) * F], xT[u][:, k, :], w_in[:, min(k, 1), :], start=True, stop=True)
                    last.then_inc(s["feat_ps"], 1)
            with pe.Fori(0, ET // EB // 2) as i:
                for u in two:
                    t = i * 2 + u
                    made(pe, s["fr_ready"], t)
                    retired(pe, s["fT_ready"], t)
                    flat = fr[u][:, :, :].rearrange("p (a b) r -> p a (b r)", b=4)
                    for a in range(4):
                        last = M.transpose(bank[4 + u][0:4 * RT, a * P:(a + 1) * P], flat[:, a, :], ident[:, :])
                    last.then_inc(s["fT_ps"], 1)
                for u in two:
                    t = i * 2 + u
                    made(pe, s["fT_ready"], t)
                    retired(pe, s["pre_ready"], t)
                    M.matmul(bank[6 + u][:, :], wr[:, :], fT[u][:, :], start=True, stop=True).then_inc(s["pre_ps"], 1)


def layer1_edges(nc, v):
    iota, edges, from_idx, to_loc, hT, agg = (v[k] for k in ("iota", "edges", "from_idx", "to_loc", "hT", "agg"))
    group_tile_i, bank, feat_dram = v["group_tile_i"], v["bank"], v["feat_dram"]
    QUADS = 4
    EB = 4 * QUADS
    with ExitStack() as ctx:
        sb, sem = allocators(nc, ctx, "edges1")
        w2 = sb("w2", [P, 4 * P])
        b2 = sb("b2", [1, 4 * P])
        ones = sb("ones", [1, P])
        hq = [sb(f"hq{q}", [P, P]) for q in range(2)]
        rows = [sb(f"rows{q}", [P, 4, P]) for q in range(QUADS)]
        idx = [sb(f"idx{q}", [P, 4], I32) for q in range(QUADS)]
        wf = [sb(f"wf{q}", [P, 4, 8, F]) for q in range(2)]
        hot = [sb(f"hot{k}", [P, P]) for k in range(4)]
        S = [sb(f"S{k}", [P, 4, P]) for k in range(4)]
        agg_flat = agg[:, :, :].rearrange("p t d -> p (t d)")
        names = ("weights_in", "w2_zero", "w2_in", "idx_ready", "gate", "hq_ready", "filter_ps", "wf_ready", "hot_ready",
                 "S0_ready", "S_ready", "sum_ready", "agg_zero", "sum_added", "weighted", "wf_made")
        s = {n: sem(n) for n in names}
        gathered = [sem(f"gathered{q}") for q in range(QUADS)]
        block = ctx.enter_context(nc.Block())

        @block.sync
        def _(sp):
            sp.dma_start(b2[:, :], v["bf_in"]).then_inc(s["weights_in"], 16)
            sp.wait_ge(s["w2_zero"], 2)
            for k in range(4):
                sp.dma_start(w2[F * k:F * k + F, P * k:P * k + P], v["wf_in"]).then_inc(s["w2_in"], 16)

        @block.gpsimd
        def _(gp):
            nc.gpsimd.memset(ones[:, :], 1.0).then_inc(s["w2_zero"], 1)
            nc.gpsimd.memset(w2[:, :], 0.0).then_inc(s["w2_zero"], 1)
            gather_quads(nc, gp, s, gathered, QUADS, ET, rows, idx, from_idx, feat_dram, s["wf_made"], 1)

        @block.vector
        def _(dve):
            V = nc.vector
            dve.sem_inc(s["hot_ready"], 4)
            dve.sem_inc(s["S0_ready"], 4)
            dve.sem_inc(s["wf_made"], QUADS)
            dve.sem_inc(s["sum_added"], 4)
            V.memset(agg[:, :, :], 0.0).then_inc(s["agg_zero"], 1)
            V.tensor_tensor(edges[:, :, R_Y:R_Y + AT], edges[:, :, R_Y:R_Y + AT],
                            edges[:, :, R_W:R_W + 1].broadcast_to([P, ET, AT]), ALU.mult).then_inc(s["weighted"], 1)
            dve.wait_ge(s["weighted"], 1)
            dve.wait_ge(s["agg_zero"], 1)

            def add(i, q):
                for g2 in range(2):
                    g = i * (EB // 2) + q * 2 + g2
                    col = dve.value_load(group_tile_i[0:1, bass.ds(g, 1)], min_val=0, max_val=T - 1) * (8 * F)
                    made(dve, s["sum_ready"], g, lead=4)
                    retired(dve, s["sum_added"], g, ring=1, lead=4)
                    V.tensor_tensor(agg_flat[:, bass.ds(col, 8 * F)], agg_flat[:, bass.ds(col, 8 * F)],
                                    bank[2 * q % 4 + g2][:, 0:8 * F], ALU.add).then_inc(s["sum_added"], 1)

            with dve.Fori(0, ET // EB) as i:
                for q in range(QUADS):
                    n = i * QUADS + q
                    for k in range(4):
                        e = n * 4 + k
                        retired(dve, s["S_ready"], e, ring=4, lead=4)
                        retired(dve, s["sum_ready"], n * 2 + k // 2, ring=2, lead=4)
                        V.tensor_scalar(hot[k][:, :], iota[:, :], to_loc[:, bass.ds(e, 1)], None, ALU.is_equal).then_inc(s["hot_ready"], 1)
                        V.tensor_scalar(S[k][:, 0, :], iota[:, :], to_loc[:, bass.ds(e, 1)], edges[:, bass.ds(e, 1), R_Y],
                                        ALU.is_equal, ALU.mult).then_inc(s["S0_ready"], 1)
                    dve.wait_ge(gathered[q], i * 64 + 64)
                    made(dve, s["filter_ps"], n)
                    retired(dve, s["sum_ready"], n * 2 + 1, ring=4, lead=4)
                    w = bank[4 + q % 2][:, :].rearrange("p (e k f) -> p e k f", e=4, k=4)
                    m, r = wf[q % 2], rows[q]
                    vec = r[:, :, F:P].rearrange("p e (c f) -> p e c f", f=F)
                    V.tensor_tensor(m[:, :, 1:4, :], vec, w[:, :, 1:2, :].broadcast_to([P, 4, 3, F]), ALU.mult).then_inc(s["wf_ready"], 1)
                    V.tensor_tensor(m[:, :, 4:7, :], vec, w[:, :, 2:3, :].broadcast_to([P, 4, 3, F]), ALU.mult).then_inc(s["wf_ready"], 1)
                    V.tensor_tensor(m[:, :, 0:8:7, :], r[:, :, 0:F].unsqueeze(2).broadcast_to([P, 4, 2, F]), w[:, :, 0:4:3, :], ALU.mult).then_inc(s["wf_made"], 1)
                    if q >= 1:
                        add(i, q - 1)
                add(i, QUADS - 1)

        @block.scalar
        def _(act):
            A = nc.scalar
            act.sem_inc(s["hq_ready"], LEAD)
            act.sem_inc(s["S_ready"], 4)
            act.wait_ge(s["weighted"], 1)
            with act.Fori(0, ET // EB) as i:
                for q in range(QUADS):
                    n = i * QUADS + q
                    retired(act, s["filter_ps"], n)
                    A.activation(hq[q % 2][:, :], hT[:, bass.ds(n * P, P)], ACT.Copy).then_inc(s["hq_ready"], 1)
                    for k in range(4):
                        e = n * 4 + k
                        made(act, s["hot_ready"], e, lead=4)
                        for c in range(1, 4):
                            last = A.activation(S[k][:, c, :], hot[k][:, :], ACT.Copy, scale=edges[:, bass.ds(e, 1), R_Y + c])
                        last.then_inc(s["S_ready"], 1)

        @block.tensor
        def _(pe):
            M = nc.tensor
            pe.sem_inc(s["filter_ps"], LEAD)
            pe.sem_inc(s["sum_ready"], 4)
            pe.wait_ge(s["weights_in"], 16)
            pe.wait_ge(s["w2_in"], 64)
            with pe.Fori(0, ET // EB) as i:
                for q in range(QUADS):
                    n = i * QUADS + q
                    made(pe, s["hq_ready"], n)
                    retired(pe, s["wf_made"], n, ring=2, lead=QUADS)
                    M.matmul(bank[4 + q % 2][:, :], hq[q % 2][:, :], w2[:, :], start=True, stop=False)
                    M.matmul(bank[4 + q % 2][:, :], ones[:, :], b2[:, :], start=False, stop=True).then_inc(s["filter_ps"], 1)
                    made(pe, s["wf_made"], n, lead=QUADS)
                    m = wf[q % 2]
                    for g2 in range(2):
                        g = n * 2 + g2
                        to = bank[2 * q % 4 + g2][:, 0:8 * F].rearrange("p (b f) -> p b f", f=F)
                        retired(pe, s["sum_added"], g, ring=4, lead=4)
                        for k in (2 * g2, 2 * g2 + 1):
                            made(pe, s["S0_ready"], n * 4 + k, lead=4)
                            made(pe, s["S_ready"], n * 4 + k, lead=4)
                            M.matmul(to[:, 1:8:2, :], S[k][:, 0, :], m[:, k, 0:4, :], start=(k % 2 == 0), stop=False, skip_group_check=True)
                            for c in range(1, 4):
                                last = M.matmul(to[:, 0:2 * c + 1:2 * c, :], S[k][:, c, :], m[:, k, 3 + c:8:4 - c, :],
                                                start=False, stop=(k % 2 == 1), skip_group_check=True)
                        last.then_inc(s["sum_ready"], 1)


def layer1_nodes(nc, v):
    x, ident, agg, bank = (v[k] for k in ("x", "ident", "agg", "bank"))
    two = range(2)
    with ExitStack() as ctx:
        sb, sem = allocators(nc, ctx, "nodes1")
        w1s = sb("w1s", [2 * F, P])
        w1v = sb("w1v", [P, P])
        w2 = sb("w2", [P, 2, P])
        a = [sb(f"a{u}", [P, 2, P]) for u in two]
        aT = [sb(f"aT{u}", [P, 2, P]) for u in two]
        oT = [sb(f"oT{u}", [P, 4, P]) for u in two]
        relu, soft = ([sb(f"{n}{u}", [P, P]) for u in two] for n in ("relu", "soft"))
        names = ("weights_in", "act_own", "gate", "w1_ready", "a_ready", "aT_ps", "aT_ready", "o1_ps", "oT_copied", "soft_ready", "relu_ready", "o1_taken",
                 "os_ready", "o2_ps", "x_s", "x_done")
        s = {n: sem(n) for n in names}
        block = ctx.enter_context(nc.Block())
        half = float(2 * F) ** -0.5

        @block.sync
        def _(sp):
            for dst, src in ((w1s[0:F, :], v["w1s_in"][F:2 * F, :]), (w1s[F:2 * F, :], v["w1s_in"][0:F, :]),
                             (w1v[0:2 * F, :], v["w1v_in"]), (w1v[2 * F:P, :], v["w1v_in"]),
                             (w2[:, 0, :], v["w2s_in"]), (w2[:, 1, :], v["w2v_in"])):
                sp.dma_start(dst, src).then_inc(s["weights_in"], 16)

        @block.gpsimd
        def _(gp):
            gp.sem_inc(s["a_ready"], LEAD)
            with gp.Fori(0, T // 2) as i:
                for u in two:
                    t = i * 2 + u
                    retired(gp, s["aT_ps"], t)
                    gp.sem_inc(s["gate"], 1)
                    nc.gpsimd.tensor_copy(a[u][:, :, :].rearrange("p a b -> p (a b)"), agg[:, bass.ds(t, 1), :].rearrange("p a d -> p (a d)")).then_inc(s["a_ready"], 1)

        @block.vector
        def _(dve):
            V = nc.vector
            for n in ("relu_ready", "os_ready", "x_done", "x_s"):
                dve.sem_inc(s[n], LEAD)
            dve.wait_ge(s["weights_in"], 6 * 16)
            V.tensor_scalar(w1s[0:F, :], w1s[0:F, :], 3.0 ** -0.5, None, ALU.mult).then_inc(s["w1_ready"], 1)
            with dve.Fori(0, T // 2) as i:
                for u in two:
                    t = i * 2 + u
                    made(dve, s["oT_copied"], t)
                    made(dve, s["soft_ready"], t)
                    V.tensor_scalar(relu[u][:, :], bank[2 + u][:, 0:P], half, 0.0, ALU.mult, ALU.max).then_inc(s["relu_ready"], 1)
                for u in two:
                    t = i * 2 + u
                    made(dve, s["relu_ready"], t)
                    retired(dve, s["o2_ps"], t)
                    V.tensor_tensor(oT[u][:, 0, :], relu[u][:, :], soft[u][:, :], ALU.add).then_inc(s["os_ready"], 1)
                for u in two:
                    t = i * 2 + u
                    made(dve, s["o2_ps"], t)
                    xt = x[:, bass.ds(t, 1), :].rearrange("p a d -> p (a d)")
                    V.scalar_tensor_tensor(xt[:, 0:P], bank[4 + u][:, 0:P], float(P) ** -0.5, xt[:, 0:P], ALU.mult, ALU.add).then_inc(s["x_s"], 1)
                    xv = xt[:, P:D].rearrange("p (d c) -> p c d", c=3)
                    V.scalar_tensor_tensor(xv, bank[4 + u][:, P:D].rearrange("p (c d) -> p c d", c=3), float(P) ** -0.5, xv,
                                           ALU.mult, ALU.add).then_inc(s["x_done"], 1)

        @block.scalar
        def _(act):
            A = nc.scalar
            own = Chain(act, s["act_own"])
            for n in ("aT_ready", "oT_copied", "soft_ready"):
                act.sem_inc(s[n], LEAD)
            with act.Fori(0, T // 2) as i:
                own.enter(i, 4)
                for u in two:
                    t = i * 2 + u
                    made(act, s["aT_ps"], t)
                    retired(act, s["o1_ps"], t)
                    A.activation(aT[u][:, :, :].rearrange("p a b -> p (a b)"), bank[u][:, 0:2 * P], ACT.Copy).then_inc(s["aT_ready"], 1)
                for u in two:
                    t = i * 2 + u
                    made(act, s["o1_ps"], t)
                    retired(act, s["o2_ps"], t)
                    retired(act, s["os_ready"], t)
                    own.link(A.activation(soft[u][:, :], bank[2 + u][:, 0:P], ACT.Abs, scale=half))
                    A.activation(oT[u][:, 2, :], bank[2 + u][:, P:2 * P], ACT.Copy, scale=half)
                    A.activation(oT[u][:, 1:4:2, :], bank[6 + u][:, 0:2 * P].rearrange("p (a b) -> p a b", a=2), ACT.Copy, scale=half).then_inc(s["oT_copied"], 1)
                    own.link(A.activation(soft[u][:, :], soft[u][:, :], ACT.Exp, scale=-1.0))
                    A.activation(soft[u][:, :], soft[u][:, :], ACT.Ln, scale=0.5, bias=0.5).then_inc(s["soft_ready"], 1)
                own.leave(T // 2)

        @block.tensor
        def _(pe):
            M = nc.tensor
            for n in ("aT_ps", "o1_ps", "o2_ps"):
                pe.sem_inc(s[n], LEAD)
            pe.wait_ge(s["weights_in"], 6 * 16)
            pe.wait_ge(s["w1_ready"], 1)
            with pe.Fori(0, T // 2) as i:
                for u in two:
                    t = i * 2 + u
                    made(pe, s["a_ready"], t)
                    for k in range(2):
                        last = M.transpose(bank[u][:, k * P:(k + 1) * P], a[u][:, k, :], ident[:, :])
                    last.then_inc(s["aT_ps"], 1)
                for u in two:
                    t = i * 2 + u
                    made(pe, s["aT_ready"], t)
                    retired(pe, s["relu_ready"], t)
                    for j in range(4):
                        q = 2 * F * (j % 2)
                        lhs = w1s[0:2 * F, :] if j == 0 else w1v[q:q + 2 * F, :]
                        last = M.matmul(bank[2 + u + 4 * (j % 2)][:, j // 2 * P:(j // 2 + 1) * P], lhs, aT[u][q:q + 2 * F, j // 2, :],
                                        start=True, stop=True)
                    last.then_inc(s["o1_ps"], 1)
                for u in two:
                    t = i * 2 + u
                    made(pe, s["oT_copied"], t)
                    made(pe, s["os_ready"], t)
                    retired(pe, s["x_done"], t)
                    for j in range(4):
                        last = M.matmul(bank[4 + u][:, j * P:(j + 1) * P], oT[u][:, j, :], w2[:, min(j, 1), :], start=True, stop=True)
                    last.then_inc(s["o2_ps"], 1)


NX, HX, NH = 64, 64, 4
CAP = 4 * N * 2 // NX
NB = 2 * N // P + NX


def layer1_route(nc, v):
    x, ident, iota, stats, mean, rstd = (v[k] for k in ("x", "ident", "iota", "stats", "mean", "rstd"))
    neghalf, shift, bank = v["neghalf"], v["shift"], v["bank"]
    tok_idx, y_idx, gain, block_expert = (v[k] for k in ("tok_idx", "y_idx", "gain", "block_expert"))
    two = range(2)
    with ExitStack() as ctx:
        sb, sem = allocators(nc, ctx, "route1")
        hp = sb("hp", [P, K, NH * NX])
        xn = [sb(f"xn{u}", [P, D]) for u in two]
        xT = [sb(f"xT{u}", [P, K, P]) for u in two]
        xn_all = sb("xn_all", [P, T, D])
        top = [sb(f"top{u}", [P, NH, 8]) for u in two]
        top_i = [sb(f"top_i{u}", [P, NH, 8], U32) for u in two]
        score, expert = sb("score", [P, T, NH]), sb("expert", [P, T, NH])
        before = sb("before", [P, NH, NH])
        beats, ties = sb("beats", [P, T, NH, NH]), sb("ties", [P, T, NH, NH])
        rank = sb("rank", [P, T, NH])
        pick = sb("pick", [P, 2, T, NH])
        sel = sb("sel", [P, 2, T])
        hot = sb("hot", [P, 2, T, NX])
        both = sb("both", [P, T * NX])
        ahead = sb("ahead", [P, T, NX])
        total = sb("total", [P, T, NX])
        run = sb("run", [P, T + 1, NX])
        place = sb("place", [P, 2, T])
        first = sb("first", [P, 2, T])
        prod = sb("prod", [P, 2, T, NX])
        keep = sb("keep", [P, 2, T])
        small = sb("small", [P, 4, NX])
        nb, bend, bstart, one = (small[:, k, :] for k in range(4))
        nb_i = sb("nb_i", [P, NX], I32)
        slot_i, lo_i, hi_i, row_i = (sb(n, [P, 2, T], I32) for n in ("slot_i", "lo_i", "hi_i", "row_i"))
        row, trash = sb("row", [P, 2, T]), sb("trash", [P, 2, T])
        token = sb("token", [P, T], I32)
        iota_blk = sb("iota_blk", [P, NB])
        bmask = sb("bmask", [P, NB, NX])
        bexp = sb("bexp", [P, NB])
        lower, ones = sb("lower", [P, P]), sb("ones", [P, P])
        empty = sb("empty", [P, NB], I32)
        names = ("weights_in", "consts_made", "pool_own", "dve_own", "var_ready", "rstd_ready", "shift_ready", "xn_ready", "xn_kept", "xn_stored",
                 "xT_ps", "xT_ready", "logit_ps", "taken", "gate", "both_ready", "sums_ready", "emptied", "row_ready", "placed", "tok_in")
        s = {n: sem(n) for n in names}
        block = ctx.enter_context(nc.Block())

        @block.sync
        def _(sp):
            sp.dma_start(hp[:, :, :], v["hp_in"].rearrange("(k p) e -> p k e", p=P)).then_inc(s["weights_in"], 16)
            with sp.Fori(0, T) as t:
                made(sp, s["xn_kept"], t)
                sp.dma_start(v["xn_dram"][bass.ds(t * P, P), :], xn_all[:, bass.ds(t, 1), :].rearrange("p a d -> p (a d)")).then_inc(s["xn_stored"], 16)
            sp.wait_ge(s["placed"], 16 * 2 * T)
            sp.dma_start(tok_idx[:, 0:NB], v["tok_dram"][0:P * NB, :].rearrange("(p b) a -> p (b a)", p=P)).then_inc(s["tok_in"], 16)
            sp.wait_ge(s["tok_in"], 16)
            sp.wait_ge(s["xn_stored"], 16 * T)

        @block.gpsimd
        def _(gp):
            G_ = nc.gpsimd
            own = Chain(gp, s["pool_own"])
            own.step(G_.memset(ones[:, :], 1.0))
            own.step(G_.memset(before[:, :, :], 1.0))
            own.step(G_.memset(empty[:, :], 0))
            G_.memset(tok_idx[:, :], 0).then_inc(s["consts_made"], 1)
            G_.iota(token[:, :], [[P, T]], base=0, channel_multiplier=1).then_inc(s["consts_made"], 1)
            G_.iota(iota_blk[:, :], [[1, NB]], base=0, channel_multiplier=0, allow_small_or_imprecise_dtypes=True).then_inc(s["consts_made"], 1)
            G_.iota(trash[:, :, :], [[N, 2], [P, T]], base=P * NB, channel_multiplier=1, allow_small_or_imprecise_dtypes=True).then_inc(s["consts_made"], 1)
            own.wait()
            G_.affine_select(out=lower[:, :], in_=ones[:, :], compare_op=ALU.is_gt, fill=0.0, base=0,
                             pattern=[[1, P]], channel_multiplier=-1).then_inc(s["consts_made"], 1)
            G_.affine_select(out=before[:, :, :], in_=before[:, :, :], compare_op=ALU.is_gt, fill=0.0, base=0,
                             pattern=[[1, NH], [-1, NH]], channel_multiplier=0).then_inc(s["consts_made"], 1)
            gp.dma_start(v["tok_dram"][0:P * NB, :].rearrange("(p b) a -> p (b a)", p=P), empty[:, :]).then_inc(s["emptied"], 16)
            gp.wait_ge(s["var_ready"], 1)
            G_.tensor_tensor(rstd[:, :], rstd[:, :], neghalf[:, 0:T], ALU.pow).then_inc(s["rstd_ready"], 1)
            gp.wait_ge(s["emptied"], 16)
            gp.wait_ge(s["row_ready"], 1)
            for k in range(2):
                for t in range(T):
                    gp.indirect_dma_start(out=v["tok_dram"], out_offset=bass.IndirectOffsetOnAxis(ap=row_i[:, k, t:t + 1], axis=0),
                                          in_=token[:, t:t + 1], in_offset=None).then_inc(s["placed"], 16)

        @block.vector
        def _(dve):
            V = nc.vector
            own = Chain(dve, s["dve_own"])
            dve.sem_inc(s["xn_kept"], LEAD)
            dve.sem_inc(s["taken"], LEAD)
            norm_stats(nc, own, x, stats, mean[:, :], rstd[:, :], s["var_ready"])
            dve.wait_ge(s["rstd_ready"], 1)
            V.scalar_tensor_tensor(shift[:, :], mean[:, :], -1.0, rstd[:, :], ALU.mult, ALU.mult).then_inc(s["shift_ready"], 1)
            with dve.Fori(0, T // 2) as i:
                own.enter(i, 16)
                for u in two:
                    t = i * 2 + u
                    V.tensor_scalar(xn_all[:, bass.ds(t, 1), :].rearrange("p a d -> p (a d)"), x[:, bass.ds(t, 1), :].rearrange("p a d -> p (a d)"),
                                    mean[:, bass.ds(t, 1)], rstd[:, bass.ds(t, 1)], ALU.subtract, ALU.mult).then_inc(s["xn_kept"], 1)
                for u in two:
                    t = i * 2 + u
                    made(dve, s["logit_ps"], t)
                    dve.sem_inc(s["gate"], 1)
                    for h in range(NH):
                        own.step(V.max(top[u][:, h, :], bank[2 + u][:, h * NX:(h + 1) * NX]))
                    own.wait()
                    dve.sem_inc(s["gate"], 1)
                    for h in range(NH):
                        own.step(V.max_index(top_i[u][:, h, :], top[u][:, h, :], bank[2 + u][:, h * NX:(h + 1) * NX]))
                    own.wait()
                    V.tensor_copy(score[:, bass.ds(t, 1), :].rearrange("p a h -> p (a h)"), top[u][:, :, 0])
                    V.tensor_copy(expert[:, bass.ds(t, 1), :].rearrange("p a h -> p (a h)"), top_i[u][:, :, 0]).then_inc(s["taken"], 1)
                own.leave(T // 2)
            dve.wait_ge(s["taken"], T + LEAD)
            dve.wait_ge(s["consts_made"], 6)
            mine = score[:, :, :].unsqueeze(3).broadcast_to([P, T, NH, NH])
            other = score[:, :, :].unsqueeze(2).broadcast_to([P, T, NH, NH])
            own.step(V.tensor_tensor(beats[:, :, :, :], other, mine, ALU.is_gt))
            own.link(V.tensor_tensor(ties[:, :, :, :], other, mine, ALU.is_equal))
            own.link(V.tensor_tensor(ties[:, :, :, :], ties[:, :, :, :], before[:, :, :].unsqueeze(1).broadcast_to([P, T, NH, NH]), ALU.mult))
            own.link(V.tensor_tensor(beats[:, :, :, :], beats[:, :, :, :], ties[:, :, :, :], ALU.add))
            own.link(V.tensor_reduce(rank[:, :, :], beats[:, :, :, :], AX.X, ALU.add))
            for k in range(2):
                own.step(V.scalar_tensor_tensor(pick[:, k, :, :], rank[:, :, :], float(k), expert[:, :, :], ALU.is_equal, ALU.mult))
            own.wait()
            own.link(V.tensor_reduce(sel[:, :, :], pick[:, :, :, :], AX.X, ALU.add))
            for k in range(2):
                own.step(V.tensor_tensor(hot[:, k, :, :], sel[:, k, :].unsqueeze(2).broadcast_to([P, T, NX]),
                                         iota[:, 0:NX].unsqueeze(1).broadcast_to([P, T, NX]), ALU.is_equal))
            own.wait()
            V.tensor_tensor(both[:, :].rearrange("p (t e) -> p t e", t=T), hot[:, 0, :, :], hot[:, 1, :, :], ALU.add).then_inc(s["both_ready"], 1)
            own.step(V.memset(run[:, 0, :], 0.0))
            own.step(V.memset(one, 1.0))
            dve.wait_ge(s["sums_ready"], 1)
            for k in range(2):
                own.step(V.tensor_copy(ahead[:, 8 * k:8 * k + 8, :].rearrange("p t e -> p (t e)"), bank[4 + k][:, :]))
                own.step(V.tensor_copy(total[:, 8 * k:8 * k + 8, :].rearrange("p t e -> p (t e)"), bank[6 + k][:, :]))
            own.wait()
            for t in range(T):
                own.link(V.tensor_tensor(run[:, t + 1, :], run[:, t, :], total[:, t, :], ALU.add))
            own.step(V.tensor_tensor(ahead[:, :, :], ahead[:, :, :], run[:, 0:T, :], ALU.add))
            own.link(V.tensor_scalar(nb_i[:, :], run[:, T, :], float(CAP), float(P - 1), ALU.min, ALU.add))
            own.link(V.tensor_scalar(nb_i[:, :], nb_i[:, :], P.bit_length() - 1, None, ALU.arith_shift_right))
            own.link(V.tensor_copy(nb, nb_i[:, :]))
            own.link(V.tensor_tensor_scan(bend, one, nb, 0.0, ALU.mult, ALU.add))
            own.link(V.tensor_tensor(bstart, bend, nb, ALU.subtract))
            own.step(V.tensor_tensor(prod[:, 0, :, :], hot[:, 0, :, :], ahead[:, :, :], ALU.mult))
            own.link(V.tensor_tensor(ahead[:, :, :], ahead[:, :, :], hot[:, 0, :, :], ALU.add))
            own.link(V.tensor_tensor(prod[:, 1, :, :], hot[:, 1, :, :], ahead[:, :, :], ALU.mult))
            own.link(V.tensor_reduce(place[:, :, :], prod[:, :, :, :], AX.X, ALU.add))
            for k in range(2):
                own.step(V.tensor_tensor(prod[:, k, :, :], hot[:, k, :, :], bstart.unsqueeze(1).broadcast_to([P, T, NX]), ALU.mult))
            own.wait()
            own.step(V.tensor_reduce(first[:, :, :], prod[:, :, :, :], AX.X, ALU.add))
            own.link(V.tensor_scalar(keep[:, :, :], place[:, :, :], float(CAP), None, ALU.is_lt))
            own.link(V.scalar_tensor_tensor(place[:, :, :], first[:, :, :], float(P), place[:, :, :], ALU.mult, ALU.add))
            own.link(V.tensor_tensor(place[:, :, :], place[:, :, :], keep[:, :, :], ALU.mult))
            own.step(V.tensor_copy(y_idx[:, 0:2 * T].rearrange("p (t k) -> p k t", k=2), place[:, :, :]))
            own.step(V.memset(y_idx[:, 2 * T:], 0))
            own.step(V.tensor_scalar(gain[:, :].rearrange("p (t k) -> p k t", k=2), keep[:, :, :], 0.5, None, ALU.mult))
            own.link(V.tensor_copy(slot_i[:, :, :], place[:, :, :]))
            own.step(V.tensor_scalar(lo_i[:, :, :], slot_i[:, :, :], P - 1, None, ALU.bitwise_and))
            own.link(V.tensor_scalar(hi_i[:, :, :], slot_i[:, :, :], P.bit_length() - 1, None, ALU.arith_shift_right))
            own.link(V.scalar_tensor_tensor(row[:, :, :], lo_i[:, :, :], float(NB), hi_i[:, :, :], ALU.mult, ALU.add))
            own.link(V.tensor_tensor(row[:, :, :], row[:, :, :], trash[:, :, :], ALU.subtract))
            own.link(V.tensor_tensor(row[:, :, :], row[:, :, :], keep[:, :, :], ALU.mult))
            V.tensor_tensor(row_i[:, :, :], row[:, :, :], trash[:, :, :], ALU.add).then_inc(s["row_ready"], 1)
            own.link(V.tensor_tensor(bmask[:, :, :], iota_blk[:, :].unsqueeze(2).broadcast_to([P, NB, NX]),
                                     bend.unsqueeze(1).broadcast_to([P, NB, NX]), ALU.is_ge))
            own.link(V.tensor_reduce(bexp[:, :], bmask[:, :, :], AX.X, ALU.add))
            own.link(V.tensor_scalar(bexp[:, :], bexp[:, :], float(NX - 1), None, ALU.min))
            own.link(V.tensor_copy(block_expert[:, :], bexp[:, :]))

        @block.scalar
        def _(act):
            A = nc.scalar
            act.sem_inc(s["xn_ready"], LEAD)
            act.sem_inc(s["xT_ready"], LEAD)
            act.wait_ge(s["shift_ready"], 1)
            with act.Fori(0, T // 2) as i:
                for u in two:
                    t = i * 2 + u
                    retired(act, s["xT_ps"], t)
                    A.activation(xn[u][:, :], x[:, bass.ds(t, 1), :].rearrange("p a d -> p (a d)"), ACT.Identity,
                                 bias=shift[:, bass.ds(t, 1)], scale=rstd[:, bass.ds(t, 1)]).then_inc(s["xn_ready"], 1)
                for u in two:
                    t = i * 2 + u
                    made(act, s["xT_ps"], t)
                    retired(act, s["logit_ps"], t)
                    A.activation(xT[u][:, :, :].rearrange("p k n -> p (k n)"), bank[u][:, :], ACT.Copy).then_inc(s["xT_ready"], 1)

        @block.tensor
        def _(pe):
            M = nc.tensor
            pe.sem_inc(s["xT_ps"], LEAD)
            pe.sem_inc(s["logit_ps"], LEAD)
            pe.wait_ge(s["weights_in"], 16)
            with pe.Fori(0, T // 2) as i:
                for u in two:
                    t = i * 2 + u
                    made(pe, s["xn_ready"], t)
                    for k in range(K):
                        last = M.transpose(bank[u][:, k * P:(k + 1) * P], xn[u][:, k * P:(k + 1) * P], ident[:, :])
                    last.then_inc(s["xT_ps"], 1)
                for u in two:
                    t = i * 2 + u
                    made(pe, s["xT_ready"], t)
                    retired(pe, s["taken"], t)
                    for k in range(K):
                        last = M.matmul(bank[2 + u][:, 0:NH * NX], xT[u][:, k, :], hp[:, k, :], start=(k == 0), stop=(k == K - 1))
                    last.then_inc(s["logit_ps"], 1)
            pe.wait_ge(s["consts_made"], 6)
            pe.wait_ge(s["both_ready"], 1)
            for k in range(2):
                M.matmul(bank[4 + k][:, :], lower[:, :], both[:, k * 512:(k + 1) * 512], start=True, stop=True)
                last = M.matmul(bank[6 + k][:, :], ones[:, :], both[:, k * 512:(k + 1) * 512], start=True, stop=True)
            last.then_inc(s["sums_ready"], 1)


def layer1_experts(nc, v):
    ident, bank, tok_idx, block_expert = (v[k] for k in ("ident", "bank", "tok_idx", "block_expert"))
    xn_dram, y_dram = v["xn_dram"], v["y_dram"]
    QUADS = 4
    two = range(2)
    with ExitStack() as ctx:
        sb, sem = allocators(nc, ctx, "experts1")
        rows = [sb(f"rows{q}", [P, 4, D]) for q in range(QUADS)]
        idx = [sb(f"idx{q}", [P, 4], I32) for q in range(QUADS)]
        w1 = [sb(f"w1{r}", [P, K, HX]) for r in range(4)]
        w2 = [sb(f"w2{r}", [HX, D]) for r in range(4)]
        xT = [sb(f"xT{u}", [P, K, P]) for u in two]
        hT = [sb(f"hT{u}", [HX, P]) for u in two]
        y = [sb(f"y{r}", [P, D]) for r in range(4)]
        names = ("idx_ready", "gate", "xT_ps", "xT_ready", "h_ps", "h_ready", "y_ps", "y_ready")
        s = {n: sem(n) for n in names}
        gathered = [sem(f"gathered{q}") for q in range(QUADS)]
        w_in = [sem(f"w_in{r}") for r in range(4)]
        y_stored = [sem(f"y_stored{r}") for r in range(4)]
        block = ctx.enter_context(nc.Block())

        @block.sync
        def _(sp):
            def load(i, r):
                b = i * 4 + r
                retired(sp, s["y_ps"], b, ring=4, lead=4)
                e = sp.value_load(block_expert[0:1, bass.ds(b, 1)], min_val=0, max_val=NX - 1)
                sp.dma_start(w1[r][:, :, :].rearrange("p k h -> p (k h)"), v["x1_in"][bass.ds(e, 1), :, :].rearrange("a p c -> (a p) c")).then_inc(w_in[r], 16)
                sp.dma_start(w2[r][:, :], v["x2_in"][bass.ds(e, 1), :, :].rearrange("a p c -> (a p) c")).then_inc(w_in[r], 16)

            def store(i, r):
                b = i * 4 + r
                made(sp, s["y_ready"], b, lead=4)
                sp.dma_start(y_dram[bass.ds(b * P, P), :], y[r][:, :]).then_inc(y_stored[r], 16)

            for r in range(4):
                load(0, r)
            with sp.Fori(1, NB // 4) as i:
                for r in range(4):
                    store(i - 1, r)
                    load(i, r)
            for r in range(4):
                store(NB // 4 - 1, r)
            for r in range(4):
                sp.wait_ge(y_stored[r], 16 * NB // 4)

        @block.gpsimd
        def _(gp):
            gather_quads(nc, gp, s, gathered, QUADS, NB, rows, idx, tok_idx, xn_dram, s["xT_ps"], 4)

        @block.vector
        def _(dve):
            dve.sem_inc(s["y_ready"], 4)

            def four(i, first):
                for r in range(4):
                    b = i * 4 + r
                    made(dve, s["y_ps"], b, lead=4)
                    if not first:
                        dve.wait_ge(y_stored[r], i * 16)
                    nc.vector.tensor_copy(y[r][:, :], bank[4 + r][:, :]).then_inc(s["y_ready"], 1)

            four(0, True)
            with dve.Fori(1, NB // 4) as i:
                four(i, False)

        @block.scalar
        def _(act):
            A = nc.scalar
            act.sem_inc(s["xT_ready"], LEAD)
            act.sem_inc(s["h_ready"], LEAD)

            def turned(i):
                for u in two:
                    b = i * 2 + u
                    made(act, s["xT_ps"], b, lead=4 * QUADS)
                    retired(act, s["h_ps"], b)
                    A.activation(xT[u][:, :, :].rearrange("p k n -> p (k n)"), bank[u][:, :], ACT.Copy).then_inc(s["xT_ready"], 1)

            def hidden(i):
                for u in two:
                    b = i * 2 + u
                    made(act, s["h_ps"], b)
                    retired(act, s["y_ps"], b, ring=2, lead=4)
                    A.activation(hT[u][:, :], bank[2 + u][0:HX, 0:P], ACT.Gelu).then_inc(s["h_ready"], 1)

            turned(0)
            with act.Fori(0, NB // 2 - 1) as i:
                hidden(i)
                turned(i + 1)
            hidden(NB // 2 - 1)

        @block.tensor
        def _(pe):
            M = nc.tensor
            pe.sem_inc(s["xT_ps"], 4 * QUADS)
            pe.sem_inc(s["h_ps"], LEAD)
            pe.sem_inc(s["y_ps"], 4)

            def turn(i, j):
                b = i * 16 + j * 2
                for u in two:
                    q, r = j // 2, 2 * (j % 2) + u
                    pe.wait_ge(gathered[q], i * 64 + 64)
                    retired(pe, s["xT_ready"], b + u)
                    for k in range(K):
                        last = M.transpose(bank[u][:, k * P:(k + 1) * P], rows[q][:, r, k:D:K], ident[:, :])
                    last.then_inc(s["xT_ps"], 1)

            def hidden(i, j):
                for u in two:
                    b, r = i * 16 + j * 2 + u, (2 * j + u) % 4
                    made(pe, s["xT_ready"], b)
                    retired(pe, s["h_ready"], b)
                    pe.wait_ge(w_in[r], (i * 4 + (2 * j + u) // 4) * 32 + 32)
                    for k in range(K):
                        last = M.matmul(bank[2 + u][0:HX, 0:P], w1[r][:, k, :], xT[u][:, k, :], start=(k == 0), stop=(k == K - 1))
                    last.then_inc(s["h_ps"], 1)

            def result(i, j):
                for u in two:
                    b, r = i * 16 + j * 2 + u, (2 * j + u) % 4
                    made(pe, s["h_ready"], b)
                    retired(pe, s["y_ready"], b, ring=4, lead=4)
                    M.matmul(bank[4 + r][:, :], hT[u][:, :], w2[r][:, :], start=True, stop=True).then_inc(s["y_ps"], 1)

            steps = NB // 16
            turn(0, 0)
            with pe.Fori(0, steps - 1) as i:
                for j in range(8):
                    hidden(i, j)
                    if j < 7:
                        turn(i, j + 1)
                    else:
                        turn(i + 1, 0)
                    result(i, j)
            for j in range(8):
                hidden(steps - 1, j)
                if j < 7:
                    turn(steps - 1, j + 1)
                result(steps - 1, j)


def layer1_combine(nc, v):
    x, y_idx, gain = (v[k] for k in ("x", "y_idx", "gain"))
    QUADS = 4
    with ExitStack() as ctx:
        sb, sem = allocators(nc, ctx, "combine1")
        rows = [sb(f"rows{q}", [P, 4, D]) for q in range(QUADS)]
        idx = [sb(f"idx{q}", [P, 4], I32) for q in range(QUADS)]
        s = {n: sem(n) for n in ("idx_ready", "gate", "added", "out_stored")}
        gathered = [sem(f"gathered{q}") for q in range(QUADS)]
        block = ctx.enter_context(nc.Block())

        @block.gpsimd
        def _(gp):
            gather_quads(nc, gp, s, gathered, QUADS, 2 * T, rows, idx, y_idx, v["y_dram"], s["added"], 4)

        @block.vector
        def _(dve):
            dve.sem_inc(s["added"], 4 * QUADS)
            with dve.Fori(0, 2 * T // (4 * QUADS)) as i:
                for r in range(4 * QUADS):
                    n = i * (4 * QUADS) + r
                    dve.wait_ge(gathered[r // 4], i * 64 + 64)
                    xt = x[:, bass.ds(i * (2 * QUADS) + r // 2, 1), :].rearrange("p a d -> p (a d)")
                    if r % 2:
                        made(dve, s["added"], n - 1, lead=4 * QUADS)
                    nc.vector.scalar_tensor_tensor(xt, rows[r // 4][:, r % 4, :], gain[:, bass.ds(n, 1)], xt,
                                                   ALU.mult, ALU.add).then_inc(s["added"], 1)

        @block.sync
        def _(sp):
            with sp.Fori(0, T // 2) as i:
                made(sp, s["added"], i * 4 + 3, lead=4 * QUADS)
                sp.dma_start(v["out"][bass.ds(i * 2 * P, 2 * P), :].rearrange("(t p) d -> p t d", p=P),
                             x[:, bass.ds(i * 2, 2), :]).then_inc(s["out_stored"], 16)
            sp.wait_ge(s["out_stored"], 16 * T // 2)


def dram_inputs(inputs):
    f = {k: np.ascontiguousarray(a) for k, a in inputs.items()}
    w, y, a20 = f["edge_weight"], f["edge_attr_4"], f["edge_attr_20"]
    rec = np.zeros((E, REC), w.dtype)
    rec[:, R_W], rec[:, R_Y:R_Y + 4], rec[:, R_F:R_F + 20] = w, y, a20
    def chunks(a):
        return a.reshape(K, P).T

    laid = {
        "x_in": f["x"], "to_in": f["src"], "from_in": f["dst"], "rec_in": rec, "wg_in": f["L0_gnn_weight"].T,
        "wg1_in": f["L0_ffn_Wg1"], "bg1_in": f["L0_ffn_bg1"].reshape(-1, 1),
        "wg2_in": f["L0_ffn_Wg2"], "bg2_in": f["L0_ffn_bg2"].reshape(1, -1),
        "w1_in": f["L0_ffn_W1"].transpose(1, 0, 2).reshape(D, D), "b1_in": f["L0_ffn_b1"].reshape(1, D),
        "gb1_in": np.stack([chunks(f["L0_ffn_g1"]), chunks(f["L0_ffn_be1"])], axis=1),
        "w2_in": f["L0_ffn_W2"], "b2_in": f["L0_ffn_b2"].reshape(1, D),
        "g2_in": f["L0_ffn_g2"].reshape(1, D), "be2_in": f["L0_ffn_be2"].reshape(1, D),
        "w_in_in": np.stack([f["L1_gnn_w_in2f_s"], f["L1_gnn_w_in2f_v"]], axis=1),
        "wr_in": f["L1_gnn_W1"], "br_in": np.tile(f["L1_gnn_b1"], 4).reshape(P, 1),
        "wf_in": f["L1_gnn_W2"].reshape(F, F, 6)[:, :, [0, 3, 1, 2]].transpose(0, 2, 1).reshape(F, P),
        "bf_in": np.tile(f["L1_gnn_b2"].reshape(F, 6)[:, [0, 3, 1, 2]].T.reshape(1, P), (1, 4)),
        "w1s_in": f["L1_gnn_w_f2o1_s"], "w1v_in": f["L1_gnn_w_f2o1_v"],
        "w2s_in": f["L1_gnn_w_f2o2_s"], "w2v_in": f["L1_gnn_w_f2o2_v"],
        "hp_in": f["L1_ffn_hash_proj"].transpose(1, 0, 2).reshape(D, NH * NX),
        "x1_in": f["L1_ffn_W1"].reshape(NX, P, K * HX), "x2_in": f["L1_ffn_W2"],
        "w3_in": f["L0_ffn_W3"].reshape(D, D), "b3_in": f["L0_ffn_b3"],
    }
    return {k: np.ascontiguousarray(a) for k, a in laid.items()}


def kernel(**inputs):
    import concourse.bacc as bacc
    from concourse.bass_utils import run_bass_kernel_spmd

    nc = bacc.Bacc("TRN2", target_bir_lowering=False, num_devices=1)
    arrays, args = {}, {}
    for name, a in dram_inputs(inputs).items():
        arrays[name] = a
        args[name] = nc.dram_tensor(name, a.shape, mybir.dt.from_np(a.dtype), kind="ExternalInput").ap()
    args["out"] = nc.dram_tensor("out", (N, D), FP32, kind="ExternalOutput").ap()
    build(nc, args)
    r = run_bass_kernel_spmd(nc, [arrays], core_ids=[0])
    return r.results[0]["out"]
```

```python
import numpy as np
import concourse.bass as bass
from concourse import mybir
from contextlib import ExitStack

FP32 = mybir.dt.float32
BF16 = mybir.dt.bfloat16
I32 = mybir.dt.int32
U32 = mybir.dt.uint32
ALU = mybir.AluOpType
ACT = mybir.ActivationFunctionType
AX = mybir.AxisListType

P = 128
N = 2048
D = 512
T = N // P
K = D // P
E = 32768
J = E // P
B = N // P
GE = 2 * P
G = E // GE + B
ET = 2 * G
REC = 28
R_W, R_Y, R_F, R_FROM, R_TO = 0, 1, 5, 25, 26
EPS = 1e-5


class Chain:

    def __init__(self, eng, sem):
        self.eng, self.sem, self.n, self.i, self.base, self.per = eng, sem, 0, None, 0, 0

    def enter(self, i, per, first=0):
        self.base, self.i, self.per, self.n = self.n, i - first, per, 0

    def leave(self, times):
        assert self.n == self.per, (self.n, self.per)
        self.n, self.i = self.base + self.per * times, None

    def step(self, ins):
        ins.then_inc(self.sem, 1)
        self.n += 1

    def wait(self):
        self.eng.wait_ge(self.sem, self.n if self.i is None else self.i * self.per + (self.base + self.n))

    def link(self, ins):
        self.step(ins)
        self.wait()


LEAD = 2


def made(eng, sem, n, lead=LEAD):
    eng.wait_ge(sem, n + 1 + lead)


def retired(eng, sem, n, ring=LEAD, lead=LEAD):
    eng.wait_ge(sem, n + 1 + lead - ring)


def allocators(nc, ctx, layer):
    def sb(name, shape, dt=FP32):
        return ctx.enter_context(nc.sbuf_tensor(f"{layer}_{name}", shape, dt))

    def sem(name):
        return nc.alloc_semaphore(f"{layer}_{name}")

    return sb, sem


def clear_semaphores(nc, before):
    nc.clear_and_free_semaphores(nc.allocated_since(before))
    nc.all_engine_barrier()


def norm_stats(nc, own, x, stats, mean, rstd, var_ready):
    V = nc.vector
    with nc.vector.Fori(0, T) as t:
        own.enter(t, 1)
        own.step(V.bn_stats(stats[:, bass.ds(t, 1), :], x[:, bass.ds(t, 1), :]))
        own.leave(T)
    own.wait()
    me, ve, mo, vo = stats[:, :, 1], stats[:, :, 2], stats[:, :, 4], stats[:, :, 5]
    own.step(V.tensor_tensor(mean, me, mo, ALU.add))
    own.link(V.tensor_tensor(rstd, me, mo, ALU.subtract))
    own.step(V.tensor_scalar(mean, mean, 0.5, None, ALU.mult))
    own.step(V.tensor_tensor(stats[:, :, 0], ve, vo, ALU.add))
    own.link(V.scalar_tensor_tensor(rstd, rstd, 0.25, rstd, ALU.mult, ALU.mult))
    own.link(V.scalar_tensor_tensor(rstd, stats[:, :, 0], 1.0 / D, rstd, ALU.mult, ALU.add))
    V.tensor_scalar(rstd, rstd, EPS, None, ALU.add).then_inc(var_ready, 1)


def build(nc, dram):
    with ExitStack() as ctx:
        sb, sem = allocators(nc, ctx, "all")
        rec_dram = nc.dram_tensor("rec_dram", [P * ET, REC], FP32, kind="Internal").ap()
        h_dram = nc.dram_tensor("h_dram", [N, D], FP32, kind="Internal").ap()
        feat_dram = nc.dram_tensor("feat_dram", [N, P], FP32, kind="Internal").ap()
        xn_dram = nc.dram_tensor("xn_dram", [N, D], FP32, kind="Internal").ap()
        tok_dram = nc.dram_tensor("tok_dram", [P * NB + 2 * N, 1], I32, kind="Internal").ap()
        y_dram = nc.dram_tensor("y_dram", [NB * P, D], FP32, kind="Internal").ap()

        x = sb("x", [P, T, D])
        ident = sb("ident", [P, P])
        iota = sb("iota", [P, P])
        edges = sb("edges", [P, ET, REC])
        from_idx = sb("from_idx", [P, ET + 16], I32)
        to_loc = sb("to_loc", [P, ET])
        group_tile = sb("group_tile", [P, G])
        group_tile_i = sb("group_tile_i", [P, G], I32)
        stats = sb("stats", [P, T, 6])
        mean = sb("mean", [P, T])
        rstd = sb("rstd", [P, T])
        shift = sb("shift", [P, T])
        neghalf = sb("neghalf", [P, P])
        bank = [ctx.enter_context(nc.psum_tensor(f"bank{k}", [P, 512], FP32)) for k in range(8)]

        v = {**dram, **locals()}
        before = nc.snapshot_sems()
        layer0_prepare(nc, v)
        with ExitStack() as layer1:
            v["hT"] = layer1.enter_context(nc.sbuf_tensor("hT", [P, F * ET], FP32))
            layer0_edges(nc, v)
            layer0_ffn(nc, v)
            clear_semaphores(nc, before)
            v["agg"] = layer1.enter_context(nc.sbuf_tensor("agg", [P, T, 8 * F], FP32))
            layer1_features(nc, v)
            layer1_edges(nc, v)
            layer1_nodes(nc, v)
        with ExitStack() as ffn1:
            def sb(name, shape, dt):
                return ffn1.enter_context(nc.sbuf_tensor(name, shape, dt))

            v["tok_idx"] = sb("tok_idx", [P, NB + 16], I32)
            v["y_idx"] = sb("y_idx", [P, 2 * T + 16], I32)
            v["gain"] = sb("gain", [P, 2 * T], FP32)
            v["block_expert"] = sb("block_expert", [P, NB], I32)
            layer1_route(nc, v)
            layer1_experts(nc, v)
            layer1_combine(nc, v)


def layer0_prepare(nc, v):
    x_in, to_in, from_in, rec_in, wg_in = (v[k] for k in ("x_in", "to_in", "from_in", "rec_in", "wg_in"))
    x, ident, iota, edges, from_idx, to_loc = (v[k] for k in ("x", "ident", "iota", "edges", "from_idx", "to_loc"))
    group_tile, group_tile_i = v["group_tile"], v["group_tile_i"]
    stats, mean, rstd, neghalf, bank = v["stats"], v["mean"], v["rstd"], v["neghalf"], v["bank"]
    rec_dram, h_dram = v["rec_dram"], v["h_dram"]
    with ExitStack() as ctx:
        sb, sem = allocators(nc, ctx, "prepare")
        rec = sb("rec", [P, J, REC])
        from_i, to_i, bkt_i = (sb(n, [P, J], I32) for n in ("from_i", "to_i", "bkt_i"))
        bkt = sb("bkt", [P, J])
        h = sb("h", [P, T, D])
        h_flat = h[:, :, :].rearrange("p t d -> p (t d)")
        mask = h_flat[:, 0:B * J].rearrange("p (b j) -> p b j", b=B)
        scan = h_flat[:, B * J:2 * B * J]
        ones_row = sb("ones_row", [P, B * J], BF16)
        pos = sb("pos", [P, J])
        pos_i, slot_i = (sb(n, [P, J], I32) for n in ("pos_i", "slot_i"))
        iota_b = sb("iota_b", [P, B])
        iota_g = sb("iota_g", [P, G])
        ones = sb("ones", [P, P])
        lower = sb("lower", [P, P])
        small = sb("small", [P, 7, B])
        cnt, lscan, pre, tot, adj, ng, gend = (small[:, k, :] for k in range(7))
        ng_i = sb("ng_i", [P, B], I32)
        gmask = sb("gmask", [P, G, B])
        STAGES, SB = 2, 16
        stage_rec = sb("stage_rec", [P, STAGES, SB, REC])
        stage_pos = sb("stage_pos", [P, STAGES, SB], I32)
        wg = sb("wg", [P, K, D])
        xn = [sb(f"xn{u}", [P, D]) for u in range(2)]
        xT = [sb(f"xT{u}", [P, K, P]) for u in range(2)]

        ends_in, rec_landed, x_landed, wg_landed = (sem(n) for n in ("ends_in", "rec_landed", "x_landed", "wg_landed"))
        consts_made, pool_own, dve_own = sem("consts_made"), sem("pool_own"), sem("dve_own")
        ends_filled, cnt_ready, sums_ready, pos_ready = (
            sem(n) for n in ("ends_filled", "cnt_ready", "sums_ready", "pos_ready"))
        pad_made, pad_written, stage_full, gate, rec_sorted = (
            sem(n) for n in ("pad_made", "pad_written", "stage_full", "gate", "rec_sorted"))
        stage_sent = [sem(f"stage_sent{q}") for q in range(STAGES)]
        edges_in, var_ready, rstd_ready = (sem(n) for n in ("edges_in", "var_ready", "rstd_ready"))
        xn_ready, xT_ps, xT_ready, h_ps, h_ready, h_stored = (
            sem(n) for n in ("xn_ready", "xT_ps", "xT_ready", "h_ps", "h_ready", "h_stored"))
        block = ctx.enter_context(nc.Block())

        @block.sync
        def _(sp):
            sp.dma_start(to_i[:, :], to_in.rearrange("(p j) -> p j", p=P)).then_inc(ends_in, 16)
            sp.dma_start(from_i[:, :], from_in.rearrange("(p j) -> p j", p=P)).then_inc(ends_in, 16)
            sp.dma_start(x[:, :, :], x_in.rearrange("(t p) d -> p t d", p=P)).then_inc(x_landed, 16)
            sp.dma_start(rec[:, :, :], rec_in.rearrange("(p j) c -> p j c", p=P)).then_inc(rec_landed, 16)
            sp.dma_start(wg[:, :, :], wg_in.rearrange("(k p) e -> p k e", p=P)).then_inc(wg_landed, 16)
            with sp.Fori(0, T) as t:
                made(sp, h_ready, t)
                sp.dma_start(h_dram[bass.ds(t * P, P), :], h[:, bass.ds(t, 1), :].rearrange("p a d -> p (a d)")).then_inc(h_stored, 16)
            sp.wait_ge(rec_sorted, 1)
            sp.dma_start(edges[:, :, :].rearrange("p t c -> p (t c)"), rec_dram.rearrange("(p t) c -> p (t c)", p=P)).then_inc(edges_in, 16)
            sp.wait_ge(h_stored, 16 * T)
            sp.wait_ge(edges_in, 16)

        @block.gpsimd
        def _(gp):
            own = Chain(gp, pool_own)
            nc.gpsimd.iota(iota[:, :], [[1, P]], base=0, channel_multiplier=0, allow_small_or_imprecise_dtypes=True).then_inc(consts_made, 1)
            nc.gpsimd.iota(iota_b[:, :], [[1, B]], base=0, channel_multiplier=0, allow_small_or_imprecise_dtypes=True).then_inc(consts_made, 1)
            nc.gpsimd.iota(iota_g[:, :], [[1, G]], base=0, channel_multiplier=0, allow_small_or_imprecise_dtypes=True).then_inc(consts_made, 1)
            nc.gpsimd.memset(ones_row[:, :], 1.0).then_inc(consts_made, 1)
            nc.gpsimd.memset(neghalf[:, :], -0.5).then_inc(consts_made, 1)
            own.step(nc.gpsimd.memset(ones[:, :], 1.0))
            own.step(nc.gpsimd.memset(ident[:, :], 0.0))
            own.link(nc.gpsimd.memset(edges[:, :, :], 0.0))
            nc.gpsimd.memset(edges[:, :, R_TO:R_TO + 1], -1.0).then_inc(pad_made, 1)
            nc.gpsimd.affine_select(out=lower[:, :], in_=ones[:, :], compare_op=ALU.is_gt, fill=0.0, base=0,
                                    pattern=[[1, P]], channel_multiplier=-1).then_inc(consts_made, 1)
            nc.gpsimd.affine_select(out=ident[:, :], in_=ident[:, :], compare_op=ALU.not_equal, fill=1.0, base=0,
                                    pattern=[[-1, P]], channel_multiplier=1).then_inc(consts_made, 1)
            gp.wait_ge(pad_made, 1)
            gp.dma_start(rec_dram.rearrange("(p t) c -> p (t c)", p=P), edges[:, :, :].rearrange("p t c -> p (t c)")).then_inc(pad_written, 16)
            gp.wait_ge(var_ready, 1)
            nc.gpsimd.tensor_tensor(rstd[:, :], rstd[:, :], neghalf[:, 0:T], ALU.pow).then_inc(rstd_ready, 1)
            gp.wait_ge(ends_filled, 2)
            gp.wait_ge(pos_ready, 1)
            def stage(j, q):
                at = (j * STAGES + q) * SB
                nc.gpsimd.tensor_copy(stage_rec[:, q, :, :], rec[:, bass.ds(at, SB), :]).then_inc(stage_full, 1)
                nc.gpsimd.tensor_copy(stage_pos[:, q, :], pos_i[:, bass.ds(at, SB)]).then_inc(stage_full, 1)

            def place(j, q, refill):
                gp.wait_ge(stage_full, (j * STAGES + q) * 2 + 2)
                gp.sem_inc(gate, 1)
                for k in range(SB):
                    gp.indirect_dma_start(out=rec_dram, in_=stage_rec[:, q, k, :], in_offset=None,
                                          out_offset=bass.IndirectOffsetOnAxis(ap=stage_pos[:, q, k:k + 1], axis=0)
                                          ).then_inc(stage_sent[q], 16)
                    if refill and k == SB // 2:
                        if refill == "again":
                            gp.wait_ge(stage_sent[1 - q], (j + q) * (16 * SB))
                            gp.sem_inc(gate, 1)
                        stage(j + q, 1 - q)

            gp.wait_ge(pad_written, 16)
            stage(0, 0)
            place(0, 0, "new")
            place(0, 1, "again")
            with gp.Fori(1, J // SB // STAGES - 1) as j:
                for q in range(STAGES):
                    place(j, q, "again")
            last = J // SB // STAGES - 1
            place(last, 0, "again")
            place(last, 1, "")
            for q in range(STAGES):
                gp.wait_ge(stage_sent[q], 16 * J // STAGES)
            gp.sem_inc(rec_sorted, 1)

        @block.vector
        def _(dve):
            own = Chain(dve, dve_own)
            V = nc.vector
            dve.sem_inc(xn_ready, LEAD)
            dve.sem_inc(h_ready, LEAD)
            dve.wait_ge(ends_in, 32)
            own.link(V.tensor_scalar(bkt_i[:, :], to_i[:, :], 7, None, ALU.arith_shift_right))
            own.link(V.tensor_copy(bkt[:, :], bkt_i[:, :]))
            dve.wait_ge(consts_made, 7)
            own.link(V.tensor_tensor(mask, bkt[:, :].unsqueeze(1).broadcast_to([P, B, J]),
                                     iota_b[:, :].unsqueeze(2).broadcast_to([P, B, J]), ALU.is_equal))
            V.tensor_reduce(cnt, mask, AX.X, ALU.add).then_inc(cnt_ready, 1)
            own.link(V.tensor_tensor_scan(scan, ones_row[:, :], h_flat[:, 0:B * J], 0.0, ALU.mult, ALU.add))
            dve.wait_ge(cnt_ready, 1)
            own.step(V.tensor_tensor_scan(lscan, ones_row[:, 0:B], cnt, 0.0, ALU.mult, ALU.add))
            dve.wait_ge(sums_ready, 1)
            own.link(V.tensor_copy(small[:, 2:4, :], bank[7][:, 0:2 * B].rearrange("p (a b) -> p a b", a=2)))
            own.link(V.tensor_scalar(ng_i[:, :], tot, float(GE - 1), None, ALU.add))
            own.link(V.tensor_scalar(ng_i[:, :], ng_i[:, :], GE.bit_length() - 1, None, ALU.arith_shift_right))
            own.link(V.tensor_copy(ng, ng_i[:, :]))
            own.link(V.tensor_tensor_scan(gend, ones_row[:, 0:B], ng, 0.0, ALU.mult, ALU.add))
            own.link(V.tensor_tensor(adj, gend, ng, ALU.subtract))
            own.link(V.scalar_tensor_tensor(adj, adj, float(GE), pre, ALU.mult, ALU.add))
            own.link(V.tensor_tensor(adj, adj, cnt, ALU.add))
            own.link(V.scalar_tensor_tensor(adj, adj, -1.0, lscan, ALU.add, ALU.subtract))
            sc3 = scan.rearrange("p (b j) -> p b j", b=B)
            own.link(V.tensor_tensor(sc3, sc3, adj.unsqueeze(2).broadcast_to([P, B, J]), ALU.add))
            own.link(V.tensor_tensor(sc3, sc3, mask, ALU.mult))
            own.link(V.tensor_reduce(pos[:, :], scan.rearrange("p (b j) -> p j b", b=B), AX.X, ALU.add))
            own.link(V.tensor_copy(slot_i[:, :], pos[:, :]))
            own.step(V.tensor_scalar(pos_i[:, :], slot_i[:, :], P - 1, None, ALU.bitwise_and))
            own.link(V.tensor_scalar(slot_i[:, :], slot_i[:, :], P.bit_length() - 1, None, ALU.arith_shift_right))
            V.scalar_tensor_tensor(pos_i[:, :], pos_i[:, :], float(ET), slot_i[:, :], ALU.mult, ALU.add).then_inc(pos_ready, 1)
            own.link(V.tensor_tensor(gmask[:, :, :], iota_g[:, :].unsqueeze(2).broadcast_to([P, G, B]),
                                     gend.unsqueeze(1).broadcast_to([P, G, B]), ALU.is_ge))
            own.link(V.tensor_reduce(group_tile[:, :], gmask[:, :, :], AX.X, ALU.add))
            own.link(V.tensor_scalar(group_tile[:, :], group_tile[:, :], float(B - 1), None, ALU.min))
            own.link(V.tensor_copy(group_tile_i[:, :], group_tile[:, :]))
            dve.wait_ge(rec_landed, 16)
            V.tensor_copy(rec[:, :, R_FROM], from_i[:, :]).then_inc(ends_filled, 1)
            V.tensor_copy(rec[:, :, R_TO], to_i[:, :]).then_inc(ends_filled, 1)
            dve.wait_ge(x_landed, 16)
            norm_stats(nc, own, x, stats, mean[:, :], rstd[:, :], var_ready)
            dve.wait_ge(rstd_ready, 1)
            with dve.Fori(0, T // 2) as i:
                for u in range(2):
                    t = i * 2 + u
                    retired(dve, xT_ps, t)
                    V.tensor_scalar(xn[u][:, :], x[:, bass.ds(t, 1), :].rearrange("p a d -> p (a d)"),
                                    mean[:, bass.ds(t, 1)], rstd[:, bass.ds(t, 1)],
                                    ALU.subtract, ALU.mult).then_inc(xn_ready, 1)
                for u in range(2):
                    t = i * 2 + u
                    made(dve, h_ps, t)
                    V.tensor_copy(h[:, bass.ds(t, 1), :].rearrange("p a d -> p (a d)"), bank[2 + u][:, :]).then_inc(h_ready, 1)

        @block.scalar
        def _(act):
            act.sem_inc(xT_ready, LEAD)
            with act.Fori(0, T // 2) as i:
                for u in range(2):
                    t = i * 2 + u
                    made(act, xT_ps, t)
                    retired(act, h_ps, t)
                    nc.scalar.activation(xT[u][:, :, :].rearrange("p k n -> p (k n)"), bank[u][:, :], ACT.Copy).then_inc(xT_ready, 1)

        @block.tensor
        def _(pe):
            pe.sem_inc(xT_ps, LEAD)
            pe.sem_inc(h_ps, LEAD)
            pe.wait_ge(consts_made, 7)
            pe.wait_ge(cnt_ready, 1)
            nc.tensor.matmul(bank[7][:, 0:B], lower[:, :], cnt, start=True, stop=True)
            nc.tensor.matmul(bank[7][:, B:2 * B], ones[:, :], cnt, start=True, stop=True).then_inc(sums_ready, 1)
            pe.wait_ge(wg_landed, 16)
            with pe.Fori(0, T // 2) as i:
                for u in range(2):
                    t = i * 2 + u
                    made(pe, xn_ready, t)
                    retired(pe, xT_ready, t)
                    for k in range(K):
                        last = nc.tensor.transpose(bank[u][:, k * P:(k + 1) * P], xn[u][:, k * P:(k + 1) * P], ident[:, :])
                    last.then_inc(xT_ps, 1)
                for u in range(2):
                    t = i * 2 + u
                    made(pe, xT_ready, t)
                    retired(pe, h_ready, t)
                    for k in range(K):
                        last = nc.tensor.matmul(bank[2 + u][:, :], xT[u][:, k, :], wg[:, k, :], start=(k == 0), stop=(k == K - 1))
                    last.then_inc(h_ps, 1)


def gather_quads(nc, gp, s, gathered, tiles, rows, idx, from_idx, table, used, per):
    def copy_idx(turn, h):
        nc.gpsimd.tensor_copy(idx[h][:, :], from_idx[:, bass.ds(turn * 16, 16)]).then_inc(s["idx_ready"], 1)

    def ring(i, h, first):
        turn = i * 2 + h
        gp.wait_ge(s["idx_ready"], turn + 1)
        gp.sem_inc(s["gate"], 1)
        for q in range(4):
            gp.wait_ge(used, (turn * 4 + q + 1) * per)
            gp.sem_inc(s["gate"], 1)
            for r in range(4):
                gp.indirect_dma_start(out=rows[q][:, r, :], out_offset=None, in_=table,
                                      in_offset=bass.IndirectOffsetOnAxis(ap=idx[h][:, 4 * q + r:4 * q + r + 1], axis=0)).then_inc(gathered[q], 16)
            if q == 1:
                if not (first and h == 0):
                    for b in range(4):
                        gp.wait_ge(gathered[b], turn * 64)
                    gp.sem_inc(s["gate"], 1)
                copy_idx(turn + 1, 1 - h)

    copy_idx(0, 0)
    for h in range(2):
        ring(0, h, True)
    if tiles > 32:
        with gp.Fori(1, tiles // 32) as i:
            for h in range(2):
                ring(i, h, False)


def softplus_less_log2(nc, act, own, out, tmp, in_, scale=1.0):
    own.link(nc.scalar.activation(tmp, in_, ACT.Abs, scale=scale))
    own.link(nc.scalar.activation(tmp, tmp, ACT.Exp, scale=-1.0))
    return nc.scalar.activation(out, tmp, ACT.Ln, scale=0.5, bias=0.5)


def layer0_edges(nc, v):
    ident, hT = v["ident"], v["hT"]
    x, iota, edges, from_idx, to_loc = (v[k] for k in ("x", "iota", "edges", "from_idx", "to_loc"))
    group_tile, group_tile_i, bank, h_dram = v["group_tile"], v["group_tile_i"], v["bank"], v["h_dram"]
    QUADS = 4
    RING = 4 * QUADS
    with ExitStack() as ctx:
        sb, sem = allocators(nc, ctx, "edges0")
        rows = [sb(f"rows{q}", [P, 4, D]) for q in range(QUADS)]
        idx = [sb(f"idx{h}", [P, 16], I32) for h in range(2)]
        S = [sb(f"S{r}", [P, P]) for r in range(8)]
        wr = sb("wr", [4 * RT, P])
        br = sb("br", [P, 1])
        fr = sb("fr", [P, RING, RT])
        fT = sb("fT", [4 * RT, 4 * P])
        pre, soft = (sb(n, [P, 4 * P]) for n in ("pre", "soft"))
        x_flat = x[:, :, :].rearrange("p t d -> p (t d)")
        prepared = sem("prepared")
        s = {n: sem(n) for n in ("idx_ready", "gate", "wr_zero", "wr_in", "act_own", "fr_ready", "fT_ps", "fT_ready", "pre_ps", "pre_ready",
                                 "soft_ready", "hT_ready")}
        gathered = [sem(f"gathered{q}") for q in range(QUADS)]
        S_ready, sum_ready, sum_added = sem("S_ready"), sem("sum_ready"), sem("sum_added")
        block = ctx.enter_context(nc.Block())

        @block.vector
        def _(dve):
            V = nc.vector
            dve.sem_inc(sum_added, 4)
            V.memset(from_idx[:, ET:], 0).then_inc(prepared, 1)
            V.tensor_copy(from_idx[:, 0:ET], edges[:, :, R_FROM]).then_inc(prepared, 1)
            e_to = edges[:, :, R_TO].rearrange("p (g k) -> p g k", k=2)
            V.scalar_tensor_tensor(to_loc[:, :].rearrange("p (g k) -> p g k", k=2),
                                   group_tile[:, :].unsqueeze(2).broadcast_to([P, G, 2]), -float(P), e_to,
                                   ALU.mult, ALU.add).then_inc(prepared, 1)
            dve.wait_ge(prepared, 3)
            V.memset(wr[:, :], 0.0).then_inc(s["wr_zero"], 1)
            dve.wait_ge(s["wr_in"], 80)

            def weights(i, pair):
                for u in range(2):
                    g = i * (RING // 2) + pair * 2 + u
                    retired(dve, sum_ready, g, ring=4, lead=RING // 2)
                    for k in range(2):
                        e = g * 2 + k
                        V.tensor_scalar(S[pair % 2 * 4 + 2 * u + k][:, :], iota[:, :], to_loc[:, bass.ds(e, 1)],
                                        edges[:, bass.ds(e, 1), R_W], ALU.is_equal, ALU.mult).then_inc(S_ready, 1)

            def add(i, pair):
                for u in range(2):
                    g = i * (RING // 2) + pair * 2 + u
                    col = dve.value_load(group_tile_i[0:1, bass.ds(g, 1)], min_val=0, max_val=T - 1) * D
                    made(dve, sum_ready, g, lead=RING // 2)
                    retired(dve, sum_added, g, ring=1, lead=4)
                    V.tensor_tensor(x_flat[:, bass.ds(col, D)], x_flat[:, bass.ds(col, D)],
                                    bank[pair % 2 * 2 + u][:, :], ALU.add).then_inc(sum_added, 1)

            def hidden(i):
                dve.wait_ge(s["soft_ready"], i + 1)
                V.scalar_tensor_tensor(hT[:, bass.ds(i * 4 * P, 4 * P)], pre[:, :], 0.0, soft[:, :],
                                       ALU.max, ALU.add).then_inc(s["hT_ready"], 1)

            def pairs(i, first):
                for pair in range(RING // 4):
                    weights(i, pair)
                    if pair == 0:
                        if not first:
                            add(i - 1, RING // 4 - 1)
                            hidden(i - 1)
                        V.tensor_copy(fr[:, :, :], edges[:, bass.ds(i * RING, RING), R_F:R_F + RT]).then_inc(s["fr_ready"], 1)
                    else:
                        add(i, pair - 1)
                    if pair == 3:
                        dve.wait_ge(s["pre_ps"], i + 1)
                        V.tensor_scalar(pre[:, :], bank[6][:, :], br[:, 0:1], None, ALU.add).then_inc(s["pre_ready"], 1)

            pairs(0, True)
            with dve.Fori(1, ET // RING) as i:
                pairs(i, False)
            add(ET // RING - 1, RING // 4 - 1)
            hidden(ET // RING - 1)

        @block.sync
        def _(sp):
            sp.dma_start(br[:, :], v["br_in"]).then_inc(s["wr_in"], 16)
            sp.wait_ge(s["wr_zero"], 1)
            for k in range(4):
                sp.dma_start(wr[RT * k:RT * k + RT, F * k:F * k + F], v["wr_in"]).then_inc(s["wr_in"], 16)

        @block.scalar
        def _(act):
            own = Chain(act, s["act_own"])
            with act.Fori(0, ET // RING) as i:
                own.enter(i, 2)
                act.wait_ge(s["fT_ps"], i + 1)
                nc.scalar.activation(fT[:, :], bank[4][0:4 * RT, :], ACT.Copy).then_inc(s["fT_ready"], 1)
                act.wait_ge(s["pre_ready"], i + 1)
                softplus_less_log2(nc, act, own, soft[:, :], soft[:, :], pre[:, :]).then_inc(s["soft_ready"], 1)
                own.leave(ET // RING)

        @block.gpsimd
        def _(gp):
            gp.wait_ge(prepared, 3)
            gather_quads(nc, gp, s, gathered, ET, rows, idx, from_idx, h_dram, sum_ready, 2)

        @block.tensor
        def _(pe):
            pe.sem_inc(sum_ready, RING // 2)
            flat = fr[:, :, :].rearrange("p (a b) r -> p a (b r)", b=4)
            pe.wait_ge(s["wr_in"], 80)
            with pe.Fori(0, ET // RING) as i:
                for q in range(RING // 2):
                    g = i * (RING // 2) + q
                    retired(pe, sum_added, g, ring=4, lead=4)
                    for k in range(2):
                        r = 2 * q + k
                        pe.wait_ge(S_ready, g * 2 + k + 1)
                        pe.wait_ge(gathered[r // 4], i * 64 + 64)
                        last = nc.tensor.matmul(bank[q % 4][:, :], S[r % 8][:, :], rows[r // 4][:, r % 4, :], start=(k == 0), stop=(k == 1))
                    last.then_inc(sum_ready, 1)
                    if q == 3:
                        pe.wait_ge(s["fr_ready"], i + 1)
                        for a in range(4):
                            last = nc.tensor.transpose(bank[4][0:4 * RT, a * P:(a + 1) * P], flat[:, a, :], ident[:, :])
                        last.then_inc(s["fT_ps"], 1)
                    if q == 5:
                        pe.wait_ge(s["fT_ready"], i + 1)
                        nc.tensor.matmul(bank[6][:, :], wr[:, :], fT[:, :], start=True, stop=True).then_inc(s["pre_ps"], 1)


def layer0_ffn(nc, v):
    x, ident, iota, stats, mean, rstd = (v[k] for k in ("x", "ident", "iota", "stats", "mean", "rstd"))
    neghalf, shift, bank = v["neghalf"], v["shift"], v["bank"]
    NE, H, GH = 8, 64, 16
    pairs = T // 2
    with ExitStack() as ctx:
        sb, sem = allocators(nc, ctx, "ffn0")
        w1, w3 = sb("w1", [P, K, D]), sb("w3", [P, K, D])
        wg1, wg2 = sb("wg1", [P, K, GH]), sb("wg2", [GH, NE])
        w2 = sb("w2", [P, K, P])
        b1, b2, g2, be2 = (sb(n, [P, D]) for n in ("b1", "b2", "g2", "be2"))
        gb1 = sb("gb1", [P, 2, K])
        bg1, bg2, b3 = sb("bg1", [GH, 1]), sb("bg2", [P, NE]), sb("b3", [NE, D])
        natural = sb("natural", [P, 2])
        two = range(2)
        xn, hb, hc = ([sb(f"{n}{u}", [P, D]) for u in two] for n in ("xn", "hb", "hc"))
        xT, aT, cT = ([sb(f"{n}{u}", [P, K, P]) for u in two] for n in ("xT", "aT", "cT"))
        gT = [sb(f"gT{u}", [GH, P]) for u in two]
        cwT = [sb(f"cwT{u}", [NE, P]) for u in two]
        lg, top = sb("lg", [P, 2, NE]), sb("top", [P, 2, NE])
        top_i, top_f = sb("top_i", [P, 2, NE], U32), sb("top_f", [P, 2, NE])
        share = sb("share", [P, 2, 4])
        cw, cw2 = sb("cw", [P, 2, NE]), sb("cw2", [P, 2, NE])
        st1, st2 = (sb(n, [P, 2, NE, 6]) for n in ("st1", "st2"))
        ms1, ms2 = (sb(n, [P, 2, 2, NE]) for n in ("ms1", "ms2"))

        names = ("weights_in", "w2_zero", "w2_in", "natural_made", "dve_own", "gate", "shift_ready", "pool_own", "var_ready", "rstd_ready",
                 "xn_ready", "xT_ps", "xT_ready", "h1_ps", "gate_ps", "gate_ready", "logit_ps", "logit_taken", "dist_ready", "exp_ready",
                 "cw_ready", "cwT_ps", "cwT_ready", "h1_taken", "var1_ready", "rstd1_ready", "a_ready", "aT_ps", "aT_ready",
                 "h2_ps", "h2_taken", "var2_ready", "rstd2_ready", "c_normed", "c_scaled", "c_active", "c_ready", "cT_ps", "cT_ready",
                 "o_ps", "x_done")
        s = {n: sem(n) for n in names}
        block = ctx.enter_context(nc.Block())

        @block.sync
        def _(sp):
            for dst, src in ((w1[:, :, :], v["w1_in"].rearrange("(k p) e -> p k e", p=P)),
                             (wg1[:, :, :], v["wg1_in"].rearrange("(k p) e -> p k e", p=P)),
                             (wg2[:, :], v["wg2_in"]), (w3[:, :, :], v["w3_in"].rearrange("(k p) e -> p k e", p=P)),
                             (b1[:, :], v["b1_in"].broadcast_to([P, D])), (b2[:, :], v["b2_in"].broadcast_to([P, D])),
                             (g2[:, :], v["g2_in"].broadcast_to([P, D])), (be2[:, :], v["be2_in"].broadcast_to([P, D])),
                             (gb1[:, :, :], v["gb1_in"]), (bg1[:, :], v["bg1_in"]), (bg2[:, :], v["bg2_in"].broadcast_to([P, NE])),
                             (b3[:, :], v["b3_in"])):
                sp.dma_start(dst, src).then_inc(s["weights_in"], 16)
            sp.wait_ge(s["w2_zero"], 1)
            for e in range(NE):
                q = H * (e % 2)
                sp.dma_start(w2[q:q + H, e // 2, q:q + H], v["w2_in"][e, :, :]).then_inc(s["w2_in"], 16)

        def weights(eng):
            eng.wait_ge(s["weights_in"], 12 * 16)

        def groups(ap):
            return ap.rearrange("p (e h) -> p e h", e=NE)

        @block.gpsimd
        def _(gp):
            G_ = nc.gpsimd
            G_.memset(w2[:, :, :], 0.0).then_inc(s["w2_zero"], 1)
            G_.memset(natural[:, :], float(np.e)).then_inc(s["natural_made"], 1)
            for n in ("c_scaled",):
                gp.sem_inc(s[n], LEAD)
            for n in ("rstd1_ready", "rstd2_ready", "exp_ready"):
                gp.sem_inc(s[n], 1)
            gp.wait_ge(s["var_ready"], 1)
            G_.tensor_tensor(rstd[:, :], rstd[:, :], neghalf[:, 0:T], ALU.pow).then_inc(s["rstd_ready"], 1)
            weights(gp)
            gp.wait_ge(s["natural_made"], 1)

            def gate_exp(i):
                made(gp, s["dist_ready"], i, lead=1)
                G_.tensor_tensor(share[:, :, 1], natural[:, :], share[:, :, 0], ALU.pow).then_inc(s["exp_ready"], 1)

            def rsqrt1(i):
                made(gp, s["var1_ready"], i, lead=1)
                G_.tensor_tensor(ms1[:, :, 1, :], ms1[:, :, 1, :], neghalf[:, 0:2 * NE].rearrange("p (a e) -> p a e", a=2), ALU.pow).then_inc(s["rstd1_ready"], 1)

            def rsqrt2(i):
                made(gp, s["var2_ready"], i, lead=1)
                G_.tensor_tensor(ms2[:, :, 1, :], ms2[:, :, 1, :], neghalf[:, 0:2 * NE].rearrange("p (a e) -> p a e", a=2), ALU.pow).then_inc(s["rstd2_ready"], 1)

            def affine2(own, i):
                for u in two:
                    made(gp, s["c_normed"], i * 2 + u)
                    own.step(G_.tensor_tensor(hc[u][:, :], hc[u][:, :], g2[:, :], ALU.mult))
                for u in two:
                    own.wait()
                    G_.tensor_tensor(hc[u][:, :], hc[u][:, :], be2[:, :], ALU.add).then_inc(s["c_scaled"], 1)

            own = Chain(gp, s["pool_own"])
            gate_exp(0)
            rsqrt1(0)
            with gp.Fori(0, pairs - 1) as i:
                own.enter(i, 2)
                rsqrt2(i)
                affine2(own, i)
                gate_exp(i + 1)
                rsqrt1(i + 1)
                own.leave(pairs - 1)
            rsqrt2(pairs - 1)
            affine2(own, pairs - 1)

        @block.vector
        def _(dve):
            V = nc.vector
            own = Chain(dve, s["dve_own"])
            for n in ("logit_taken", "h1_taken", "h2_taken", "a_ready", "c_normed", "c_ready", "x_done", "cT_ready"):
                dve.sem_inc(s[n], LEAD)
            for n in ("dist_ready", "cw_ready", "var1_ready", "var2_ready"):
                dve.sem_inc(s[n], 1)
            norm_stats(nc, own, x, stats, mean[:, :], rstd[:, :], s["var_ready"])
            dve.wait_ge(s["rstd_ready"], 1)
            V.scalar_tensor_tensor(shift[:, :], mean[:, :], -1.0, rstd[:, :], ALU.mult, ALU.mult).then_inc(s["shift_ready"], 1)
            weights(dve)

            def route(i):
                retired(dve, s["cwT_ps"], i * 2 + 1)
                for u in two:
                    made(dve, s["logit_ps"], i * 2 + u)
                    V.tensor_tensor(lg[:, u, :], bank[6 + u][:, P:P + NE], bg2[:, :], ALU.add).then_inc(s["logit_taken"], 1)
                made(dve, s["logit_taken"], i * 2 + 1)
                dve.sem_inc(s["gate"], 1)
                for u in two:
                    own.step(V.max(top[:, u, :], lg[:, u, :]))
                own.wait()
                dve.sem_inc(s["gate"], 1)
                for u in two:
                    own.step(V.max_index(top_i[:, u, :], top[:, u, :], lg[:, u, :]))
                V.tensor_tensor(share[:, :, 0], top[:, :, 1], top[:, :, 0], ALU.subtract).then_inc(s["dist_ready"], 1)
                own.wait()
                own.step(V.tensor_copy(top_f[:, :, :], top_i[:, :, :]))
                made(dve, s["exp_ready"], i, lead=1)
                own.link(V.tensor_scalar(share[:, :, 2], share[:, :, 1], 1.0, None, ALU.add))
                own.link(V.reciprocal(share[:, :, 2], share[:, :, 2]))
                own.link(V.tensor_tensor(share[:, :, 3], share[:, :, 2], share[:, :, 1], ALU.mult))
                for u in two:
                    own.step(V.tensor_scalar(cw[:, u, :], iota[:, 0:NE], top_f[:, u, 0:1], share[:, u, 2:3], ALU.is_equal, ALU.mult))
                    own.step(V.tensor_scalar(cw2[:, u, :], iota[:, 0:NE], top_f[:, u, 1:2], share[:, u, 3:4], ALU.is_equal, ALU.mult))
                own.wait()
                V.tensor_tensor(cw[:, :, :], cw[:, :, :], cw2[:, :, :], ALU.add).then_inc(s["cw_ready"], 1)

            def norm(i, h_ps, first, taken, bias, hx, read_by, st, ms, var, rst, out):
                for u in two:
                    retired(dve, read_by, i * 2 + u)
                    made(dve, h_ps, i * 2 + u)
                    V.tensor_tensor(hx[u][:, :], bank[first + u][:, :], bias[:, :], ALU.add).then_inc(taken, 1)
                for u in two:
                    made(dve, taken, i * 2 + u)
                    for e in range(NE):
                        own.step(V.bn_stats(st[:, u, e, :], hx[u][:, e * H:(e + 1) * H]))
                own.wait()
                me, ve, mo, vo = (st[:, :, :, c] for c in (1, 2, 4, 5))
                m, r = ms[:, :, 0, :], ms[:, :, 1, :]
                own.step(V.tensor_tensor(m, me, mo, ALU.add))
                own.step(V.tensor_tensor(r, me, mo, ALU.subtract))
                own.link(V.tensor_tensor(st[:, :, :, 0], ve, vo, ALU.add))
                own.step(V.tensor_scalar(m, m, 0.5, None, ALU.mult))
                own.link(V.scalar_tensor_tensor(r, r, 0.25, r, ALU.mult, ALU.mult))
                own.link(V.scalar_tensor_tensor(r, st[:, :, :, 0], 1.0 / H, r, ALU.mult, ALU.add))
                V.tensor_scalar(r, r, EPS, None, ALU.add).then_inc(var, 1)
                for u in two:
                    own.step(V.tensor_tensor(groups(hx[u][:, :]), groups(hx[u][:, :]), ms[:, u, 0, :].unsqueeze(2).broadcast_to([P, NE, H]), ALU.subtract))
                own.wait()
                made(dve, rst, i, lead=1)
                for u in two:
                    V.tensor_tensor(groups(hx[u][:, :]), groups(hx[u][:, :]), ms[:, u, 1, :].unsqueeze(2).broadcast_to([P, NE, H]), ALU.mult).then_inc(out, 1)

            def norm1(i):
                norm(i, s["h1_ps"], 2, s["h1_taken"], b1, hb, s["aT_ps"], st1, ms1, s["var1_ready"], s["rstd1_ready"], s["a_ready"])

            def norm2(i):
                norm(i, s["h2_ps"], 4, s["h2_taken"], b2, hc, s["cT_ps"], st2, ms2, s["var2_ready"], s["rstd2_ready"], s["c_normed"])

            def weigh(i):
                made(dve, s["cw_ready"], i, lead=1)
                for u in two:
                    made(dve, s["c_active"], i * 2 + u)
                    V.tensor_tensor(groups(hc[u][:, :]), groups(hc[u][:, :]), cw[:, u, :].unsqueeze(2).broadcast_to([P, NE, H]), ALU.mult).then_inc(s["c_ready"], 1)

            def add_out(i):
                for u in two:
                    xt = x[:, bass.ds(i * 2 + u, 1), :].rearrange("p a d -> p (a d)")
                    made(dve, s["o_ps"], i * 2 + u)
                    V.tensor_tensor(xt, xt, bank[4 + u][:, :], ALU.add).then_inc(s["x_done"], 1)

            route(0)
            norm1(0)
            with dve.Fori(0, pairs - 1) as i:
                own.enter(i, 60)
                norm2(i)
                weigh(i)
                route(i + 1)
                norm1(i + 1)
                add_out(i)
                own.leave(pairs - 1)
            norm2(pairs - 1)
            weigh(pairs - 1)
            add_out(pairs - 1)

        @block.scalar
        def _(act):
            A = nc.scalar
            for n in ("xn_ready", "xT_ready", "gate_ready", "cwT_ready", "aT_ready", "c_active"):
                act.sem_inc(s[n], LEAD)
            weights(act)
            act.wait_ge(s["shift_ready"], 1)

            def first(i):
                for u in two:
                    t = i * 2 + u
                    retired(act, s["xT_ps"], t)
                    A.activation(xn[u][:, :], x[:, bass.ds(t, 1), :].rearrange("p a d -> p (a d)"), ACT.Identity,
                                 bias=shift[:, bass.ds(t, 1)], scale=rstd[:, bass.ds(t, 1)]).then_inc(s["xn_ready"], 1)
                for u in two:
                    t = i * 2 + u
                    made(act, s["xT_ps"], t)
                    retired(act, s["gate_ps"], t)
                    A.activation(xT[u][:, :, :].rearrange("p k n -> p (k n)"), bank[u][:, :], ACT.Copy).then_inc(s["xT_ready"], 1)
                for u in two:
                    t = i * 2 + u
                    made(act, s["gate_ps"], t)
                    retired(act, s["logit_ps"], t)
                    A.activation(gT[u][:, :], bank[6 + u][0:GH, 0:P], ACT.Gelu, bias=bg1[:, 0:1]).then_inc(s["gate_ready"], 1)

            def second(i):
                for u in two:
                    t = i * 2 + u
                    made(act, s["cwT_ps"], t)
                    retired(act, s["o_ps"], t)
                    A.activation(cwT[u][:, :], bank[6 + u][0:NE, 256:256 + P], ACT.Copy).then_inc(s["cwT_ready"], 1)
                for u in two:
                    t = i * 2 + u
                    made(act, s["aT_ps"], t)
                    retired(act, s["h2_ps"], t)
                    for c in range(K):
                        last = A.activation(aT[u][:, c, :], bank[u][:, c * P:(c + 1) * P], ACT.Gelu, bias=gb1[:, 1, c:c + 1], scale=gb1[:, 0, c:c + 1])
                    last.then_inc(s["aT_ready"], 1)

            def third(i):
                for u in two:
                    t = i * 2 + u
                    made(act, s["c_scaled"], t)
                    A.activation(hc[u][:, :], hc[u][:, :], ACT.Gelu).then_inc(s["c_active"], 1)
                for u in two:
                    t = i * 2 + u
                    made(act, s["cT_ps"], t)
                    retired(act, s["o_ps"], t)
                    A.activation(cT[u][:, :, :].rearrange("p k n -> p (k n)"), bank[u][:, :], ACT.Copy).then_inc(s["cT_ready"], 1)

            first(0)
            with act.Fori(0, pairs - 1) as i:
                second(i)
                first(i + 1)
                third(i)
            second(pairs - 1)
            third(pairs - 1)

        @block.tensor
        def _(pe):
            M = nc.tensor
            for n in ("xT_ps", "h1_ps", "gate_ps", "logit_ps", "cwT_ps", "aT_ps", "h2_ps", "cT_ps", "o_ps"):
                pe.sem_inc(s[n], LEAD)
            weights(pe)
            pe.wait_ge(s["w2_in"], NE * 16)

            def turn(i, ready, src, done):
                for u in two:
                    made(pe, ready, i * 2 + u)
                    for k in range(K):
                        last = M.transpose(bank[u][:, k * P:(k + 1) * P], src[u][:, k * P:(k + 1) * P], ident[:, :])
                    last.then_inc(done, 1)

            def first(i):
                turn(i, s["xn_ready"], xn, s["xT_ps"])
                for u in two:
                    t = i * 2 + u
                    made(pe, s["xT_ready"], t)
                    retired(pe, s["h1_taken"], t)
                    for k in range(K):
                        last = M.matmul(bank[2 + u][:, :], xT[u][:, k, :], w1[:, k, :], start=(k == 0), stop=(k == K - 1))
                    last.then_inc(s["h1_ps"], 1)
                    retired(pe, s["logit_taken"], t)
                    retired(pe, s["cwT_ready"], t)
                    for k in range(K):
                        last = M.matmul(bank[6 + u][0:GH, 0:P], wg1[:, k, :], xT[u][:, k, :], start=(k == 0), stop=(k == K - 1))
                    last.then_inc(s["gate_ps"], 1)
                for u in two:
                    made(pe, s["gate_ready"], i * 2 + u)
                    M.matmul(bank[6 + u][:, P:P + NE], gT[u][:, :], wg2[:, :], start=True, stop=True).then_inc(s["logit_ps"], 1)

            def second(i):
                made(pe, s["cw_ready"], i, lead=1)
                for u in two:
                    M.transpose(bank[6 + u][0:NE, 256:256 + P], cw[:, u, :], ident[:, :]).then_inc(s["cwT_ps"], 1)
                turn(i, s["a_ready"], hb, s["aT_ps"])
                for u in two:
                    t = i * 2 + u
                    made(pe, s["aT_ready"], t)
                    retired(pe, s["x_done"], t)
                    for c in range(K):
                        last = M.matmul(bank[4 + u][:, c * P:(c + 1) * P], aT[u][:, c, :], w2[:, c, :], start=True, stop=True)
                    last.then_inc(s["h2_ps"], 1)

            def third(i):
                turn(i, s["c_ready"], hc, s["cT_ps"])
                for u in two:
                    t = i * 2 + u
                    made(pe, s["cwT_ready"], t)
                    M.matmul(bank[4 + u][:, :], cwT[u][:, :], b3[:, :], start=True, stop=False)
                    made(pe, s["cT_ready"], t)
                    for c in range(K):
                        last = M.matmul(bank[4 + u][:, :], cT[u][:, c, :], w3[:, c, :], start=False, stop=(c == K - 1))
                    last.then_inc(s["o_ps"], 1)

            first(0)
            with pe.Fori(0, pairs - 1) as i:
                second(i)
                first(i + 1)
                third(i)
            second(pairs - 1)
            third(pairs - 1)


F = 32
AT, RT = 4, 20
LOG2 = float(np.log(2.0))


def layer1_features(nc, v):
    x, ident, stats, mean, rstd = (v[k] for k in ("x", "ident", "stats", "mean", "rstd"))
    neghalf, shift, bank, feat_dram = v["neghalf"], v["shift"], v["bank"], v["feat_dram"]
    two = range(2)
    with ExitStack() as ctx:
        sb, sem = allocators(nc, ctx, "feat1")
        w_in = sb("w_in", [P, 2, F])
        xn = [sb(f"xn{u}", [P, D]) for u in two]
        xT = [sb(f"xT{u}", [P, K, P]) for u in two]
        feat = sb("feat", [P, T, P])
        names = ("weights_in", "dve_own", "var_ready", "rstd_ready", "shift_ready", "xn_ready", "xT_ps", "xT_ready", "feat_ps",
                 "feat_ready", "feat_stored")
        s = {n: sem(n) for n in names}
        block = ctx.enter_context(nc.Block())

        @block.sync
        def _(sp):
            sp.dma_start(w_in[:, :, :], v["w_in_in"]).then_inc(s["weights_in"], 16)
            with sp.Fori(0, T) as t:
                made(sp, s["feat_ready"], t)
                sp.dma_start(feat_dram[bass.ds(t * P, P), :], feat[:, bass.ds(t, 1), :].rearrange("p a d -> p (a d)")).then_inc(s["feat_stored"], 16)
            sp.wait_ge(s["feat_stored"], 16 * T)

        @block.gpsimd
        def _(gp):
            gp.wait_ge(s["var_ready"], 1)
            nc.gpsimd.tensor_tensor(rstd[:, :], rstd[:, :], neghalf[:, 0:T], ALU.pow).then_inc(s["rstd_ready"], 1)

        @block.vector
        def _(dve):
            V = nc.vector
            own = Chain(dve, s["dve_own"])
            dve.sem_inc(s["feat_ready"], LEAD)
            norm_stats(nc, own, x, stats, mean[:, :], rstd[:, :], s["var_ready"])
            dve.wait_ge(s["weights_in"], 16)
            dve.wait_ge(s["rstd_ready"], 1)
            V.scalar_tensor_tensor(shift[:, :], mean[:, :], -1.0, rstd[:, :], ALU.mult, ALU.mult).then_inc(s["shift_ready"], 1)
            with dve.Fori(0, T // 2) as i:
                for u in two:
                    t = i * 2 + u
                    made(dve, s["feat_ps"], t)
                    V.tensor_scalar(feat[:, bass.ds(t, 1), :].rearrange("p a d -> p (a d)"), bank[2 + u][:, 0:P],
                                    float(P) ** -0.5, None, ALU.mult).then_inc(s["feat_ready"], 1)

        @block.scalar
        def _(act):
            A = nc.scalar
            for n in ("xn_ready", "xT_ready"):
                act.sem_inc(s[n], LEAD)
            act.wait_ge(s["shift_ready"], 1)
            with act.Fori(0, T // 2) as i:
                for u in two:
                    t = i * 2 + u
                    retired(act, s["xT_ps"], t)
                    A.activation(xn[u][:, :], x[:, bass.ds(t, 1), :].rearrange("p a d -> p (a d)"), ACT.Identity,
                                 bias=shift[:, bass.ds(t, 1)], scale=rstd[:, bass.ds(t, 1)]).then_inc(s["xn_ready"], 1)
                for u in two:
                    t = i * 2 + u
                    made(act, s["xT_ps"], t)
                    retired(act, s["feat_ps"], t)
                    A.activation(xT[u][:, :, :].rearrange("p k n -> p (k n)"), bank[u][:, :], ACT.Copy).then_inc(s["xT_ready"], 1)

        @block.tensor
        def _(pe):
            M = nc.tensor
            for n in ("xT_ps", "feat_ps"):
                pe.sem_inc(s[n], LEAD)
            pe.wait_ge(s["weights_in"], 16)
            with pe.Fori(0, T // 2) as i:
                for u in two:
                    t = i * 2 + u
                    made(pe, s["xn_ready"], t)
                    for k in range(K):
                        src = xn[u][:, 0:P] if k == 0 else xn[u][:, P + k - 1:D:3]
                        last = M.transpose(bank[u][:, k * P:(k + 1) * P], src, ident[:, :])
                    last.then_inc(s["xT_ps"], 1)
                for u in two:
                    t = i * 2 + u
                    made(pe, s["xT_ready"], t)
                    retired(pe, s["feat_ready"], t)
                    for k in range(K):
                        last = M.matmul(bank[2 + u][:, k * F:(k + 1) * F], xT[u][:, k, :], w_in[:, min(k, 1), :], start=True, stop=True)
                    last.then_inc(s["feat_ps"], 1)


def layer1_edges(nc, v):
    iota, edges, from_idx, to_loc, hT, agg = (v[k] for k in ("iota", "edges", "from_idx", "to_loc", "hT", "agg"))
    group_tile_i, bank, feat_dram = v["group_tile_i"], v["bank"], v["feat_dram"]
    QUADS = 4
    EB = 4 * QUADS
    STEPS = ET // EB
    two = range(2)
    with ExitStack() as ctx:
        sb, sem = allocators(nc, ctx, "edges1")
        w2 = sb("w2", [P, 4 * P])
        PARTS = (0, 32, 64)
        b2, b2_rest = sb("b2", [96, 4 * P]), sb("b2_rest", [96, 4 * P])
        b2_part = [sb(f"b2_part{k}", [96, 4 * P], BF16) for k in range(3)]
        b2_parts = sb("b2_parts", [96, 4 * P], BF16)
        ones = sb("ones", [96, P], BF16)
        hq = [sb(f"hq{u}", [P, P]) for u in two]
        rows = [sb(f"rows{q}", [P, 4, P]) for q in range(QUADS)]
        idx = [sb(f"idx{h}", [P, 16], I32) for h in range(2)]
        attr = [sb(f"attr{u}", [P, 4, 8, F]) for u in two]
        vy = [sb(f"vy{u}", [P, 4, 3, F]) for u in two]
        msg = [sb(f"msg{u}", [P, 4, 8, F]) for u in two]
        hot = [[sb(f"hot{u}{k}", [P, P]) for k in range(4)] for u in two]
        agg_flat = agg[:, :, :].rearrange("p t d -> p (t d)")
        names = ("weights_in", "consts_made", "dve_own", "b2_split", "w2_in", "idx_ready", "gate", "hq_ready", "filter_ps", "hot_ready",
                 "own_attr", "act_attr", "sum_ready", "agg_zero", "sum_added", "msg_ready")
        s = {n: sem(n) for n in names}
        gathered = [sem(f"gathered{q}") for q in range(QUADS)]
        block = ctx.enter_context(nc.Block())

        @block.sync
        def _(sp):
            sp.dma_start(b2[:, :], v["bf_in"].broadcast_to([96, 4 * P])).then_inc(s["weights_in"], 16)
            sp.wait_ge(s["consts_made"], 3)
            for k in range(4):
                sp.dma_start(w2[F * k:F * k + F, P * k:P * k + P], v["wf_in"]).then_inc(s["w2_in"], 16)

        @block.gpsimd
        def _(gp):
            nc.gpsimd.memset(ones[:, :], 1.0).then_inc(s["consts_made"], 1)
            nc.gpsimd.memset(b2_parts[:, :], 0.0).then_inc(s["consts_made"], 1)
            nc.gpsimd.memset(w2[:, :], 0.0).then_inc(s["consts_made"], 1)
            gather_quads(nc, gp, s, gathered, ET, rows, idx, from_idx, feat_dram, s["msg_ready"], 1)

        @block.vector
        def _(dve):
            V = nc.vector
            own = Chain(dve, s["dve_own"])
            dve.sem_inc(s["msg_ready"], QUADS)
            dve.sem_inc(s["sum_added"], 4)
            own.step(V.memset(agg[:, :, :], 0.0))
            dve.wait_ge(s["weights_in"], 16)
            own.step(V.tensor_copy(b2_part[0][:, :], b2[:, :]))
            V.tensor_tensor(edges[:, :, R_Y:R_Y + AT], edges[:, :, R_Y:R_Y + AT],
                            edges[:, :, R_W:R_W + 1].broadcast_to([P, ET, AT]), ALU.mult).then_inc(s["agg_zero"], 1)
            own.wait()
            dve.wait_ge(s["agg_zero"], 1)
            own.link(V.tensor_tensor(b2_rest[:, :], b2[:, :], b2_part[0][:, :], ALU.subtract))
            own.link(V.tensor_copy(b2_part[1][:, :], b2_rest[:, :]))
            own.link(V.tensor_tensor(b2_part[2][:, :], b2_rest[:, :], b2_part[1][:, :], ALU.subtract))
            dve.wait_ge(s["consts_made"], 3)
            for k, p in enumerate(PARTS):
                V.tensor_copy(b2_parts[p:p + 1, :], b2_part[k][p:p + 1, :]).then_inc(s["b2_split"], 1)

            def add(i, q):
                for g2 in two:
                    g = i * (EB // 2) + q * 2 + g2
                    col = dve.value_load(group_tile_i[0:1, bass.ds(g, 1)], min_val=0, max_val=T - 1) * (8 * F)
                    made(dve, s["sum_ready"], g, lead=4)
                    retired(dve, s["sum_added"], g, ring=1, lead=4)
                    V.tensor_tensor(agg_flat[:, bass.ds(col, 8 * F)], agg_flat[:, bass.ds(col, 8 * F)],
                                    bank[2 * q % 4 + g2][:, 0:8 * F], ALU.add).then_inc(s["sum_added"], 1)

            def messages(i, q):
                n, u = i * QUADS + q, q % 2
                r, a, m = rows[q], attr[u], msg[u]
                y = edges[:, bass.ds(n * 4, 4), R_Y + 1:R_Y + 4]
                retired(dve, s["sum_ready"], n * 2 + 1, ring=4, lead=4)
                for k in range(4):
                    last = V.tensor_scalar(hot[u][k][:, :], iota[:, :], to_loc[:, bass.ds(n * 4 + k, 1)], None, ALU.is_equal)
                last.then_inc(s["hot_ready"], 1)
                dve.wait_ge(gathered[q], i * 64 + 64)
                V.tensor_tensor(vy[u][:, :, :, :], r[:, :, F:P].rearrange("p e (c f) -> p e c f", f=F),
                                y.unsqueeze(3).broadcast_to([P, 4, 3, F]), ALU.mult).then_inc(s["own_attr"], 1)
                V.tensor_tensor(a[:, :, 2:8:2, :], r[:, :, 0:F].unsqueeze(2).broadcast_to([P, 4, 3, F]),
                                y.unsqueeze(3).broadcast_to([P, 4, 3, F]), ALU.mult).then_inc(s["own_attr"], 1)
                dve.wait_ge(s["own_attr"], n * 3 + 2)
                V.tensor_reduce(a[:, :, 0, :], vy[u][:, :, :, :].rearrange("p e c f -> p e f c"), AX.X, ALU.add).then_inc(s["own_attr"], 1)
                w = bank[4 + u][:, :].rearrange("p (e x) -> p e x", e=4)
                made(dve, s["filter_ps"], n)
                dve.wait_ge(s["act_attr"], n + 1)
                V.tensor_tensor(m[:, :, 2:8, :].rearrange("p e (c j) f -> p e c (j f)", c=3), a[:, :, 2:8, :].rearrange("p e (c j) f -> p e c (j f)", c=3),
                                w[:, :, 2 * F:4 * F].unsqueeze(2).broadcast_to([P, 4, 3, 2 * F]), ALU.mult)
                dve.wait_ge(s["own_attr"], n * 3 + 3)
                V.tensor_tensor(m[:, :, 0:2, :].rearrange("p e b f -> p e (b f)"), a[:, :, 0:2, :].rearrange("p e b f -> p e (b f)"),
                                w[:, :, 0:2 * F], ALU.mult).then_inc(s["msg_ready"], 1)

            def quads(i, first):
                for q in range(QUADS):
                    messages(i, q)
                    if q >= 1:
                        add(i, q - 1)
                    elif not first:
                        add(i - 1, QUADS - 1)

            quads(0, True)
            with dve.Fori(1, STEPS) as i:
                quads(i, False)
            add(STEPS - 1, QUADS - 1)

        @block.scalar
        def _(act):
            A = nc.scalar
            act.sem_inc(s["hq_ready"], LEAD)
            act.wait_ge(s["agg_zero"], 1)
            for u in two:
                A.activation(hq[u][:, :], hT[:, u * P:u * P + P], ACT.Copy).then_inc(s["hq_ready"], 1)

            def quads(i, last):
                for q in range(QUADS):
                    n, u = i * QUADS + q, q % 2
                    act.wait_ge(gathered[q], i * 64 + 64)
                    retired(act, s["msg_ready"], n, ring=2, lead=QUADS)
                    for k in range(4):
                        done = A.activation(attr[u][:, k, 1:8:2, :], rows[q][:, k, :].rearrange("p (b f) -> p b f", f=F), ACT.Copy,
                                            scale=edges[:, bass.ds(n * 4 + k, 1), R_Y])
                    done.then_inc(s["act_attr"], 1)
                    if not (last and q >= QUADS - 2):
                        made(act, s["filter_ps"], n)
                        A.activation(hq[u][:, :], hT[:, bass.ds((n + 2) * P, P)], ACT.Copy).then_inc(s["hq_ready"], 1)

            with act.Fori(0, STEPS - 1) as i:
                quads(i, False)
            quads(STEPS - 1, True)

        @block.tensor
        def _(pe):
            M = nc.tensor
            pe.sem_inc(s["filter_ps"], LEAD)
            pe.sem_inc(s["sum_ready"], 4)
            pe.wait_ge(s["b2_split"], 3)
            pe.wait_ge(s["w2_in"], 64)

            def filter_(n, u):
                made(pe, s["hq_ready"], n)
                retired(pe, s["msg_ready"], n, ring=2, lead=QUADS)
                M.matmul(bank[4 + u][:, :], ones[:, :], b2_parts[:, :], start=True, stop=False)
                M.matmul(bank[4 + u][:, :], hq[u][:, :], w2[:, :], start=False, stop=True).then_inc(s["filter_ps"], 1)

            def quads(i, last):
                for q in range(QUADS):
                    n, u = i * QUADS + q, q % 2
                    if not (last and q == QUADS - 1):
                        filter_(n + 1, 1 - u)
                    made(pe, s["hot_ready"], n, lead=0)
                    made(pe, s["msg_ready"], n, lead=QUADS)
                    for g2 in two:
                        retired(pe, s["sum_added"], n * 2 + g2, ring=4, lead=4)
                        for k in (2 * g2, 2 * g2 + 1):
                            done = M.matmul(bank[2 * q % 4 + g2][:, 0:8 * F], hot[u][k][:, :], msg[u][:, k, :, :].rearrange("p b f -> p (b f)"),
                                            start=(k % 2 == 0), stop=(k % 2 == 1))
                        done.then_inc(s["sum_ready"], 1)

            filter_(0, 0)
            with pe.Fori(0, STEPS - 1) as i:
                quads(i, False)
            quads(STEPS - 1, True)


def layer1_nodes(nc, v):
    x, ident, agg, bank = (v[k] for k in ("x", "ident", "agg", "bank"))
    two = range(2)
    with ExitStack() as ctx:
        sb, sem = allocators(nc, ctx, "nodes1")
        w1s = sb("w1s", [2 * F, P])
        w1v = sb("w1v", [P, P])
        w2 = sb("w2", [P, 2, P])
        a = [sb(f"a{u}", [P, 2, P]) for u in two]
        aT = [sb(f"aT{u}", [P, 2, P]) for u in two]
        oT = [sb(f"oT{u}", [P, 4, P]) for u in two]
        relu, soft = ([sb(f"{n}{u}", [P, P]) for u in two] for n in ("relu", "soft"))
        names = ("weights_in", "act_own", "gate", "w1_ready", "a_ready", "aT_ps", "aT_ready", "o1_ps", "oT_copied", "soft_ready", "relu_ready", "o1_taken",
                 "os_ready", "o2_ps", "x_s", "x_done")
        s = {n: sem(n) for n in names}
        block = ctx.enter_context(nc.Block())
        half = float(2 * F) ** -0.5

        @block.sync
        def _(sp):
            for dst, src in ((w1s[0:F, :], v["w1s_in"][F:2 * F, :]), (w1s[F:2 * F, :], v["w1s_in"][0:F, :]),
                             (w1v[0:2 * F, :], v["w1v_in"]), (w1v[2 * F:P, :], v["w1v_in"]),
                             (w2[:, 0, :], v["w2s_in"]), (w2[:, 1, :], v["w2v_in"])):
                sp.dma_start(dst, src).then_inc(s["weights_in"], 16)

        @block.gpsimd
        def _(gp):
            gp.sem_inc(s["a_ready"], LEAD)
            with gp.Fori(0, T // 2) as i:
                for u in two:
                    t = i * 2 + u
                    retired(gp, s["aT_ps"], t)
                    gp.sem_inc(s["gate"], 1)
                    nc.gpsimd.tensor_copy(a[u][:, :, :].rearrange("p a b -> p (a b)"), agg[:, bass.ds(t, 1), :].rearrange("p a d -> p (a d)")).then_inc(s["a_ready"], 1)

        @block.vector
        def _(dve):
            V = nc.vector
            for n in ("relu_ready", "os_ready", "x_done", "x_s"):
                dve.sem_inc(s[n], LEAD)
            dve.wait_ge(s["weights_in"], 6 * 16)
            V.tensor_scalar(w1s[0:F, :], w1s[0:F, :], 3.0 ** -0.5, None, ALU.mult).then_inc(s["w1_ready"], 1)
            with dve.Fori(0, T // 2) as i:
                for u in two:
                    t = i * 2 + u
                    made(dve, s["oT_copied"], t)
                    made(dve, s["soft_ready"], t)
                    V.tensor_scalar(relu[u][:, :], bank[2 + u][:, 0:P], half, 0.0, ALU.mult, ALU.max).then_inc(s["relu_ready"], 1)
                for u in two:
                    t = i * 2 + u
                    made(dve, s["relu_ready"], t)
                    retired(dve, s["o2_ps"], t)
                    V.tensor_tensor(oT[u][:, 0, :], relu[u][:, :], soft[u][:, :], ALU.add).then_inc(s["os_ready"], 1)
                for u in two:
                    t = i * 2 + u
                    made(dve, s["o2_ps"], t)
                    xt = x[:, bass.ds(t, 1), :].rearrange("p a d -> p (a d)")
                    V.scalar_tensor_tensor(xt[:, 0:P], bank[4 + u][:, 0:P], float(P) ** -0.5, xt[:, 0:P], ALU.mult, ALU.add).then_inc(s["x_s"], 1)
                    xv = xt[:, P:D].rearrange("p (d c) -> p c d", c=3)
                    V.scalar_tensor_tensor(xv, bank[4 + u][:, P:D].rearrange("p (c d) -> p c d", c=3), float(P) ** -0.5, xv,
                                           ALU.mult, ALU.add).then_inc(s["x_done"], 1)

        @block.scalar
        def _(act):
            A = nc.scalar
            own = Chain(act, s["act_own"])
            for n in ("aT_ready", "oT_copied", "soft_ready"):
                act.sem_inc(s[n], LEAD)
            with act.Fori(0, T // 2) as i:
                own.enter(i, 4)
                for u in two:
                    t = i * 2 + u
                    made(act, s["aT_ps"], t)
                    retired(act, s["o1_ps"], t)
                    A.activation(aT[u][:, :, :].rearrange("p a b -> p (a b)"), bank[u][:, 0:2 * P], ACT.Copy).then_inc(s["aT_ready"], 1)
                for u in two:
                    t = i * 2 + u
                    made(act, s["o1_ps"], t)
                    retired(act, s["o2_ps"], t)
                    retired(act, s["os_ready"], t)
                    own.link(A.activation(soft[u][:, :], bank[2 + u][:, 0:P], ACT.Abs, scale=half))
                    A.activation(oT[u][:, 2, :], bank[2 + u][:, P:2 * P], ACT.Copy, scale=half)
                    A.activation(oT[u][:, 1:4:2, :], bank[6 + u][:, 0:2 * P].rearrange("p (a b) -> p a b", a=2), ACT.Copy, scale=half).then_inc(s["oT_copied"], 1)
                    own.link(A.activation(soft[u][:, :], soft[u][:, :], ACT.Exp, scale=-1.0))
                    A.activation(soft[u][:, :], soft[u][:, :], ACT.Ln, scale=0.5, bias=0.5).then_inc(s["soft_ready"], 1)
                own.leave(T // 2)

        @block.tensor
        def _(pe):
            M = nc.tensor
            for n in ("aT_ps", "o1_ps", "o2_ps"):
                pe.sem_inc(s[n], LEAD)
            pe.wait_ge(s["weights_in"], 6 * 16)
            pe.wait_ge(s["w1_ready"], 1)
            with pe.Fori(0, T // 2) as i:
                for u in two:
                    t = i * 2 + u
                    made(pe, s["a_ready"], t)
                    for k in range(2):
                        last = M.transpose(bank[u][:, k * P:(k + 1) * P], a[u][:, k, :], ident[:, :])
                    last.then_inc(s["aT_ps"], 1)
                for u in two:
                    t = i * 2 + u
                    made(pe, s["aT_ready"], t)
                    retired(pe, s["relu_ready"], t)
                    for j in range(4):
                        q = 2 * F * (j % 2)
                        lhs = w1s[0:2 * F, :] if j == 0 else w1v[q:q + 2 * F, :]
                        last = M.matmul(bank[2 + u + 4 * (j % 2)][:, j // 2 * P:(j // 2 + 1) * P], lhs, aT[u][q:q + 2 * F, j // 2, :],
                                        start=True, stop=True)
                    last.then_inc(s["o1_ps"], 1)
                for u in two:
                    t = i * 2 + u
                    made(pe, s["oT_copied"], t)
                    made(pe, s["os_ready"], t)
                    retired(pe, s["x_done"], t)
                    for j in range(4):
                        last = M.matmul(bank[4 + u][:, j * P:(j + 1) * P], oT[u][:, j, :], w2[:, min(j, 1), :], start=True, stop=True)
                    last.then_inc(s["o2_ps"], 1)


NX, HX, NH = 64, 64, 4
CAP = 4 * N * 2 // NX
NB = 2 * N // P + NX


def layer1_route(nc, v):
    x, ident, iota, stats, mean, rstd = (v[k] for k in ("x", "ident", "iota", "stats", "mean", "rstd"))
    neghalf, shift, bank = v["neghalf"], v["shift"], v["bank"]
    tok_idx, y_idx, gain, block_expert = (v[k] for k in ("tok_idx", "y_idx", "gain", "block_expert"))
    two = range(2)
    with ExitStack() as ctx:
        sb, sem = allocators(nc, ctx, "route1")
        hp = sb("hp", [P, K, NH * NX])
        xn = [sb(f"xn{u}", [P, D]) for u in two]
        xT = [sb(f"xT{u}", [P, K, P]) for u in two]
        xn_all = sb("xn_all", [P, T, D])
        top = [sb(f"top{u}", [P, NH, 8]) for u in two]
        top_i = [sb(f"top_i{u}", [P, NH, 8], U32) for u in two]
        score, expert = sb("score", [P, T, NH]), sb("expert", [P, T, NH])
        before = sb("before", [P, NH, NH])
        beats, ties = sb("beats", [P, T, NH, NH]), sb("ties", [P, T, NH, NH])
        rank = sb("rank", [P, T, NH])
        pick = sb("pick", [P, 2, T, NH])
        sel = sb("sel", [P, 2, T])
        hot = sb("hot", [P, 2, T, NX])
        both = sb("both", [P, T * NX])
        ahead = sb("ahead", [P, T, NX])
        total = sb("total", [P, T, NX])
        run = sb("run", [P, T + 1, NX])
        place = sb("place", [P, 2, T])
        first = sb("first", [P, 2, T])
        prod = sb("prod", [P, 2, T, NX])
        keep = sb("keep", [P, 2, T])
        small = sb("small", [P, 4, NX])
        nb, bend, bstart, one = (small[:, k, :] for k in range(4))
        nb_i = sb("nb_i", [P, NX], I32)
        slot_i, lo_i, hi_i, row_i = (sb(n, [P, 2, T], I32) for n in ("slot_i", "lo_i", "hi_i", "row_i"))
        row, trash = sb("row", [P, 2, T]), sb("trash", [P, 2, T])
        token = sb("token", [P, T], I32)
        iota_blk = sb("iota_blk", [P, NB])
        bmask = sb("bmask", [P, NB, NX])
        bexp = sb("bexp", [P, NB])
        lower, ones = sb("lower", [P, P]), sb("ones", [P, P])
        empty = sb("empty", [P, NB], I32)
        names = ("weights_in", "consts_made", "pool_own", "dve_own", "var_ready", "rstd_ready", "shift_ready", "xn_ready", "xn_kept", "xn_stored",
                 "xT_ps", "xT_ready", "logit_ps", "taken", "gate", "both_ready", "sums_ready", "emptied", "row_ready", "placed", "tok_in")
        s = {n: sem(n) for n in names}
        block = ctx.enter_context(nc.Block())

        @block.sync
        def _(sp):
            sp.dma_start(hp[:, :, :], v["hp_in"].rearrange("(k p) e -> p k e", p=P)).then_inc(s["weights_in"], 16)
            with sp.Fori(0, T) as t:
                made(sp, s["xn_kept"], t)
                sp.dma_start(v["xn_dram"][bass.ds(t * P, P), :], xn_all[:, bass.ds(t, 1), :].rearrange("p a d -> p (a d)")).then_inc(s["xn_stored"], 16)
            sp.wait_ge(s["placed"], 16 * 2 * T)
            sp.dma_start(tok_idx[:, 0:NB], v["tok_dram"][0:P * NB, :].rearrange("(p b) a -> p (b a)", p=P)).then_inc(s["tok_in"], 16)
            sp.wait_ge(s["tok_in"], 16)
            sp.wait_ge(s["xn_stored"], 16 * T)

        @block.gpsimd
        def _(gp):
            G_ = nc.gpsimd
            own = Chain(gp, s["pool_own"])
            own.step(G_.memset(ones[:, :], 1.0))
            own.step(G_.memset(before[:, :, :], 1.0))
            own.step(G_.memset(empty[:, :], 0))
            G_.memset(tok_idx[:, :], 0).then_inc(s["consts_made"], 1)
            G_.iota(token[:, :], [[P, T]], base=0, channel_multiplier=1).then_inc(s["consts_made"], 1)
            G_.iota(iota_blk[:, :], [[1, NB]], base=0, channel_multiplier=0, allow_small_or_imprecise_dtypes=True).then_inc(s["consts_made"], 1)
            G_.iota(trash[:, :, :], [[N, 2], [P, T]], base=P * NB, channel_multiplier=1, allow_small_or_imprecise_dtypes=True).then_inc(s["consts_made"], 1)
            own.wait()
            G_.affine_select(out=lower[:, :], in_=ones[:, :], compare_op=ALU.is_gt, fill=0.0, base=0,
                             pattern=[[1, P]], channel_multiplier=-1).then_inc(s["consts_made"], 1)
            G_.affine_select(out=before[:, :, :], in_=before[:, :, :], compare_op=ALU.is_gt, fill=0.0, base=0,
                             pattern=[[1, NH], [-1, NH]], channel_multiplier=0).then_inc(s["consts_made"], 1)
            gp.dma_start(v["tok_dram"][0:P * NB, :].rearrange("(p b) a -> p (b a)", p=P), empty[:, :]).then_inc(s["emptied"], 16)
            gp.wait_ge(s["var_ready"], 1)
            G_.tensor_tensor(rstd[:, :], rstd[:, :], neghalf[:, 0:T], ALU.pow).then_inc(s["rstd_ready"], 1)
            gp.wait_ge(s["emptied"], 16)
            gp.wait_ge(s["row_ready"], 1)
            for k in range(2):
                for t in range(T):
                    gp.indirect_dma_start(out=v["tok_dram"], out_offset=bass.IndirectOffsetOnAxis(ap=row_i[:, k, t:t + 1], axis=0),
                                          in_=token[:, t:t + 1], in_offset=None).then_inc(s["placed"], 16)

        @block.vector
        def _(dve):
            V = nc.vector
            own = Chain(dve, s["dve_own"])
            dve.sem_inc(s["xn_kept"], LEAD)
            dve.sem_inc(s["taken"], LEAD)
            norm_stats(nc, own, x, stats, mean[:, :], rstd[:, :], s["var_ready"])
            dve.wait_ge(s["rstd_ready"], 1)
            V.scalar_tensor_tensor(shift[:, :], mean[:, :], -1.0, rstd[:, :], ALU.mult, ALU.mult).then_inc(s["shift_ready"], 1)
            with dve.Fori(0, T // 2) as i:
                own.enter(i, 16)
                for u in two:
                    t = i * 2 + u
                    V.tensor_scalar(xn_all[:, bass.ds(t, 1), :].rearrange("p a d -> p (a d)"), x[:, bass.ds(t, 1), :].rearrange("p a d -> p (a d)"),
                                    mean[:, bass.ds(t, 1)], rstd[:, bass.ds(t, 1)], ALU.subtract, ALU.mult).then_inc(s["xn_kept"], 1)
                for u in two:
                    t = i * 2 + u
                    made(dve, s["logit_ps"], t)
                    dve.sem_inc(s["gate"], 1)
                    for h in range(NH):
                        own.step(V.max(top[u][:, h, :], bank[2 + u][:, h * NX:(h + 1) * NX]))
                    own.wait()
                    dve.sem_inc(s["gate"], 1)
                    for h in range(NH):
                        own.step(V.max_index(top_i[u][:, h, :], top[u][:, h, :], bank[2 + u][:, h * NX:(h + 1) * NX]))
                    own.wait()
                    V.tensor_copy(score[:, bass.ds(t, 1), :].rearrange("p a h -> p (a h)"), top[u][:, :, 0])
                    V.tensor_copy(expert[:, bass.ds(t, 1), :].rearrange("p a h -> p (a h)"), top_i[u][:, :, 0]).then_inc(s["taken"], 1)
                own.leave(T // 2)
            dve.wait_ge(s["taken"], T + LEAD)
            dve.wait_ge(s["consts_made"], 6)
            mine = score[:, :, :].unsqueeze(3).broadcast_to([P, T, NH, NH])
            other = score[:, :, :].unsqueeze(2).broadcast_to([P, T, NH, NH])
            own.step(V.tensor_tensor(beats[:, :, :, :], other, mine, ALU.is_gt))
            own.link(V.tensor_tensor(ties[:, :, :, :], other, mine, ALU.is_equal))
            own.link(V.tensor_tensor(ties[:, :, :, :], ties[:, :, :, :], before[:, :, :].unsqueeze(1).broadcast_to([P, T, NH, NH]), ALU.mult))
            own.link(V.tensor_tensor(beats[:, :, :, :], beats[:, :, :, :], ties[:, :, :, :], ALU.add))
            own.link(V.tensor_reduce(rank[:, :, :], beats[:, :, :, :], AX.X, ALU.add))
            for k in range(2):
                own.step(V.scalar_tensor_tensor(pick[:, k, :, :], rank[:, :, :], float(k), expert[:, :, :], ALU.is_equal, ALU.mult))
            own.wait()
            own.link(V.tensor_reduce(sel[:, :, :], pick[:, :, :, :], AX.X, ALU.add))
            for k in range(2):
                own.step(V.tensor_tensor(hot[:, k, :, :], sel[:, k, :].unsqueeze(2).broadcast_to([P, T, NX]),
                                         iota[:, 0:NX].unsqueeze(1).broadcast_to([P, T, NX]), ALU.is_equal))
            own.wait()
            V.tensor_tensor(both[:, :].rearrange("p (t e) -> p t e", t=T), hot[:, 0, :, :], hot[:, 1, :, :], ALU.add).then_inc(s["both_ready"], 1)
            own.step(V.memset(run[:, 0, :], 0.0))
            own.step(V.memset(one, 1.0))
            dve.wait_ge(s["sums_ready"], 1)
            for k in range(2):
                own.step(V.tensor_copy(ahead[:, 8 * k:8 * k + 8, :].rearrange("p t e -> p (t e)"), bank[4 + k][:, :]))
                own.step(V.tensor_copy(total[:, 8 * k:8 * k + 8, :].rearrange("p t e -> p (t e)"), bank[6 + k][:, :]))
            own.wait()
            for t in range(T):
                own.link(V.tensor_tensor(run[:, t + 1, :], run[:, t, :], total[:, t, :], ALU.add))
            own.step(V.tensor_tensor(ahead[:, :, :], ahead[:, :, :], run[:, 0:T, :], ALU.add))
            own.link(V.tensor_scalar(nb_i[:, :], run[:, T, :], float(CAP), float(P - 1), ALU.min, ALU.add))
            own.link(V.tensor_scalar(nb_i[:, :], nb_i[:, :], P.bit_length() - 1, None, ALU.arith_shift_right))
            own.link(V.tensor_copy(nb, nb_i[:, :]))
            own.link(V.tensor_tensor_scan(bend, one, nb, 0.0, ALU.mult, ALU.add))
            own.link(V.tensor_tensor(bstart, bend, nb, ALU.subtract))
            own.step(V.tensor_tensor(prod[:, 0, :, :], hot[:, 0, :, :], ahead[:, :, :], ALU.mult))
            own.link(V.tensor_tensor(ahead[:, :, :], ahead[:, :, :], hot[:, 0, :, :], ALU.add))
            own.link(V.tensor_tensor(prod[:, 1, :, :], hot[:, 1, :, :], ahead[:, :, :], ALU.mult))
            own.link(V.tensor_reduce(place[:, :, :], prod[:, :, :, :], AX.X, ALU.add))
            for k in range(2):
                own.step(V.tensor_tensor(prod[:, k, :, :], hot[:, k, :, :], bstart.unsqueeze(1).broadcast_to([P, T, NX]), ALU.mult))
            own.wait()
            own.step(V.tensor_reduce(first[:, :, :], prod[:, :, :, :], AX.X, ALU.add))
            own.link(V.tensor_scalar(keep[:, :, :], place[:, :, :], float(CAP), None, ALU.is_lt))
            own.link(V.scalar_tensor_tensor(place[:, :, :], first[:, :, :], float(P), place[:, :, :], ALU.mult, ALU.add))
            own.link(V.tensor_tensor(place[:, :, :], place[:, :, :], keep[:, :, :], ALU.mult))
            own.step(V.tensor_copy(y_idx[:, 0:2 * T].rearrange("p (t k) -> p k t", k=2), place[:, :, :]))
            own.step(V.memset(y_idx[:, 2 * T:], 0))
            own.step(V.tensor_scalar(gain[:, :].rearrange("p (t k) -> p k t", k=2), keep[:, :, :], 0.5, None, ALU.mult))
            own.link(V.tensor_copy(slot_i[:, :, :], place[:, :, :]))
            own.step(V.tensor_scalar(lo_i[:, :, :], slot_i[:, :, :], P - 1, None, ALU.bitwise_and))
            own.link(V.tensor_scalar(hi_i[:, :, :], slot_i[:, :, :], P.bit_length() - 1, None, ALU.arith_shift_right))
            own.link(V.scalar_tensor_tensor(row[:, :, :], lo_i[:, :, :], float(NB), hi_i[:, :, :], ALU.mult, ALU.add))
            own.link(V.tensor_tensor(row[:, :, :], row[:, :, :], trash[:, :, :], ALU.subtract))
            own.link(V.tensor_tensor(row[:, :, :], row[:, :, :], keep[:, :, :], ALU.mult))
            V.tensor_tensor(row_i[:, :, :], row[:, :, :], trash[:, :, :], ALU.add).then_inc(s["row_ready"], 1)
            own.link(V.tensor_tensor(bmask[:, :, :], iota_blk[:, :].unsqueeze(2).broadcast_to([P, NB, NX]),
                                     bend.unsqueeze(1).broadcast_to([P, NB, NX]), ALU.is_ge))
            own.link(V.tensor_reduce(bexp[:, :], bmask[:, :, :], AX.X, ALU.add))
            own.link(V.tensor_scalar(bexp[:, :], bexp[:, :], float(NX - 1), None, ALU.min))
            own.link(V.tensor_copy(block_expert[:, :], bexp[:, :]))

        @block.scalar
        def _(act):
            A = nc.scalar
            act.sem_inc(s["xn_ready"], LEAD)
            act.sem_inc(s["xT_ready"], LEAD)
            act.wait_ge(s["shift_ready"], 1)
            with act.Fori(0, T // 2) as i:
                for u in two:
                    t = i * 2 + u
                    retired(act, s["xT_ps"], t)
                    A.activation(xn[u][:, :], x[:, bass.ds(t, 1), :].rearrange("p a d -> p (a d)"), ACT.Identity,
                                 bias=shift[:, bass.ds(t, 1)], scale=rstd[:, bass.ds(t, 1)]).then_inc(s["xn_ready"], 1)
                for u in two:
                    t = i * 2 + u
                    made(act, s["xT_ps"], t)
                    retired(act, s["logit_ps"], t)
                    A.activation(xT[u][:, :, :].rearrange("p k n -> p (k n)"), bank[u][:, :], ACT.Copy).then_inc(s["xT_ready"], 1)

        @block.tensor
        def _(pe):
            M = nc.tensor
            pe.sem_inc(s["xT_ps"], LEAD)
            pe.sem_inc(s["logit_ps"], LEAD)
            pe.wait_ge(s["weights_in"], 16)
            with pe.Fori(0, T // 2) as i:
                for u in two:
                    t = i * 2 + u
                    made(pe, s["xn_ready"], t)
                    for k in range(K):
                        last = M.transpose(bank[u][:, k * P:(k + 1) * P], xn[u][:, k * P:(k + 1) * P], ident[:, :])
                    last.then_inc(s["xT_ps"], 1)
                for u in two:
                    t = i * 2 + u
                    made(pe, s["xT_ready"], t)
                    retired(pe, s["taken"], t)
                    for k in range(K):
                        last = M.matmul(bank[2 + u][:, 0:NH * NX], xT[u][:, k, :], hp[:, k, :], start=(k == 0), stop=(k == K - 1))
                    last.then_inc(s["logit_ps"], 1)
            pe.wait_ge(s["consts_made"], 6)
            pe.wait_ge(s["both_ready"], 1)
            for k in range(2):
                M.matmul(bank[4 + k][:, :], lower[:, :], both[:, k * 512:(k + 1) * 512], start=True, stop=True)
                last = M.matmul(bank[6 + k][:, :], ones[:, :], both[:, k * 512:(k + 1) * 512], start=True, stop=True)
            last.then_inc(s["sums_ready"], 1)


def layer1_experts(nc, v):
    ident, bank, tok_idx, block_expert = (v[k] for k in ("ident", "bank", "tok_idx", "block_expert"))
    xn_dram, y_dram = v["xn_dram"], v["y_dram"]
    QUADS = 4
    PAIRS = NB // 2
    DH = D // 2
    two = range(2)
    with ExitStack() as ctx:
        sb, sem = allocators(nc, ctx, "experts1")
        rows = [sb(f"rows{q}", [P, 4, D]) for q in range(QUADS)]
        idx = [sb(f"idx{h}", [P, 16], I32) for h in range(2)]
        w = [sb(f"w{r}", [P, K * HX + DH]) for r in range(4)]
        xT = [sb(f"xT{u}", [P, K, P]) for u in two]
        hT = [sb(f"hT{u}", [P, P]) for u in two]
        y = [sb(f"y{q}", [P, 2, D]) for q in two]
        names = ("idx_ready", "gate", "xT_ps", "xT_ready", "h_ps", "h_ready", "y_ps", "y_ready")
        s = {n: sem(n) for n in names}
        gathered = [sem(f"gathered{q}") for q in range(QUADS)]
        w_in = [sem(f"w_in{r}") for r in range(4)]
        y_stored = [sem(f"y_stored{q}") for q in two]
        block = ctx.enter_context(nc.Block())

        @block.sync
        def _(sp):
            def load(i, q):
                m = i * 2 + q
                retired(sp, s["y_ps"], m)
                for u in two:
                    e = sp.value_load(block_expert[0:1, bass.ds(m * 2 + u, 1)], min_val=0, max_val=NX - 1)
                    sp.dma_start(w[2 * q + u][:, :], v["x12_in"][bass.ds(e, 1), :, :].rearrange("a p c -> (a p) c")).then_inc(w_in[2 * q + u], 16)

            def store(i, q):
                m = i * 2 + q
                made(sp, s["y_ready"], m)
                sp.dma_start(y_dram[bass.ds(m * (2 * P), 2 * P), :].rearrange("(t p) d -> p t d", p=P), y[q][:, :, :]).then_inc(y_stored[q], 16)

            for q in two:
                load(0, q)
            with sp.Fori(1, PAIRS // 2) as i:
                for q in two:
                    load(i, q)
                    store(i - 1, q)
            for q in two:
                store(PAIRS // 2 - 1, q)
            for q in two:
                sp.wait_ge(y_stored[q], 16 * PAIRS // 2)

        @block.gpsimd
        def _(gp):
            gather_quads(nc, gp, s, gathered, NB, rows, idx, tok_idx, xn_dram, s["xT_ps"], 4)

        @block.vector
        def _(dve):
            V = nc.vector
            dve.sem_inc(s["xT_ready"], LEAD)
            dve.sem_inc(s["y_ready"], LEAD)

            def turned(i, q):
                for u in two:
                    b = i * 4 + q * 2 + u
                    made(dve, s["xT_ps"], b, lead=4 * QUADS)
                    retired(dve, s["h_ps"], b)
                    V.tensor_copy(xT[u][:, :, :].rearrange("p k n -> p (k n)"), bank[u][:, :]).then_inc(s["xT_ready"], 1)

            def result(i, q, first):
                made(dve, s["y_ps"], i * 2 + q)
                if not first:
                    dve.wait_ge(y_stored[q], i * 16)
                for h in two:
                    last = V.tensor_copy(y[q][:, :, h * DH:(h + 1) * DH], bank[4 + 2 * q + h][:, :].rearrange("p (t c) -> p t c", c=DH))
                last.then_inc(s["y_ready"], 1)

            turned(0, 0)
            turned(0, 1)
            result(0, 0, True)
            turned(1, 0)
            result(0, 1, True)
            with dve.Fori(1, PAIRS // 2 - 1) as i:
                turned(i, 1)
                result(i, 0, False)
                turned(i + 1, 0)
                result(i, 1, False)
            turned(PAIRS // 2 - 1, 1)
            for q in two:
                result(PAIRS // 2 - 1, q, False)

        @block.scalar
        def _(act):
            act.sem_inc(s["h_ready"], LEAD)
            with act.Fori(0, PAIRS) as m:
                for u in two:
                    b = m * 2 + u
                    made(act, s["h_ps"], b)
                    retired(act, s["y_ps"], m, ring=1)
                    nc.scalar.activation(hT[u][0:HX, :], bank[2 + u][0:HX, 0:P], ACT.Gelu)
                    nc.scalar.activation(hT[u][HX:, :], bank[2 + u][0:HX, 0:P], ACT.Gelu).then_inc(s["h_ready"], 1)

        @block.tensor
        def _(pe):
            M = nc.tensor
            pe.sem_inc(s["xT_ps"], 4 * QUADS)
            pe.sem_inc(s["h_ps"], LEAD)
            pe.sem_inc(s["y_ps"], LEAD)

            def turn(i, j):
                for u in two:
                    q, r = j // 2, 2 * (j % 2) + u
                    pe.wait_ge(gathered[q], i * 64 + 64)
                    retired(pe, s["xT_ready"], i * 16 + j * 2 + u)
                    for k in range(K):
                        last = M.transpose(bank[u][:, k * P:(k + 1) * P], rows[q][:, r, k:D:K], ident[:, :])
                    last.then_inc(s["xT_ps"], 1)

            def hidden(i, j):
                for u in two:
                    b, r = i * 16 + j * 2 + u, (2 * j + u) % 4
                    made(pe, s["xT_ready"], b)
                    retired(pe, s["h_ready"], b)
                    pe.wait_ge(w_in[r], (i * 4 + (2 * j + u) // 4) * 16 + 16)
                    for k in range(K):
                        last = M.matmul(bank[2 + u][0:HX, 0:P], w[r][:, k * HX:(k + 1) * HX], xT[u][:, k, :], start=(k == 0), stop=(k == K - 1))
                    last.then_inc(s["h_ps"], 1)

            def result(i, j):
                a, b = bank[4 + 2 * (j % 2)], bank[5 + 2 * (j % 2)]
                retired(pe, s["y_ready"], i * 8 + j)
                for u in two:
                    made(pe, s["h_ready"], i * 16 + j * 2 + u)
                    w2 = w[(2 * j + u) % 4][:, K * HX:]
                    M.matmul(a[:, u * DH:(u + 1) * DH], hT[u][0:HX, :], w2[0:HX, :], start=True, stop=True)
                    last = M.matmul(b[:, u * DH:(u + 1) * DH], hT[u][HX:, :], w2[HX:, :], start=True, stop=True)
                last.then_inc(s["y_ps"], 1)

            steps = NB // 16
            turn(0, 0)
            with pe.Fori(0, steps - 1) as i:
                for j in range(8):
                    hidden(i, j)
                    if j < 7:
                        turn(i, j + 1)
                    else:
                        turn(i + 1, 0)
                    result(i, j)
            for j in range(8):
                hidden(steps - 1, j)
                if j < 7:
                    turn(steps - 1, j + 1)
                result(steps - 1, j)


def layer1_combine(nc, v):
    x, y_idx, gain = (v[k] for k in ("x", "y_idx", "gain"))
    QUADS = 4
    with ExitStack() as ctx:
        sb, sem = allocators(nc, ctx, "combine1")
        rows = [sb(f"rows{q}", [P, 4, D]) for q in range(QUADS)]
        idx = [sb(f"idx{h}", [P, 16], I32) for h in range(2)]
        s = {n: sem(n) for n in ("idx_ready", "gate", "added", "out_stored")}
        gathered = [sem(f"gathered{q}") for q in range(QUADS)]
        block = ctx.enter_context(nc.Block())

        @block.gpsimd
        def _(gp):
            gather_quads(nc, gp, s, gathered, 2 * T, rows, idx, y_idx, v["y_dram"], s["added"], 4)

        @block.vector
        def _(dve):
            dve.sem_inc(s["added"], 4 * QUADS)
            with dve.Fori(0, 2 * T // (4 * QUADS)) as i:
                for r in range(4 * QUADS):
                    n = i * (4 * QUADS) + r
                    dve.wait_ge(gathered[r // 4], i * 64 + 64)
                    xt = x[:, bass.ds(i * (2 * QUADS) + r // 2, 1), :].rearrange("p a d -> p (a d)")
                    if r % 2:
                        made(dve, s["added"], n - 1, lead=4 * QUADS)
                    nc.vector.scalar_tensor_tensor(xt, rows[r // 4][:, r % 4, :], gain[:, bass.ds(n, 1)], xt,
                                                   ALU.mult, ALU.add).then_inc(s["added"], 1)

        @block.sync
        def _(sp):
            with sp.Fori(0, T // 2) as i:
                made(sp, s["added"], i * 4 + 3, lead=4 * QUADS)
                sp.dma_start(v["out"][bass.ds(i * 2 * P, 2 * P), :].rearrange("(t p) d -> p t d", p=P),
                             x[:, bass.ds(i * 2, 2), :]).then_inc(s["out_stored"], 16)
            sp.wait_ge(s["out_stored"], 16 * T // 2)


KINDS = [1, 0, 2, 3]


def dram_inputs(inputs):
    f = {k: np.ascontiguousarray(a) for k, a in inputs.items()}
    w, y, a20 = f["edge_weight"], f["edge_attr_4"], f["edge_attr_20"]
    rec = np.zeros((E, REC), w.dtype)
    rec[:, R_W], rec[:, R_Y:R_Y + 4], rec[:, R_F:R_F + 20] = w, y, a20
    def chunks(a):
        return a.reshape(K, P).T

    laid = {
        "x_in": f["x"], "to_in": f["src"], "from_in": f["dst"], "rec_in": rec, "wg_in": f["L0_gnn_weight"].T,
        "wg1_in": f["L0_ffn_Wg1"], "bg1_in": f["L0_ffn_bg1"].reshape(-1, 1),
        "wg2_in": f["L0_ffn_Wg2"], "bg2_in": f["L0_ffn_bg2"].reshape(1, -1),
        "w1_in": f["L0_ffn_W1"].transpose(1, 0, 2).reshape(D, D), "b1_in": f["L0_ffn_b1"].reshape(1, D),
        "gb1_in": np.stack([chunks(f["L0_ffn_g1"]), chunks(f["L0_ffn_be1"])], axis=1),
        "w2_in": f["L0_ffn_W2"], "b2_in": f["L0_ffn_b2"].reshape(1, D),
        "g2_in": f["L0_ffn_g2"].reshape(1, D), "be2_in": f["L0_ffn_be2"].reshape(1, D),
        "w_in_in": np.stack([f["L1_gnn_w_in2f_s"], f["L1_gnn_w_in2f_v"]], axis=1),
        "wr_in": f["L1_gnn_W1"], "br_in": np.tile(f["L1_gnn_b1"], 4).reshape(P, 1),
        "wf_in": f["L1_gnn_W2"].reshape(F, F, 6)[:, :, KINDS].transpose(0, 2, 1).reshape(F, P),
        "bf_in": np.tile(f["L1_gnn_b2"].reshape(F, 6)[:, KINDS].T.reshape(1, P), (1, 4)),
        "w1s_in": f["L1_gnn_w_f2o1_s"], "w1v_in": f["L1_gnn_w_f2o1_v"],
        "w2s_in": f["L1_gnn_w_f2o2_s"], "w2v_in": f["L1_gnn_w_f2o2_v"],
        "hp_in": f["L1_ffn_hash_proj"].transpose(1, 0, 2).reshape(D, NH * NX),
        "x12_in": np.concatenate([f["L1_ffn_W1"].reshape(NX, P, K * HX),
                                  f["L1_ffn_W2"].reshape(NX, HX, 2, D // 2).transpose(0, 2, 1, 3).reshape(NX, P, D // 2)], axis=2),
        "w3_in": f["L0_ffn_W3"].reshape(D, D), "b3_in": f["L0_ffn_b3"],
    }
    return {k: np.ascontiguousarray(a) for k, a in laid.items()}


def kernel(**inputs):
    import concourse.bacc as bacc
    from concourse.bass_utils import run_bass_kernel_spmd

    nc = bacc.Bacc("TRN2", target_bir_lowering=False, num_devices=1)
    arrays, args = {}, {}
    for name, a in dram_inputs(inputs).items():
        arrays[name] = a
        args[name] = nc.dram_tensor(name, a.shape, mybir.dt.from_np(a.dtype), kind="ExternalInput").ap()
    args["out"] = nc.dram_tensor("out", (N, D), FP32, kind="ExternalOutput").ap()
    build(nc, args)
    r = run_bass_kernel_spmd(nc, [arrays], core_ids=[0])
    return r.results[0]["out"]
```

```python
import numpy as np
import concourse.bass as bass
from concourse import mybir
from contextlib import ExitStack

FP32 = mybir.dt.float32
BF16 = mybir.dt.bfloat16
I32 = mybir.dt.int32
U32 = mybir.dt.uint32
ALU = mybir.AluOpType
ACT = mybir.ActivationFunctionType
AX = mybir.AxisListType

P = 128
N = 2048
D = 512
T = N // P
K = D // P
E = 32768
J = E // P
B = N // P
GE = 2 * P
G = E // GE + B
ET = 2 * G
REC = 28
R_W, R_Y, R_F, R_FROM, R_TO = 0, 1, 5, 25, 26
EPS = 1e-5


class Chain:

    def __init__(self, eng, sem):
        self.eng, self.sem, self.n, self.i, self.base, self.per = eng, sem, 0, None, 0, 0

    def enter(self, i, per, first=0):
        self.base, self.i, self.per, self.n = self.n, i - first, per, 0

    def leave(self, times):
        assert self.n == self.per, (self.n, self.per)
        self.n, self.i = self.base + self.per * times, None

    def step(self, ins):
        ins.then_inc(self.sem, 1)
        self.n += 1

    def wait(self):
        self.eng.wait_ge(self.sem, self.n if self.i is None else self.i * self.per + (self.base + self.n))

    def link(self, ins):
        self.step(ins)
        self.wait()


LEAD = 2


def made(eng, sem, n, lead=LEAD):
    eng.wait_ge(sem, n + 1 + lead)


def retired(eng, sem, n, ring=LEAD, lead=LEAD):
    eng.wait_ge(sem, n + 1 + lead - ring)


def allocators(nc, ctx, layer):
    def sb(name, shape, dt=FP32):
        return ctx.enter_context(nc.sbuf_tensor(f"{layer}_{name}", shape, dt))

    def sem(name):
        return nc.alloc_semaphore(f"{layer}_{name}")

    return sb, sem


def clear_semaphores(nc, before):
    nc.clear_and_free_semaphores(nc.allocated_since(before))
    nc.all_engine_barrier()


def norm_stats(nc, own, x, stats, mean, rstd, var_ready, tiles=(0, T), collected=False):
    V = nc.vector
    start, end = tiles
    if not collected:
        with nc.vector.Fori(start, end) as t:
            own.enter(t, 1, first=start)
            own.step(V.bn_stats(stats[:, bass.ds(t, 1), :], x[:, bass.ds(t, 1), :]))
            own.leave(end - start)
        own.wait()
    mean, rstd, stats = mean[:, start:end], rstd[:, start:end], stats[:, start:end, :]
    me, ve, mo, vo = stats[:, :, 1], stats[:, :, 2], stats[:, :, 4], stats[:, :, 5]
    own.step(V.tensor_tensor(mean, me, mo, ALU.add))
    own.link(V.tensor_tensor(rstd, me, mo, ALU.subtract))
    own.step(V.tensor_scalar(mean, mean, 0.5, None, ALU.mult))
    own.step(V.tensor_tensor(stats[:, :, 0], ve, vo, ALU.add))
    own.link(V.scalar_tensor_tensor(rstd, rstd, 0.25, rstd, ALU.mult, ALU.mult))
    own.link(V.scalar_tensor_tensor(rstd, stats[:, :, 0], 1.0 / D, rstd, ALU.mult, ALU.add))
    V.tensor_scalar(rstd, rstd, EPS, None, ALU.add).then_inc(var_ready, 1)


def build(nc, dram):
    with ExitStack() as ctx:
        sb, sem = allocators(nc, ctx, "all")
        rec_dram = nc.dram_tensor("rec_dram", [P * ET, REC], FP32, kind="Internal").ap()
        h_dram = nc.dram_tensor("h_dram", [N, D], FP32, kind="Internal").ap()
        feat_dram = nc.dram_tensor("feat_dram", [N, P], FP32, kind="Internal").ap()
        xn_dram = nc.dram_tensor("xn_dram", [N, D], FP32, kind="Internal").ap()
        tok_dram = nc.dram_tensor("tok_dram", [P * NB + 2 * N, 1], I32, kind="Internal").ap()
        y_dram = nc.dram_tensor("y_dram", [NB * P, D], FP32, kind="Internal").ap()

        x = sb("x", [P, T, D])
        ident = sb("ident", [P, P])
        iota = sb("iota", [P, P])
        edges = sb("edges", [P, ET, REC])
        from_idx = sb("from_idx", [P, ET + 16], I32)
        to_loc = sb("to_loc", [P, ET])
        group_tile = sb("group_tile", [P, G])
        group_tile_i = sb("group_tile_i", [P, G], I32)
        stats = sb("stats", [P, T, 6])
        mean = sb("mean", [P, T])
        rstd = sb("rstd", [P, T])
        shift = sb("shift", [P, T])
        neghalf = sb("neghalf", [P, P])
        bank = [ctx.enter_context(nc.psum_tensor(f"bank{k}", [P, 512], FP32)) for k in range(8)]

        v = {**dram, **locals()}
        before = nc.snapshot_sems()
        layer0_prepare(nc, v)
        with ExitStack() as layer1:
            v["hT"] = layer1.enter_context(nc.sbuf_tensor("hT", [P, F * ET], FP32))
            layer0_edges(nc, v)
            layer0_ffn(nc, v)
            clear_semaphores(nc, before)
            v["agg"] = layer1.enter_context(nc.sbuf_tensor("agg", [P, T, 8 * F], FP32))
            layer1_features(nc, v)
            layer1_edges(nc, v)
            layer1_nodes(nc, v)
        with ExitStack() as ffn1:
            def sb(name, shape, dt):
                return ffn1.enter_context(nc.sbuf_tensor(name, shape, dt))

            v["tok_idx"] = sb("tok_idx", [P, NB + 16], I32)
            v["y_idx"] = sb("y_idx", [P, 2 * T + 16], I32)
            v["gain"] = sb("gain", [P, 2 * T], FP32)
            v["block_expert"] = sb("block_expert", [P, NB], I32)
            layer1_route(nc, v)
            layer1_experts(nc, v)
            layer1_combine(nc, v)


def layer0_prepare(nc, v):
    x_in, to_in, from_in, rec_in, wg_in = (v[k] for k in ("x_in", "to_in", "from_in", "rec_in", "wg_in"))
    x, ident, iota, edges, from_idx, to_loc = (v[k] for k in ("x", "ident", "iota", "edges", "from_idx", "to_loc"))
    group_tile, group_tile_i = v["group_tile"], v["group_tile_i"]
    stats, mean, rstd, neghalf, bank = v["stats"], v["mean"], v["rstd"], v["neghalf"], v["bank"]
    rec_dram, h_dram = v["rec_dram"], v["h_dram"]
    with ExitStack() as ctx:
        sb, sem = allocators(nc, ctx, "prepare")
        rec = sb("rec", [P, J, REC])
        from_i, to_i, bkt_i = (sb(n, [P, J], I32) for n in ("from_i", "to_i", "bkt_i"))
        bkt = sb("bkt", [P, J])
        h = sb("h", [P, T, D])
        h_flat = h[:, :, :].rearrange("p t d -> p (t d)")
        mask = h_flat[:, 0:B * J].rearrange("p (b j) -> p b j", b=B)
        scan = h_flat[:, B * J:2 * B * J]
        ones_row = sb("ones_row", [P, B * J], BF16)
        pos = sb("pos", [P, J])
        pos_i, slot_i = (sb(n, [P, J], I32) for n in ("pos_i", "slot_i"))
        iota_b = sb("iota_b", [P, B])
        iota_g = sb("iota_g", [P, G])
        ones = sb("ones", [P, P])
        lower = sb("lower", [P, P])
        small = sb("small", [P, 7, B])
        cnt, before, pre, tot, adj, ng, gend = (small[:, k, :] for k in range(7))
        ng_i = sb("ng_i", [P, B], I32)
        gmask = sb("gmask", [P, G, B])
        STAGES, SB = 2, 16
        stage_rec = sb("stage_rec", [P, STAGES, SB, REC])
        stage_pos = sb("stage_pos", [P, STAGES, SB], I32)
        wg = sb("wg", [P, K, D])
        xn = [sb(f"xn{u}", [P, D]) for u in range(2)]
        xT = [sb(f"xT{u}", [P, K, P]) for u in range(2)]

        ends_in, rec_landed, x_landed, wg_landed = (sem(n) for n in ("ends_in", "rec_landed", "x_landed", "wg_landed"))
        iotas_made, consts_made, pool_own, dve_own = (sem(n) for n in ("iotas_made", "consts_made", "pool_own", "dve_own"))
        ends_filled, cnt_ready, sums_ready, pos_ready = (
            sem(n) for n in ("ends_filled", "cnt_ready", "sums_ready", "pos_ready"))
        pad_made, pad_written, pos_staged, rec_staged, gate = (
            sem(n) for n in ("pad_made", "pad_written", "pos_staged", "rec_staged", "gate"))
        stage_sent = [sem(f"stage_sent{q}") for q in range(STAGES)]
        var_ready, rstd_ready = (sem(n) for n in ("var_ready", "rstd_ready"))
        xn_ready, xT_ps, xT_ready, h_ps, h_ready, h_stored = (
            sem(n) for n in ("xn_ready", "xT_ps", "xT_ready", "h_ps", "h_ready", "h_stored"))
        block = ctx.enter_context(nc.Block())

        @block.sync
        def _(sp):
            sp.dma_start(to_i[:, :], to_in.rearrange("(p j) -> p j", p=P)).then_inc(ends_in, 16)
            sp.dma_start(from_i[:, :], from_in.rearrange("(p j) -> p j", p=P)).then_inc(ends_in, 16)
            sp.dma_start(rec[:, :, :], rec_in.rearrange("(p j) c -> p j c", p=P)).then_inc(rec_landed, 16)
            sp.wait_ge(pad_written, 16)
            sp.dma_start(x[:, :, :], x_in.rearrange("(t p) d -> p t d", p=P)).then_inc(x_landed, 16)
            sp.dma_start(wg[:, :, :], wg_in.rearrange("(k p) e -> p k e", p=P)).then_inc(wg_landed, 16)
            with sp.Fori(0, T) as t:
                made(sp, h_ready, t)
                sp.dma_start(h_dram[bass.ds(t * P, P), :], h[:, bass.ds(t, 1), :].rearrange("p a d -> p (a d)")).then_inc(h_stored, 16)
            sp.wait_ge(h_stored, 16 * T)

        @block.gpsimd
        def _(gp):
            own = Chain(gp, pool_own)
            nc.gpsimd.iota(iota_b[:, :], [[1, B]], base=0, channel_multiplier=0, allow_small_or_imprecise_dtypes=True).then_inc(iotas_made, 1)
            nc.gpsimd.iota(iota_g[:, :], [[1, G]], base=0, channel_multiplier=0, allow_small_or_imprecise_dtypes=True).then_inc(iotas_made, 1)
            own.step(nc.gpsimd.memset(ones[:, :], 1.0))
            own.step(nc.gpsimd.memset(ident[:, :], 0.0))
            nc.gpsimd.memset(ones_row[:, :], 1.0).then_inc(iotas_made, 1)
            own.wait()
            nc.gpsimd.affine_select(out=lower[:, :], in_=ones[:, :], compare_op=ALU.is_gt, fill=0.0, base=0,
                                    pattern=[[1, P]], channel_multiplier=-1).then_inc(consts_made, 1)
            own.link(nc.gpsimd.memset(edges[:, :, :], 0.0))
            nc.gpsimd.memset(edges[:, :, R_TO:R_TO + 1], -1.0).then_inc(pad_made, 1)
            gp.wait_ge(pad_made, 1)
            gp.dma_start(rec_dram.rearrange("(p t) c -> p (t c)", p=P), edges[:, :, :].rearrange("p t c -> p (t c)")).then_inc(pad_written, 16)
            nc.gpsimd.iota(iota[:, :], [[1, P]], base=0, channel_multiplier=0, allow_small_or_imprecise_dtypes=True).then_inc(consts_made, 1)
            nc.gpsimd.memset(neghalf[:, :], -0.5).then_inc(consts_made, 1)
            nc.gpsimd.affine_select(out=ident[:, :], in_=ident[:, :], compare_op=ALU.not_equal, fill=1.0, base=0,
                                    pattern=[[-1, P]], channel_multiplier=1).then_inc(consts_made, 1)
            gp.wait_ge(pos_ready, 1)
            def stage(j, q):
                at = (j * STAGES + q) * SB
                nc.gpsimd.tensor_copy(stage_pos[:, q, :], pos_i[:, bass.ds(at, SB)]).then_inc(pos_staged, 1)

            def place(j, q, refill):
                gp.wait_ge(pos_staged, j * STAGES + q + 1)
                gp.sem_inc(gate, 1)
                gp.wait_ge(rec_staged, j * STAGES + q + 1)
                gp.sem_inc(gate, 1)
                for k in range(SB):
                    gp.indirect_dma_start(out=rec_dram, in_=stage_rec[:, q, k, :], in_offset=None,
                                          out_offset=bass.IndirectOffsetOnAxis(ap=stage_pos[:, q, k:k + 1], axis=0)
                                          ).then_inc(stage_sent[q], 16)
                    if refill and k == SB // 2:
                        if refill == "again":
                            gp.wait_ge(stage_sent[1 - q], (j + q) * (16 * SB))
                            gp.sem_inc(gate, 1)
                        stage(j + q, 1 - q)

            gp.wait_ge(pad_written, 16)
            stage(0, 0)
            place(0, 0, "new")
            place(0, 1, "again")
            gp.wait_ge(var_ready, 1)
            gp.wait_ge(consts_made, 4)
            nc.gpsimd.tensor_tensor(rstd[:, :], rstd[:, :], neghalf[:, 0:T], ALU.pow).then_inc(rstd_ready, 1)
            with gp.Fori(1, J // SB // STAGES - 1) as j:
                for q in range(STAGES):
                    place(j, q, "again")
            last = J // SB // STAGES - 1
            place(last, 0, "again")
            place(last, 1, "")
            for q in range(STAGES):
                gp.wait_ge(stage_sent[q], 16 * J // STAGES)

        @block.vector
        def _(dve):
            own = Chain(dve, dve_own)
            V = nc.vector
            dve.sem_inc(xn_ready, LEAD)
            dve.sem_inc(h_ready, LEAD)
            dve.wait_ge(ends_in, 32)
            own.link(V.tensor_scalar(bkt_i[:, :], to_i[:, :], 7, None, ALU.arith_shift_right))
            own.link(V.tensor_copy(bkt[:, :], bkt_i[:, :]))
            dve.wait_ge(iotas_made, 3)
            own.link(V.tensor_tensor(mask, bkt[:, :].unsqueeze(1).broadcast_to([P, B, J]),
                                     iota_b[:, :].unsqueeze(2).broadcast_to([P, B, J]), ALU.is_equal))
            sc3 = scan.rearrange("p (b j) -> p b j", b=B)
            own.step(V.memset(before[:, 0:1], 0.0))
            own.link(V.tensor_tensor_scan(scan, ones_row[:, :], h_flat[:, 0:B * J], 0.0, ALU.mult, ALU.add))
            own.link(V.tensor_copy(before[:, 1:B], sc3[:, 0:B - 1, J - 1]))
            V.tensor_tensor(cnt, sc3[:, :, J - 1], before, ALU.subtract).then_inc(cnt_ready, 1)
            dve.wait_ge(rec_landed, 16)
            V.tensor_copy(rec[:, :, R_FROM], from_i[:, :]).then_inc(ends_filled, 1)
            V.tensor_copy(rec[:, :, R_TO], to_i[:, :]).then_inc(ends_filled, 1)
            dve.wait_ge(sums_ready, 1)
            own.link(V.tensor_copy(small[:, 2:4, :], bank[7][:, 0:2 * B].rearrange("p (a b) -> p a b", a=2)))
            own.link(V.tensor_scalar(ng_i[:, :], tot, float(GE - 1), None, ALU.add))
            own.link(V.tensor_scalar(ng_i[:, :], ng_i[:, :], GE.bit_length() - 1, None, ALU.arith_shift_right))
            own.link(V.tensor_copy(ng, ng_i[:, :]))
            own.link(V.tensor_tensor_scan(gend, ones_row[:, 0:B], ng, 0.0, ALU.mult, ALU.add))
            own.link(V.tensor_tensor(adj, gend, ng, ALU.subtract))
            own.link(V.scalar_tensor_tensor(adj, adj, float(GE), pre, ALU.mult, ALU.add))
            own.link(V.scalar_tensor_tensor(adj, adj, -1.0, before, ALU.add, ALU.subtract))
            for b in range(B):
                own.step(V.scalar_tensor_tensor(sc3[:, b, :], sc3[:, b, :], adj[:, b:b + 1], mask[:, b, :], ALU.add, ALU.mult))
            own.wait()
            own.link(V.tensor_reduce(pos[:, :], scan.rearrange("p (b j) -> p j b", b=B), AX.X, ALU.add))
            own.link(V.tensor_copy(slot_i[:, :], pos[:, :]))
            own.step(V.tensor_scalar(pos_i[:, :], slot_i[:, :], P - 1, None, ALU.bitwise_and))
            own.link(V.tensor_scalar(slot_i[:, :], slot_i[:, :], P.bit_length() - 1, None, ALU.arith_shift_right))
            V.scalar_tensor_tensor(pos_i[:, :], pos_i[:, :], float(ET), slot_i[:, :], ALU.mult, ALU.add).then_inc(pos_ready, 1)
            own.link(V.tensor_tensor(gmask[:, :, :], iota_g[:, :].unsqueeze(2).broadcast_to([P, G, B]),
                                     gend.unsqueeze(1).broadcast_to([P, G, B]), ALU.is_ge))
            own.link(V.tensor_reduce(group_tile[:, :], gmask[:, :, :], AX.X, ALU.add))
            own.link(V.tensor_scalar(group_tile[:, :], group_tile[:, :], float(B - 1), None, ALU.min))
            own.link(V.tensor_copy(group_tile_i[:, :], group_tile[:, :]))
            dve.wait_ge(x_landed, 16)
            norm_stats(nc, own, x, stats, mean, rstd, var_ready)
            dve.wait_ge(rstd_ready, 1)
            with dve.Fori(0, T // 2) as i:
                for u in range(2):
                    t = i * 2 + u
                    retired(dve, xT_ps, t)
                    V.tensor_scalar(xn[u][:, :], x[:, bass.ds(t, 1), :].rearrange("p a d -> p (a d)"),
                                    mean[:, bass.ds(t, 1)], rstd[:, bass.ds(t, 1)],
                                    ALU.subtract, ALU.mult).then_inc(xn_ready, 1)
                for u in range(2):
                    t = i * 2 + u
                    made(dve, h_ps, t)
                    V.tensor_copy(h[:, bass.ds(t, 1), :].rearrange("p a d -> p (a d)"), bank[2 + u][:, :]).then_inc(h_ready, 1)

        @block.scalar
        def _(act):
            act.sem_inc(xT_ready, LEAD)

            def stage(j, q):
                at = (j * STAGES + q) * SB
                nc.scalar.activation(stage_rec[:, q, :, :], rec[:, bass.ds(at, SB), :], ACT.Copy).then_inc(rec_staged, 1)

            def turned(i):
                for u in range(2):
                    t = i * 2 + u
                    made(act, xT_ps, t)
                    retired(act, h_ps, t)
                    nc.scalar.activation(xT[u][:, :, :].rearrange("p k n -> p (k n)"), bank[u][:, :], ACT.Copy).then_inc(xT_ready, 1)

            act.wait_ge(ends_filled, 2)
            assert J == T // 2 * STAGES * SB
            for q in range(STAGES):
                stage(0, q)
            with act.Fori(0, T // 2 - 1) as i:
                for q in range(STAGES):
                    act.wait_ge(stage_sent[q], i * (16 * SB) + 16 * SB)
                    stage(i + 1, q)
                turned(i)
            turned(T // 2 - 1)

        @block.tensor
        def _(pe):
            pe.sem_inc(xT_ps, LEAD)
            pe.sem_inc(h_ps, LEAD)
            pe.wait_ge(consts_made, 4)
            pe.wait_ge(cnt_ready, 1)
            nc.tensor.matmul(bank[7][:, 0:B], lower[:, :], cnt, start=True, stop=True)
            nc.tensor.matmul(bank[7][:, B:2 * B], ones[:, :], cnt, start=True, stop=True).then_inc(sums_ready, 1)
            pe.wait_ge(wg_landed, 16)
            with pe.Fori(0, T // 2) as i:
                for u in range(2):
                    t = i * 2 + u
                    made(pe, xn_ready, t)
                    retired(pe, xT_ready, t)
                    for k in range(K):
                        last = nc.tensor.transpose(bank[u][:, k * P:(k + 1) * P], xn[u][:, k * P:(k + 1) * P], ident[:, :])
                    last.then_inc(xT_ps, 1)
                for u in range(2):
                    t = i * 2 + u
                    made(pe, xT_ready, t)
                    retired(pe, h_ready, t)
                    for k in range(K):
                        last = nc.tensor.matmul(bank[2 + u][:, :], xT[u][:, k, :], wg[:, k, :], start=(k == 0), stop=(k == K - 1))
                    last.then_inc(h_ps, 1)


def gather_quads(nc, gp, s, gathered, tiles, rows, idx, from_idx, table, used, per, rest=None):
    def copy_idx(turn, h):
        nc.gpsimd.tensor_copy(idx[h][:, :], from_idx[:, bass.ds(turn * 16, 16)]).then_inc(s["idx_ready"], 1)

    def ring(i, h, first):
        turn = i * 2 + h
        gp.wait_ge(s["idx_ready"], turn + 1)
        gp.sem_inc(s["gate"], 1)
        for q in range(4):
            gp.wait_ge(used, (turn * 4 + q + 1) * per)
            gp.sem_inc(s["gate"], 1)
            for r in range(4):
                gp.indirect_dma_start(out=rows[q][:, r, :], out_offset=None, in_=table,
                                      in_offset=bass.IndirectOffsetOnAxis(ap=idx[h][:, 4 * q + r:4 * q + r + 1], axis=0)).then_inc(gathered[q], 16)
            if q == 1:
                if not (first and h == 0):
                    for b in range(4):
                        gp.wait_ge(gathered[b], turn * 64)
                    gp.sem_inc(s["gate"], 1)
                copy_idx(turn + 1, 1 - h)

    copy_idx(0, 0)
    ring(0, 0, True)
    ring(0, 1, True)
    if rest:
        gp.wait_ge(*rest)
    if tiles > 32:
        with gp.Fori(1, tiles // 32) as i:
            for h in range(2):
                ring(i, h, False)


def softplus_less_log2(nc, act, own, out, tmp, in_, scale=1.0):
    own.link(nc.scalar.activation(tmp, in_, ACT.Abs, scale=scale))
    own.link(nc.scalar.activation(tmp, tmp, ACT.Exp, scale=-1.0))
    return nc.scalar.activation(out, tmp, ACT.Ln, scale=0.5, bias=0.5)


def layer0_edges(nc, v):
    ident, hT = v["ident"], v["hT"]
    x, iota, edges, from_idx, to_loc = (v[k] for k in ("x", "iota", "edges", "from_idx", "to_loc"))
    group_tile, group_tile_i, bank, h_dram = v["group_tile"], v["group_tile_i"], v["bank"], v["h_dram"]
    QUADS = 4
    RING = 4 * QUADS
    HEAD = 3 * RING
    with ExitStack() as ctx:
        sb, sem = allocators(nc, ctx, "edges0")
        rows = [sb(f"rows{q}", [P, 4, D]) for q in range(QUADS)]
        idx = [sb(f"idx{h}", [P, 16], I32) for h in range(2)]
        S = [sb(f"S{r}", [P, P]) for r in range(8)]
        wr = sb("wr", [4 * RT, P])
        br = sb("br", [P, 1])
        fr = sb("fr", [P, RING, RT])
        fT = sb("fT", [4 * RT, 4 * P])
        pre, soft = (sb(n, [P, 4 * P]) for n in ("pre", "soft"))
        x_flat = x[:, :, :].rearrange("p t d -> p (t d)")
        prepared = sem("prepared")
        s = {n: sem(n) for n in ("edges_in", "idx_ready", "gate", "wr_zero", "wr_in", "act_own", "fr_ready", "fT_ps", "fT_ready", "pre_ps", "pre_ready",
                                 "soft_ready", "hT_ready")}
        gathered = [sem(f"gathered{q}") for q in range(QUADS)]
        S_ready, sum_ready, sum_added = sem("S_ready"), sem("sum_ready"), sem("sum_added")
        block = ctx.enter_context(nc.Block())

        @block.vector
        def _(dve):
            V = nc.vector
            dve.sem_inc(sum_added, 4)
            V.memset(wr[:, :], 0.0).then_inc(s["wr_zero"], 1)
            V.memset(from_idx[:, ET:], 0).then_inc(prepared, 1)
            dve.wait_ge(s["edges_in"], 16)
            V.tensor_copy(from_idx[:, 0:HEAD], edges[:, 0:HEAD, R_FROM]).then_inc(prepared, 1)
            dve.wait_ge(s["edges_in"], 32)
            V.tensor_copy(from_idx[:, HEAD:ET], edges[:, HEAD:ET, R_FROM]).then_inc(prepared, 1)
            e_to = edges[:, :, R_TO].rearrange("p (g k) -> p g k", k=2)
            V.scalar_tensor_tensor(to_loc[:, :].rearrange("p (g k) -> p g k", k=2),
                                   group_tile[:, :].unsqueeze(2).broadcast_to([P, G, 2]), -float(P), e_to,
                                   ALU.mult, ALU.add).then_inc(prepared, 1)
            dve.wait_ge(prepared, 4)
            dve.wait_ge(s["wr_in"], 80)

            def weights(i, pair):
                for u in range(2):
                    g = i * (RING // 2) + pair * 2 + u
                    retired(dve, sum_ready, g, ring=4, lead=RING // 2)
                    for k in range(2):
                        e = g * 2 + k
                        V.tensor_scalar(S[pair % 2 * 4 + 2 * u + k][:, :], iota[:, :], to_loc[:, bass.ds(e, 1)],
                                        edges[:, bass.ds(e, 1), R_W], ALU.is_equal, ALU.mult).then_inc(S_ready, 1)

            def add(i, pair):
                for u in range(2):
                    g = i * (RING // 2) + pair * 2 + u
                    col = dve.value_load(group_tile_i[0:1, bass.ds(g, 1)], min_val=0, max_val=T - 1) * D
                    made(dve, sum_ready, g, lead=RING // 2)
                    retired(dve, sum_added, g, ring=1, lead=4)
                    V.tensor_tensor(x_flat[:, bass.ds(col, D)], x_flat[:, bass.ds(col, D)],
                                    bank[pair % 2 * 2 + u][:, :], ALU.add).then_inc(sum_added, 1)

            def hidden(i):
                dve.wait_ge(s["soft_ready"], i + 1)
                V.scalar_tensor_tensor(hT[:, bass.ds(i * 4 * P, 4 * P)], pre[:, :], 0.0, soft[:, :],
                                       ALU.max, ALU.add).then_inc(s["hT_ready"], 1)

            def pairs(i, first):
                for pair in range(RING // 4):
                    weights(i, pair)
                    if pair == 0:
                        if not first:
                            add(i - 1, RING // 4 - 1)
                            hidden(i - 1)
                        V.tensor_copy(fr[:, :, :], edges[:, bass.ds(i * RING, RING), R_F:R_F + RT]).then_inc(s["fr_ready"], 1)
                    else:
                        add(i, pair - 1)
                    if pair == 3:
                        dve.wait_ge(s["pre_ps"], i + 1)
                        V.tensor_scalar(pre[:, :], bank[6][:, :], br[:, 0:1], None, ALU.add).then_inc(s["pre_ready"], 1)

            pairs(0, True)
            with dve.Fori(1, ET // RING) as i:
                pairs(i, False)
            add(ET // RING - 1, RING // 4 - 1)
            hidden(ET // RING - 1)

        @block.sync
        def _(sp):
            sorted_rec = v["rec_dram"].rearrange("(p t) c -> p t c", p=P)
            sp.dma_start(edges[:, 0:HEAD, :], sorted_rec[:, 0:HEAD, :]).then_inc(s["edges_in"], 16)
            sp.dma_start(br[:, :], v["br_in"]).then_inc(s["wr_in"], 16)
            sp.wait_ge(s["wr_zero"], 1)
            for k in range(4):
                sp.dma_start(wr[RT * k:RT * k + RT, F * k:F * k + F], v["wr_in"]).then_inc(s["wr_in"], 16)
            sp.wait_ge(s["edges_in"], 16)
            sp.dma_start(edges[:, HEAD:, :], sorted_rec[:, HEAD:, :]).then_inc(s["edges_in"], 16)

        @block.scalar
        def _(act):
            own = Chain(act, s["act_own"])
            with act.Fori(0, ET // RING) as i:
                own.enter(i, 2)
                act.wait_ge(s["fT_ps"], i + 1)
                nc.scalar.activation(fT[:, :], bank[4][0:4 * RT, :], ACT.Copy).then_inc(s["fT_ready"], 1)
                act.wait_ge(s["pre_ready"], i + 1)
                softplus_less_log2(nc, act, own, soft[:, :], soft[:, :], pre[:, :]).then_inc(s["soft_ready"], 1)
                own.leave(ET // RING)

        @block.gpsimd
        def _(gp):
            gp.wait_ge(prepared, 2)
            gather_quads(nc, gp, s, gathered, ET, rows, idx, from_idx, h_dram, sum_ready, 2, rest=(prepared, 3))

        @block.tensor
        def _(pe):
            pe.sem_inc(sum_ready, RING // 2)
            flat = fr[:, :, :].rearrange("p (a b) r -> p a (b r)", b=4)
            pe.wait_ge(s["wr_in"], 80)
            with pe.Fori(0, ET // RING) as i:
                for q in range(RING // 2):
                    g = i * (RING // 2) + q
                    retired(pe, sum_added, g, ring=4, lead=4)
                    for k in range(2):
                        r = 2 * q + k
                        pe.wait_ge(S_ready, g * 2 + k + 1)
                        pe.wait_ge(gathered[r // 4], i * 64 + 64)
                        last = nc.tensor.matmul(bank[q % 4][:, :], S[r % 8][:, :], rows[r // 4][:, r % 4, :], start=(k == 0), stop=(k == 1))
                    last.then_inc(sum_ready, 1)
                    if q == 3:
                        pe.wait_ge(s["fr_ready"], i + 1)
                        for a in range(4):
                            last = nc.tensor.transpose(bank[4][0:4 * RT, a * P:(a + 1) * P], flat[:, a, :], ident[:, :])
                        last.then_inc(s["fT_ps"], 1)
                    if q == 5:
                        pe.wait_ge(s["fT_ready"], i + 1)
                        nc.tensor.matmul(bank[6][:, :], wr[:, :], fT[:, :], start=True, stop=True).then_inc(s["pre_ps"], 1)


def layer0_ffn(nc, v):
    x, ident, iota, stats, mean, rstd = (v[k] for k in ("x", "ident", "iota", "stats", "mean", "rstd"))
    neghalf, shift, bank = v["neghalf"], v["shift"], v["bank"]
    NE, H, GH = 8, 64, 16
    pairs = T // 2
    PARTS = ((0, 2), (2, T))
    with ExitStack() as ctx:
        sb, sem = allocators(nc, ctx, "ffn0")
        w1, w3 = sb("w1", [P, K, D]), sb("w3", [P, K, D])
        wg1, wg2 = sb("wg1", [P, K, GH]), sb("wg2", [GH, NE])
        w2 = sb("w2", [P, K, P])
        b1, b2, g2, be2 = (sb(n, [P, D]) for n in ("b1", "b2", "g2", "be2"))
        gb1 = sb("gb1", [P, 2, K])
        bg1, bg2, b3 = sb("bg1", [GH, 1]), sb("bg2", [P, NE]), sb("b3", [NE, D])
        natural = sb("natural", [P, 2])
        two = range(2)
        xn, hb, hc = ([sb(f"{n}{u}", [P, D]) for u in two] for n in ("xn", "hb", "hc"))
        xT, aT, cT = ([sb(f"{n}{u}", [P, K, P]) for u in two] for n in ("xT", "aT", "cT"))
        gT = [sb(f"gT{u}", [GH, P]) for u in two]
        cwT = [sb(f"cwT{u}", [NE, P]) for u in two]
        lg, top = sb("lg", [P, 2, NE]), sb("top", [P, 2, NE])
        top_i, top_f = sb("top_i", [P, 2, NE], U32), sb("top_f", [P, 2, NE])
        share = sb("share", [P, 2, 4])
        cw, cw2 = sb("cw", [P, 2, NE]), sb("cw2", [P, 2, NE])
        st1, st2 = (sb(n, [P, 2, NE, 6]) for n in ("st1", "st2"))
        ms1, ms2 = (sb(n, [P, 2, 2, NE]) for n in ("ms1", "ms2"))

        names = ("first_in", "weights_in", "w2_zero", "w2_in", "natural_made", "dve_own", "gate", "shift_ready", "var_ready", "rstd_ready",
                 "xn_ready", "xT_ps", "xT_ready", "h1_ps", "gate_ps", "gate_ready", "logit_ps", "logit_taken", "dist_ready", "exp_ready",
                 "cw_ready", "cwT_ps", "cwT_ready", "h1_taken", "var1_ready", "rstd1_ready", "a_ready", "aT_ps", "aT_ready",
                 "h2_ps", "h2_taken", "var2_ready", "rstd2_ready", "c_normed", "c_times_g", "c_scaled", "c_active", "c_ready", "cT_ps", "cT_ready",
                 "o_ps", "x_done")
        s = {n: sem(n) for n in names}
        block = ctx.enter_context(nc.Block())

        @block.sync
        def _(sp):
            for dst, src in ((wg1[:, :, :], v["wg1_in"].rearrange("(k p) e -> p k e", p=P)), (wg2[:, :], v["wg2_in"]),
                             (w1[:, :, :], v["w1_in"].rearrange("(k p) e -> p k e", p=P))):
                sp.dma_start(dst, src).then_inc(s["first_in"], 16)
            for dst, src in ((w3[:, :, :], v["w3_in"].rearrange("(k p) e -> p k e", p=P)),
                             (b1[:, :], v["b1_in"].broadcast_to([P, D])), (b2[:, :], v["b2_in"].broadcast_to([P, D])),
                             (g2[:, :], v["g2_in"].broadcast_to([P, D])), (be2[:, :], v["be2_in"].broadcast_to([P, D])),
                             (gb1[:, :, :], v["gb1_in"]), (bg1[:, :], v["bg1_in"]), (bg2[:, :], v["bg2_in"].broadcast_to([P, NE])),
                             (b3[:, :], v["b3_in"])):
                sp.dma_start(dst, src).then_inc(s["weights_in"], 16)
            sp.wait_ge(s["w2_zero"], 1)
            for e in range(NE):
                q = H * (e % 2)
                sp.dma_start(w2[q:q + H, e // 2, q:q + H], v["w2_in"][e, :, :]).then_inc(s["w2_in"], 16)

        def weights(eng):
            eng.wait_ge(s["weights_in"], 9 * 16)

        def groups(ap):
            return ap.rearrange("p (e h) -> p e h", e=NE)

        @block.gpsimd
        def _(gp):
            G_ = nc.gpsimd
            G_.memset(w2[:, :, :], 0.0).then_inc(s["w2_zero"], 1)
            G_.memset(natural[:, :], float(np.e)).then_inc(s["natural_made"], 1)
            for n in ("rstd1_ready", "rstd2_ready", "exp_ready"):
                gp.sem_inc(s[n], 1)
            for k, (start, end) in enumerate(PARTS):
                gp.wait_ge(s["var_ready"], k + 1)
                G_.tensor_tensor(rstd[:, start:end], rstd[:, start:end], neghalf[:, start:end], ALU.pow).then_inc(s["rstd_ready"], 1)
            weights(gp)
            gp.wait_ge(s["natural_made"], 1)

            def gate_exp(i):
                made(gp, s["dist_ready"], i, lead=1)
                G_.tensor_tensor(share[:, :, 1], natural[:, :], share[:, :, 0], ALU.pow).then_inc(s["exp_ready"], 1)

            def rsqrt1(i):
                made(gp, s["var1_ready"], i, lead=1)
                for u in two:
                    G_.tensor_tensor(ms1[:, u, 1, :], ms1[:, u, 1, :], neghalf[:, 0:NE], ALU.pow).then_inc(s["rstd1_ready"], 1)

            def rsqrt2(i):
                made(gp, s["var2_ready"], i, lead=1)
                for u in two:
                    G_.tensor_tensor(ms2[:, u, 1, :], ms2[:, u, 1, :], neghalf[:, 0:NE], ALU.pow).then_inc(s["rstd2_ready"], 1)

            rsqrt1(0)
            gate_exp(0)
            with gp.Fori(0, pairs - 1) as i:
                rsqrt2(i)
                rsqrt1(i + 1)
                gate_exp(i + 1)
            rsqrt2(pairs - 1)

        @block.vector
        def _(dve):
            V = nc.vector
            own = Chain(dve, s["dve_own"])
            for n in ("logit_taken", "h1_taken", "h2_taken", "a_ready", "c_normed", "c_times_g", "c_scaled", "c_ready", "x_done", "cT_ready"):
                dve.sem_inc(s[n], LEAD)
            for n in ("dist_ready", "cw_ready", "var1_ready", "var2_ready"):
                dve.sem_inc(s[n], 1)
            for k, (start, end) in enumerate(PARTS):
                norm_stats(nc, own, x, stats, mean, rstd, s["var_ready"], tiles=(start, end))
                dve.wait_ge(s["rstd_ready"], k + 1)
                V.scalar_tensor_tensor(shift[:, start:end], mean[:, start:end], -1.0, rstd[:, start:end],
                                       ALU.mult, ALU.mult).then_inc(s["shift_ready"], 1)
            weights(dve)

            def best(i):
                for u in two:
                    made(dve, s["logit_ps"], i * 2 + u)
                    V.tensor_tensor(lg[:, u, :], bank[6 + u][:, P:P + NE], bg2[:, :], ALU.add).then_inc(s["logit_taken"], 1)
                made(dve, s["logit_taken"], i * 2 + 1)
                dve.sem_inc(s["gate"], 1)
                for u in two:
                    own.step(V.max(top[:, u, :], lg[:, u, :]))
                own.wait()
                dve.sem_inc(s["gate"], 1)
                for u in two:
                    own.step(V.max_index(top_i[:, u, :], top[:, u, :], lg[:, u, :]))
                V.tensor_tensor(share[:, :, 0], top[:, :, 1], top[:, :, 0], ALU.subtract).then_inc(s["dist_ready"], 1)

            def shares(i):
                own.wait()
                retired(dve, s["cwT_ps"], i * 2 + 1)
                own.step(V.tensor_copy(top_f[:, :, :], top_i[:, :, :]))
                made(dve, s["exp_ready"], i, lead=1)
                own.link(V.tensor_scalar(share[:, :, 2], share[:, :, 1], 1.0, None, ALU.add))
                own.link(V.reciprocal(share[:, :, 2], share[:, :, 2]))
                own.link(V.tensor_tensor(share[:, :, 3], share[:, :, 2], share[:, :, 1], ALU.mult))
                for u in two:
                    own.step(V.tensor_scalar(cw[:, u, :], iota[:, 0:NE], top_f[:, u, 0:1], share[:, u, 2:3], ALU.is_equal, ALU.mult))
                    own.step(V.tensor_scalar(cw2[:, u, :], iota[:, 0:NE], top_f[:, u, 1:2], share[:, u, 3:4], ALU.is_equal, ALU.mult))
                own.wait()
                V.tensor_tensor(cw[:, :, :], cw[:, :, :], cw2[:, :, :], ALU.add).then_inc(s["cw_ready"], 1)

            def norm(i, h_ps, first, taken, bias, hx, read_by, st, ms, var):
                for u in two:
                    retired(dve, read_by, i * 2 + u)
                    made(dve, h_ps, i * 2 + u)
                    V.tensor_tensor(hx[u][:, :], bank[first + u][:, :], bias[:, :], ALU.add).then_inc(taken, 1)
                for u in two:
                    made(dve, taken, i * 2 + u)
                    for e in range(NE):
                        own.step(V.bn_stats(st[:, u, e, :], hx[u][:, e * H:(e + 1) * H]))
                own.wait()
                me, ve, mo, vo = (st[:, :, :, c] for c in (1, 2, 4, 5))
                m, r = ms[:, :, 0, :], ms[:, :, 1, :]
                own.step(V.tensor_tensor(m, me, mo, ALU.add))
                own.step(V.tensor_tensor(r, me, mo, ALU.subtract))
                own.link(V.tensor_tensor(st[:, :, :, 0], ve, vo, ALU.add))
                own.step(V.tensor_scalar(m, m, 0.5, None, ALU.mult))
                own.link(V.scalar_tensor_tensor(r, r, 0.25, r, ALU.mult, ALU.mult))
                own.link(V.scalar_tensor_tensor(r, st[:, :, :, 0], 1.0 / H, r, ALU.mult, ALU.add))
                V.tensor_scalar(r, r, EPS, None, ALU.add).then_inc(var, 1)
                for u in two:
                    own.step(V.tensor_tensor(groups(hx[u][:, :]), groups(hx[u][:, :]), ms[:, u, 0, :].unsqueeze(2).broadcast_to([P, NE, H]), ALU.subtract))
                own.wait()

            def scale1(i):
                for u in two:
                    made(dve, s["rstd1_ready"], i * 2 + u, lead=1)
                    V.tensor_tensor(groups(hb[u][:, :]), groups(hb[u][:, :]), ms1[:, u, 1, :].unsqueeze(2).broadcast_to([P, NE, H]), ALU.mult).then_inc(s["a_ready"], 1)

            def norm1(i):
                norm(i, s["h1_ps"], 2, s["h1_taken"], b1, hb, s["aT_ps"], st1, ms1, s["var1_ready"])

            def norm2(i):
                norm(i, s["h2_ps"], 4, s["h2_taken"], b2, hc, s["cT_ps"], st2, ms2, s["var2_ready"])

            def scale2(i):
                def times_rstd(u):
                    made(dve, s["rstd2_ready"], i * 2 + u, lead=1)
                    V.tensor_tensor(groups(hc[u][:, :]), groups(hc[u][:, :]), ms2[:, u, 1, :].unsqueeze(2).broadcast_to([P, NE, H]), ALU.mult).then_inc(s["c_normed"], 1)

                def times_g(u):
                    made(dve, s["c_normed"], i * 2 + u)
                    V.tensor_tensor(hc[u][:, :], hc[u][:, :], g2[:, :], ALU.mult).then_inc(s["c_times_g"], 1)

                def plus_be(u):
                    made(dve, s["c_times_g"], i * 2 + u)
                    V.tensor_tensor(hc[u][:, :], hc[u][:, :], be2[:, :], ALU.add).then_inc(s["c_scaled"], 1)

                times_rstd(0)
                times_g(0)
                times_rstd(1)
                plus_be(0)
                times_g(1)
                plus_be(1)

            def weigh(i):
                made(dve, s["cw_ready"], i, lead=1)
                for u in two:
                    made(dve, s["c_active"], i * 2 + u)
                    V.tensor_tensor(groups(hc[u][:, :]), groups(hc[u][:, :]), cw[:, u, :].unsqueeze(2).broadcast_to([P, NE, H]), ALU.mult).then_inc(s["c_ready"], 1)

            def add_out(i):
                for u in two:
                    xt = x[:, bass.ds(i * 2 + u, 1), :].rearrange("p a d -> p (a d)")
                    made(dve, s["o_ps"], i * 2 + u)
                    V.tensor_tensor(xt, xt, bank[4 + u][:, :], ALU.add).then_inc(s["x_done"], 1)
                for u in two:
                    made(dve, s["x_done"], i * 2 + u)
                    own.step(V.bn_stats(stats[:, bass.ds(i * 2 + u, 1), :], x[:, bass.ds(i * 2 + u, 1), :]))

            norm1(0)
            best(0)
            scale1(0)
            shares(0)
            with dve.Fori(0, pairs - 1) as i:
                own.enter(i, 62)
                norm2(i)
                scale2(i)
                weigh(i)
                norm1(i + 1)
                best(i + 1)
                scale1(i + 1)
                shares(i + 1)
                add_out(i)
                own.leave(pairs - 1)
            norm2(pairs - 1)
            scale2(pairs - 1)
            weigh(pairs - 1)
            add_out(pairs - 1)

        @block.scalar
        def _(act):
            A = nc.scalar
            for n in ("xn_ready", "xT_ready", "gate_ready", "cwT_ready", "aT_ready", "c_active"):
                act.sem_inc(s[n], LEAD)
            act.wait_ge(s["shift_ready"], 1)

            def normed(i):
                for u in two:
                    t = i * 2 + u
                    retired(act, s["xT_ps"], t)
                    A.activation(xn[u][:, :], x[:, bass.ds(t, 1), :].rearrange("p a d -> p (a d)"), ACT.Identity,
                                 bias=shift[:, bass.ds(t, 1)], scale=rstd[:, bass.ds(t, 1)]).then_inc(s["xn_ready"], 1)

            def turned(i):
                for u in two:
                    t = i * 2 + u
                    made(act, s["xT_ps"], t)
                    retired(act, s["gate_ps"], t)
                    A.activation(xT[u][:, :, :].rearrange("p k n -> p (k n)"), bank[2 + u][:, :], ACT.Copy).then_inc(s["xT_ready"], 1)

            def gated(i):
                for u in two:
                    t = i * 2 + u
                    made(act, s["gate_ps"], t)
                    retired(act, s["logit_ps"], t)
                    A.activation(gT[u][:, :], bank[6 + u][0:GH, 0:P], ACT.Gelu, bias=bg1[:, 0:1]).then_inc(s["gate_ready"], 1)

            def active(i):
                for u in two:
                    t = i * 2 + u
                    made(act, s["aT_ps"], t)
                    retired(act, s["h2_ps"], t)
                    for c in range(K):
                        last = A.activation(aT[u][:, c, :], bank[u][:, c * P:(c + 1) * P], ACT.Gelu, bias=gb1[:, 1, c:c + 1], scale=gb1[:, 0, c:c + 1])
                    last.then_inc(s["aT_ready"], 1)

            def shares(i):
                for u in two:
                    t = i * 2 + u
                    made(act, s["cwT_ps"], t)
                    retired(act, s["o_ps"], t)
                    A.activation(cwT[u][:, :], bank[6 + u][0:NE, 256:256 + P], ACT.Copy).then_inc(s["cwT_ready"], 1)

            def third(i):
                for u in two:
                    t = i * 2 + u
                    made(act, s["c_scaled"], t)
                    A.activation(hc[u][:, :], hc[u][:, :], ACT.Gelu).then_inc(s["c_active"], 1)
                for u in two:
                    t = i * 2 + u
                    made(act, s["cT_ps"], t)
                    retired(act, s["o_ps"], t)
                    A.activation(cT[u][:, :, :].rearrange("p k n -> p (k n)"), bank[u][:, :], ACT.Copy).then_inc(s["cT_ready"], 1)

            normed(0)
            turned(0)
            weights(act)
            gated(0)
            act.wait_ge(s["shift_ready"], 2)
            with act.Fori(0, pairs - 1) as i:
                normed(i + 1)
                active(i)
                turned(i + 1)
                shares(i)
                gated(i + 1)
                third(i)
            active(pairs - 1)
            shares(pairs - 1)
            third(pairs - 1)

        @block.tensor
        def _(pe):
            M = nc.tensor
            for n in ("xT_ps", "h1_ps", "gate_ps", "logit_ps", "cwT_ps", "aT_ps", "h2_ps", "cT_ps", "o_ps"):
                pe.sem_inc(s[n], LEAD)

            def turn(i, ready, src, done, into=0):
                for u in two:
                    made(pe, ready, i * 2 + u)
                    if into:
                        retired(pe, s["h1_taken"], i * 2 + u)
                    for k in range(K):
                        last = M.transpose(bank[into + u][:, k * P:(k + 1) * P], src[u][:, k * P:(k + 1) * P], ident[:, :])
                    last.then_inc(done, 1)

            def turn_x(i):
                turn(i, s["xn_ready"], xn, s["xT_ps"], into=2)

            def first(i):
                for u in two:
                    t = i * 2 + u
                    made(pe, s["xT_ready"], t)
                    for k in range(K):
                        last = M.matmul(bank[2 + u][:, :], xT[u][:, k, :], w1[:, k, :], start=(k == 0), stop=(k == K - 1))
                    last.then_inc(s["h1_ps"], 1)
                    retired(pe, s["logit_taken"], t)
                    retired(pe, s["cwT_ready"], t)
                    for k in range(K):
                        last = M.matmul(bank[6 + u][0:GH, 0:P], wg1[:, k, :], xT[u][:, k, :], start=(k == 0), stop=(k == K - 1))
                    last.then_inc(s["gate_ps"], 1)
                for u in two:
                    made(pe, s["gate_ready"], i * 2 + u)
                    M.matmul(bank[6 + u][:, P:P + NE], gT[u][:, :], wg2[:, :], start=True, stop=True).then_inc(s["logit_ps"], 1)

            def turn_a(i):
                turn(i, s["a_ready"], hb, s["aT_ps"])

            def second(i):
                made(pe, s["cw_ready"], i, lead=1)
                for u in two:
                    M.transpose(bank[6 + u][0:NE, 256:256 + P], cw[:, u, :], ident[:, :]).then_inc(s["cwT_ps"], 1)
                for u in two:
                    t = i * 2 + u
                    made(pe, s["aT_ready"], t)
                    retired(pe, s["x_done"], t)
                    for c in range(K):
                        last = M.matmul(bank[4 + u][:, c * P:(c + 1) * P], aT[u][:, c, :], w2[:, c, :], start=True, stop=True)
                    last.then_inc(s["h2_ps"], 1)

            def third(i):
                turn(i, s["c_ready"], hc, s["cT_ps"])
                for u in two:
                    t = i * 2 + u
                    made(pe, s["cwT_ready"], t)
                    M.matmul(bank[4 + u][:, :], cwT[u][:, :], b3[:, :], start=True, stop=False)
                    made(pe, s["cT_ready"], t)
                    for c in range(K):
                        last = M.matmul(bank[4 + u][:, :], cT[u][:, c, :], w3[:, c, :], start=False, stop=(c == K - 1))
                    last.then_inc(s["o_ps"], 1)

            turn_x(0)
            pe.wait_ge(s["first_in"], 3 * 16)
            first(0)
            weights(pe)
            pe.wait_ge(s["w2_in"], NE * 16)
            with pe.Fori(0, pairs - 1) as i:
                turn_a(i)
                turn_x(i + 1)
                second(i)
                first(i + 1)
                third(i)
            turn_a(pairs - 1)
            second(pairs - 1)
            third(pairs - 1)


F = 32
AT, RT = 4, 20
LOG2 = float(np.log(2.0))


def layer1_features(nc, v):
    x, ident, stats, mean, rstd = (v[k] for k in ("x", "ident", "stats", "mean", "rstd"))
    neghalf, shift, bank, feat_dram = v["neghalf"], v["shift"], v["bank"], v["feat_dram"]
    two = range(2)
    with ExitStack() as ctx:
        sb, sem = allocators(nc, ctx, "feat1")
        w_in = sb("w_in", [P, 2, F])
        xn = [sb(f"xn{u}", [P, D]) for u in two]
        xT = [sb(f"xT{u}", [P, K, P]) for u in two]
        feat = sb("feat", [P, T, P])
        names = ("weights_in", "dve_own", "var_ready", "rstd_ready", "shift_ready", "xn_ready", "xT_ps", "xT_ready", "feat_ps",
                 "feat_ready", "feat_stored")
        s = {n: sem(n) for n in names}
        block = ctx.enter_context(nc.Block())

        @block.sync
        def _(sp):
            sp.dma_start(w_in[:, :, :], v["w_in_in"]).then_inc(s["weights_in"], 16)
            with sp.Fori(0, T) as t:
                made(sp, s["feat_ready"], t)
                sp.dma_start(feat_dram[bass.ds(t * P, P), :], feat[:, bass.ds(t, 1), :].rearrange("p a d -> p (a d)")).then_inc(s["feat_stored"], 16)
            sp.wait_ge(s["feat_stored"], 16 * T)

        @block.gpsimd
        def _(gp):
            gp.wait_ge(s["var_ready"], 1)
            nc.gpsimd.tensor_tensor(rstd[:, :], rstd[:, :], neghalf[:, 0:T], ALU.pow).then_inc(s["rstd_ready"], 1)

        @block.vector
        def _(dve):
            V = nc.vector
            own = Chain(dve, s["dve_own"])
            dve.sem_inc(s["feat_ready"], LEAD)
            norm_stats(nc, own, x, stats, mean, rstd, s["var_ready"], collected=True)
            dve.wait_ge(s["weights_in"], 16)
            dve.wait_ge(s["rstd_ready"], 1)
            V.scalar_tensor_tensor(shift[:, :], mean[:, :], -1.0, rstd[:, :], ALU.mult, ALU.mult).then_inc(s["shift_ready"], 1)
            with dve.Fori(0, T // 2) as i:
                for u in two:
                    t = i * 2 + u
                    made(dve, s["feat_ps"], t)
                    V.tensor_scalar(feat[:, bass.ds(t, 1), :].rearrange("p a d -> p (a d)"), bank[2 + u][:, 0:P],
                                    float(P) ** -0.5, None, ALU.mult).then_inc(s["feat_ready"], 1)

        @block.scalar
        def _(act):
            A = nc.scalar
            for n in ("xn_ready", "xT_ready"):
                act.sem_inc(s[n], LEAD)
            act.wait_ge(s["shift_ready"], 1)
            with act.Fori(0, T // 2) as i:
                for u in two:
                    t = i * 2 + u
                    retired(act, s["xT_ps"], t)
                    A.activation(xn[u][:, :], x[:, bass.ds(t, 1), :].rearrange("p a d -> p (a d)"), ACT.Identity,
                                 bias=shift[:, bass.ds(t, 1)], scale=rstd[:, bass.ds(t, 1)]).then_inc(s["xn_ready"], 1)
                for u in two:
                    t = i * 2 + u
                    made(act, s["xT_ps"], t)
                    retired(act, s["feat_ps"], t)
                    A.activation(xT[u][:, :, :].rearrange("p k n -> p (k n)"), bank[u][:, :], ACT.Copy).then_inc(s["xT_ready"], 1)

        @block.tensor
        def _(pe):
            M = nc.tensor
            for n in ("xT_ps", "feat_ps"):
                pe.sem_inc(s[n], LEAD)
            pe.wait_ge(s["weights_in"], 16)
            with pe.Fori(0, T // 2) as i:
                for u in two:
                    t = i * 2 + u
                    made(pe, s["xn_ready"], t)
                    for k in range(K):
                        src = xn[u][:, 0:P] if k == 0 else xn[u][:, P + k - 1:D:3]
                        last = M.transpose(bank[u][:, k * P:(k + 1) * P], src, ident[:, :])
                    last.then_inc(s["xT_ps"], 1)
                for u in two:
                    t = i * 2 + u
                    made(pe, s["xT_ready"], t)
                    retired(pe, s["feat_ready"], t)
                    for k in range(K):
                        last = M.matmul(bank[2 + u][:, k * F:(k + 1) * F], xT[u][:, k, :], w_in[:, min(k, 1), :], start=True, stop=True)
                    last.then_inc(s["feat_ps"], 1)


def layer1_edges(nc, v):
    iota, edges, from_idx, to_loc, hT, agg = (v[k] for k in ("iota", "edges", "from_idx", "to_loc", "hT", "agg"))
    group_tile_i, bank, feat_dram = v["group_tile_i"], v["bank"], v["feat_dram"]
    QUADS = 4
    EB = 4 * QUADS
    STEPS = ET // EB
    two = range(2)
    with ExitStack() as ctx:
        sb, sem = allocators(nc, ctx, "edges1")
        w2 = sb("w2", [P, 4 * P])
        PARTS = (0, 32, 64)
        b2, b2_rest = sb("b2", [96, 4 * P]), sb("b2_rest", [96, 4 * P])
        b2_part = [sb(f"b2_part{k}", [96, 4 * P], BF16) for k in range(3)]
        b2_parts = sb("b2_parts", [96, 4 * P], BF16)
        ones = sb("ones", [96, P], BF16)
        hq = [sb(f"hq{u}", [P, P]) for u in two]
        rows = [sb(f"rows{q}", [P, 4, P]) for q in range(QUADS)]
        idx = [sb(f"idx{h}", [P, 16], I32) for h in range(2)]
        attr = [sb(f"attr{u}", [P, 4, 8, F]) for u in two]
        vy = [sb(f"vy{u}", [P, 4, 3, F]) for u in two]
        msg = [sb(f"msg{u}", [P, 4, 8, F]) for u in two]
        hot = [sb(f"hot{u}", [P, 4, P]) for u in two]
        agg_flat = agg[:, :, :].rearrange("p t d -> p (t d)")
        names = ("weights_in", "consts_made", "dve_own", "b2_split", "w2_in", "idx_ready", "gate", "hq_ready", "filter_ps", "hot_ready",
                 "own_attr", "vy_ready", "act_attr", "sum_ready", "agg_zero", "sum_added", "msg_ready")
        s = {n: sem(n) for n in names}
        gathered = [sem(f"gathered{q}") for q in range(QUADS)]
        block = ctx.enter_context(nc.Block())

        @block.sync
        def _(sp):
            sp.dma_start(b2[:, :], v["bf_in"].broadcast_to([96, 4 * P])).then_inc(s["weights_in"], 16)
            sp.wait_ge(s["consts_made"], 3)
            for k in range(4):
                sp.dma_start(w2[F * k:F * k + F, P * k:P * k + P], v["wf_in"]).then_inc(s["w2_in"], 16)

        @block.gpsimd
        def _(gp):
            nc.gpsimd.memset(ones[:, :], 1.0).then_inc(s["consts_made"], 1)
            nc.gpsimd.memset(b2_parts[:, :], 0.0).then_inc(s["consts_made"], 1)
            nc.gpsimd.memset(w2[:, :], 0.0).then_inc(s["consts_made"], 1)
            gather_quads(nc, gp, s, gathered, ET, rows, idx, from_idx, feat_dram, s["msg_ready"], 1)

        @block.vector
        def _(dve):
            V = nc.vector
            own = Chain(dve, s["dve_own"])
            dve.sem_inc(s["msg_ready"], QUADS)
            dve.sem_inc(s["sum_added"], 4)
            own.step(V.memset(agg[:, :, :], 0.0))
            dve.wait_ge(s["weights_in"], 16)
            own.step(V.tensor_copy(b2_part[0][:, :], b2[:, :]))
            V.tensor_tensor(edges[:, :, R_Y:R_Y + AT], edges[:, :, R_Y:R_Y + AT],
                            edges[:, :, R_W:R_W + 1].broadcast_to([P, ET, AT]), ALU.mult).then_inc(s["agg_zero"], 1)
            own.wait()
            dve.wait_ge(s["agg_zero"], 1)
            own.link(V.tensor_tensor(b2_rest[:, :], b2[:, :], b2_part[0][:, :], ALU.subtract))
            own.link(V.tensor_copy(b2_part[1][:, :], b2_rest[:, :]))
            own.link(V.tensor_tensor(b2_part[2][:, :], b2_rest[:, :], b2_part[1][:, :], ALU.subtract))
            dve.wait_ge(s["consts_made"], 3)
            for k, p in enumerate(PARTS):
                V.tensor_copy(b2_parts[p:p + 1, :], b2_part[k][p:p + 1, :]).then_inc(s["b2_split"], 1)

            def add(i, q):
                for g2 in two:
                    g = i * (EB // 2) + q * 2 + g2
                    col = dve.value_load(group_tile_i[0:1, bass.ds(g, 1)], min_val=0, max_val=T - 1) * (8 * F)
                    made(dve, s["sum_ready"], g, lead=4)
                    retired(dve, s["sum_added"], g, ring=1, lead=4)
                    V.tensor_tensor(agg_flat[:, bass.ds(col, 8 * F)], agg_flat[:, bass.ds(col, 8 * F)],
                                    bank[2 * q % 4 + g2][:, 0:8 * F], ALU.add).then_inc(s["sum_added"], 1)

            def messages(i, q):
                n, u = i * QUADS + q, q % 2
                r, a, m = rows[q], attr[u], msg[u]
                y = edges[:, bass.ds(n * 4, 4), R_Y + 1:R_Y + 4]
                retired(dve, s["sum_ready"], n * 2 + 1, ring=4, lead=4)
                V.tensor_tensor(hot[u][:, :, :], iota[:, :].unsqueeze(1).broadcast_to([P, 4, P]),
                                to_loc[:, bass.ds(n * 4, 4)].unsqueeze(2).broadcast_to([P, 4, P]), ALU.is_equal).then_inc(s["hot_ready"], 1)
                dve.wait_ge(gathered[q], i * 64 + 64)
                V.tensor_tensor(a[:, :, 2:8:2, :], r[:, :, 0:F].unsqueeze(2).broadcast_to([P, 4, 3, F]),
                                y.unsqueeze(3).broadcast_to([P, 4, 3, F]), ALU.mult).then_inc(s["own_attr"], 1)
                dve.wait_ge(s["vy_ready"], n + 1)
                V.tensor_reduce(a[:, :, 0, :], vy[u][:, :, :, :].rearrange("p e c f -> p e f c"), AX.X, ALU.add).then_inc(s["own_attr"], 1)
                w = bank[4 + u][:, :].rearrange("p (e x) -> p e x", e=4)
                made(dve, s["filter_ps"], n)
                dve.wait_ge(s["act_attr"], n + 1)
                dve.wait_ge(s["own_attr"], n * 2 + 1)
                V.tensor_tensor(m[:, :, 2:8, :].rearrange("p e (c j) f -> p e c (j f)", c=3), a[:, :, 2:8, :].rearrange("p e (c j) f -> p e c (j f)", c=3),
                                w[:, :, 2 * F:4 * F].unsqueeze(2).broadcast_to([P, 4, 3, 2 * F]), ALU.mult)
                dve.wait_ge(s["own_attr"], n * 2 + 2)
                V.tensor_tensor(m[:, :, 0:2, :].rearrange("p e b f -> p e (b f)"), a[:, :, 0:2, :].rearrange("p e b f -> p e (b f)"),
                                w[:, :, 0:2 * F], ALU.mult).then_inc(s["msg_ready"], 1)

            def quads(i, first):
                for q in range(QUADS):
                    messages(i, q)
                    if q >= 1:
                        add(i, q - 1)
                    elif not first:
                        add(i - 1, QUADS - 1)

            quads(0, True)
            with dve.Fori(1, STEPS) as i:
                quads(i, False)
            add(STEPS - 1, QUADS - 1)

        @block.scalar
        def _(act):
            A = nc.scalar
            act.sem_inc(s["hq_ready"], LEAD)
            act.wait_ge(s["agg_zero"], 1)
            for u in two:
                A.activation(hq[u][:, :], hT[:, u * P:u * P + P], ACT.Copy).then_inc(s["hq_ready"], 1)

            def quads(i, last):
                for q in range(QUADS):
                    n, u = i * QUADS + q, q % 2
                    act.wait_ge(gathered[q], i * 64 + 64)
                    retired(act, s["msg_ready"], n, ring=2, lead=QUADS)
                    for k in range(4):
                        for c in range(3):
                            done = A.activation(vy[u][:, k, c, :], rows[q][:, k, F + c * F:2 * F + c * F], ACT.Copy,
                                                scale=edges[:, bass.ds(n * 4 + k, 1), R_Y + 1 + c])
                    done.then_inc(s["vy_ready"], 1)
                    for k in range(4):
                        done = A.activation(attr[u][:, k, 1:8:2, :], rows[q][:, k, :].rearrange("p (b f) -> p b f", f=F), ACT.Copy,
                                            scale=edges[:, bass.ds(n * 4 + k, 1), R_Y])
                    done.then_inc(s["act_attr"], 1)
                    if not (last and q >= QUADS - 2):
                        made(act, s["filter_ps"], n)
                        A.activation(hq[u][:, :], hT[:, bass.ds((n + 2) * P, P)], ACT.Copy).then_inc(s["hq_ready"], 1)

            with act.Fori(0, STEPS - 1) as i:
                quads(i, False)
            quads(STEPS - 1, True)

        @block.tensor
        def _(pe):
            M = nc.tensor
            pe.sem_inc(s["filter_ps"], LEAD)
            pe.sem_inc(s["sum_ready"], 4)
            pe.wait_ge(s["b2_split"], 3)
            pe.wait_ge(s["w2_in"], 64)

            def filter_(n, u):
                made(pe, s["hq_ready"], n)
                retired(pe, s["msg_ready"], n, ring=2, lead=QUADS)
                M.matmul(bank[4 + u][:, :], ones[:, :], b2_parts[:, :], start=True, stop=False)
                M.matmul(bank[4 + u][:, :], hq[u][:, :], w2[:, :], start=False, stop=True).then_inc(s["filter_ps"], 1)

            def quads(i, last):
                for q in range(QUADS):
                    n, u = i * QUADS + q, q % 2
                    if not (last and q == QUADS - 1):
                        filter_(n + 1, 1 - u)
                    made(pe, s["hot_ready"], n, lead=0)
                    made(pe, s["msg_ready"], n, lead=QUADS)
                    for g2 in two:
                        retired(pe, s["sum_added"], n * 2 + g2, ring=4, lead=4)
                        for k in (2 * g2, 2 * g2 + 1):
                            done = M.matmul(bank[2 * q % 4 + g2][:, 0:8 * F], hot[u][:, k, :], msg[u][:, k, :, :].rearrange("p b f -> p (b f)"),
                                            start=(k % 2 == 0), stop=(k % 2 == 1))
                        done.then_inc(s["sum_ready"], 1)

            filter_(0, 0)
            with pe.Fori(0, STEPS - 1) as i:
                quads(i, False)
            quads(STEPS - 1, True)


def layer1_nodes(nc, v):
    x, ident, agg, bank, stats = (v[k] for k in ("x", "ident", "agg", "bank", "stats"))
    two = range(2)
    with ExitStack() as ctx:
        sb, sem = allocators(nc, ctx, "nodes1")
        w1s = sb("w1s", [2 * F, P])
        w1v = sb("w1v", [P, P])
        w2 = sb("w2", [P, 2, P])
        a = [sb(f"a{u}", [P, 2, P]) for u in two]
        aT = [sb(f"aT{u}", [P, 2, P]) for u in two]
        sT = sb("sT", [P, T, P])
        soft = sb("soft", [P, T, P])
        vT = sb("vT", [P, T, 3, P])
        o = [sb(f"o{u}", [P, 4, P]) for u in two]
        names = ("weights_in", "act_own", "dve_own", "gate", "w1_ready", "a_ready", "aT_ps", "aT_ready", "o1_ps", "s_ready", "v_ready",
                 "soft_ready", "scalars_ready", "o_ready", "o2_ps", "x_s", "x_done")
        s = {n: sem(n) for n in names}
        block = ctx.enter_context(nc.Block())
        half = float(2 * F) ** -0.5

        @block.sync
        def _(sp):
            for dst, src in ((w1s[0:F, :], v["w1s_in"][F:2 * F, :]), (w1s[F:2 * F, :], v["w1s_in"][0:F, :]),
                             (w1v[0:2 * F, :], v["w1v_in"]), (w1v[2 * F:P, :], v["w1v_in"]),
                             (w2[:, 0, :], v["w2s_in"]), (w2[:, 1, :], v["w2v_in"])):
                sp.dma_start(dst, src).then_inc(s["weights_in"], 16)

        @block.gpsimd
        def _(gp):
            gp.sem_inc(s["a_ready"], LEAD)
            gp.sem_inc(s["o_ready"], LEAD)
            with gp.Fori(0, T // 2) as i:
                for u in two:
                    t = i * 2 + u
                    retired(gp, s["aT_ps"], t)
                    gp.sem_inc(s["gate"], 1)
                    nc.gpsimd.tensor_copy(a[u][:, :, :].rearrange("p a b -> p (a b)"), agg[:, bass.ds(t, 1), :].rearrange("p a d -> p (a d)")).then_inc(s["a_ready"], 1)

        @block.vector
        def _(dve):
            V = nc.vector
            own = Chain(dve, s["dve_own"])
            for n in ("s_ready", "x_done", "x_s"):
                dve.sem_inc(s[n], LEAD)
            dve.wait_ge(s["weights_in"], 6 * 16)
            V.tensor_scalar(w1s[0:F, :], w1s[0:F, :], 3.0 ** -0.5, None, ALU.mult).then_inc(s["w1_ready"], 1)
            with dve.Fori(0, T // 2) as i:
                for u in two:
                    t = i * 2 + u
                    made(dve, s["o1_ps"], t)
                    V.tensor_scalar(sT[:, bass.ds(t, 1), :].rearrange("p a d -> p (a d)"), bank[2 + u][:, 0:P], half, None, ALU.mult).then_inc(s["s_ready"], 1)
            dve.wait_ge(s["soft_ready"], 1)
            V.scalar_tensor_tensor(sT[:, :, :], sT[:, :, :], 0.0, soft[:, :, :], ALU.max, ALU.add).then_inc(s["scalars_ready"], 1)
            with dve.Fori(0, T // 2) as i:
                for u in two:
                    t = i * 2 + u
                    made(dve, s["o2_ps"], t)
                    xt = x[:, bass.ds(t, 1), :].rearrange("p a d -> p (a d)")
                    V.scalar_tensor_tensor(xt[:, 0:P], bank[4 + u][:, 0:P], float(P) ** -0.5, xt[:, 0:P], ALU.mult, ALU.add).then_inc(s["x_s"], 1)
                    xv = xt[:, P:D].rearrange("p (d c) -> p c d", c=3)
                    V.scalar_tensor_tensor(xv, bank[4 + u][:, P:D].rearrange("p (c d) -> p c d", c=3), float(P) ** -0.5, xv,
                                           ALU.mult, ALU.add).then_inc(s["x_done"], 1)
                for u in two:
                    t = i * 2 + u
                    made(dve, s["x_s"], t)
                    made(dve, s["x_done"], t)
                    V.bn_stats(stats[:, bass.ds(t, 1), :], x[:, bass.ds(t, 1), :])

        @block.scalar
        def _(act):
            A = nc.scalar
            own = Chain(act, s["act_own"])
            for n in ("aT_ready", "v_ready"):
                act.sem_inc(s[n], LEAD)
            with act.Fori(0, T // 2) as i:
                for u in two:
                    t = i * 2 + u
                    made(act, s["aT_ps"], t)
                    retired(act, s["o1_ps"], t)
                    A.activation(aT[u][:, :, :].rearrange("p a b -> p (a b)"), bank[u][:, 0:2 * P], ACT.Copy).then_inc(s["aT_ready"], 1)
                for u in two:
                    t = i * 2 + u
                    made(act, s["o1_ps"], t)
                    vt = vT[:, bass.ds(t, 1), :, :].rearrange("p a c n -> p (a c) n")
                    A.activation(vt[:, 0:3:2, :], bank[6 + u][:, 0:2 * P].rearrange("p (a b) -> p a b", a=2), ACT.Copy, scale=half)
                    made(act, s["s_ready"], t)
                    A.activation(vt[:, 1, :], bank[2 + u][:, P:2 * P], ACT.Copy, scale=half).then_inc(s["v_ready"], 1)
            act.wait_ge(s["s_ready"], T + LEAD)
            softplus_less_log2(nc, act, own, soft[:, :, :], soft[:, :, :], sT[:, :, :]).then_inc(s["soft_ready"], 1)
            act.wait_ge(s["scalars_ready"], 1)
            with act.Fori(0, T // 2) as i:
                for u in two:
                    t = i * 2 + u
                    retired(act, s["o2_ps"], t)
                    A.activation(o[u][:, 0, :], sT[:, bass.ds(t, 1), :].rearrange("p a d -> p (a d)"), ACT.Copy)
                    A.activation(o[u][:, 1:4, :], vT[:, bass.ds(t, 1), :, :].rearrange("p a c n -> p (a c) n"), ACT.Copy).then_inc(s["o_ready"], 1)

        @block.tensor
        def _(pe):
            M = nc.tensor
            for n in ("aT_ps", "o1_ps", "o2_ps"):
                pe.sem_inc(s[n], LEAD)
            pe.wait_ge(s["weights_in"], 6 * 16)
            pe.wait_ge(s["w1_ready"], 1)

            def turn(i):
                for u in two:
                    t = i * 2 + u
                    made(pe, s["a_ready"], t)
                    retired(pe, s["aT_ready"], t)
                    for k in range(2):
                        last = M.transpose(bank[u][:, k * P:(k + 1) * P], a[u][:, k, :], ident[:, :])
                    last.then_inc(s["aT_ps"], 1)

            def layer(i):
                for u in two:
                    t = i * 2 + u
                    made(pe, s["aT_ready"], t)
                    retired(pe, s["v_ready"], t)
                    for j in range(4):
                        q = 2 * F * (j % 2)
                        lhs = w1s[0:2 * F, :] if j == 0 else w1v[q:q + 2 * F, :]
                        last = M.matmul(bank[2 + u + 4 * (j % 2)][:, j // 2 * P:(j // 2 + 1) * P], lhs, aT[u][q:q + 2 * F, j // 2, :],
                                        start=True, stop=True)
                    last.then_inc(s["o1_ps"], 1)

            turn(0)
            with pe.Fori(0, T // 2 - 1) as i:
                layer(i)
                turn(i + 1)
            layer(T // 2 - 1)
            with pe.Fori(0, T // 2) as i:
                for u in two:
                    t = i * 2 + u
                    made(pe, s["o_ready"], t)
                    retired(pe, s["x_done"], t)
                    for j in range(4):
                        last = M.matmul(bank[4 + u][:, j * P:(j + 1) * P], o[u][:, j, :], w2[:, min(j, 1), :], start=True, stop=True)
                    last.then_inc(s["o2_ps"], 1)


NX, HX, NH = 64, 64, 4
CAP = 4 * N * 2 // NX
NB = 2 * N // P + NX


def layer1_route(nc, v):
    x, ident, iota, stats, mean, rstd = (v[k] for k in ("x", "ident", "iota", "stats", "mean", "rstd"))
    neghalf, shift, bank = v["neghalf"], v["shift"], v["bank"]
    tok_idx, y_idx, gain, block_expert = (v[k] for k in ("tok_idx", "y_idx", "gain", "block_expert"))
    two = range(2)
    with ExitStack() as ctx:
        sb, sem = allocators(nc, ctx, "route1")
        hp = sb("hp", [P, K, NH * NX])
        xn = [sb(f"xn{u}", [P, D]) for u in two]
        xT = [sb(f"xT{u}", [P, K, P]) for u in two]
        xn_all = sb("xn_all", [P, T, D])
        top = [sb(f"top{u}", [P, NH, 8]) for u in two]
        top_i = [sb(f"top_i{u}", [P, NH, 8], U32) for u in two]
        score, expert = sb("score", [P, T, NH]), sb("expert", [P, T, NH])
        before = sb("before", [P, NH, NH])
        beats, ties = sb("beats", [P, T, NH, NH]), sb("ties", [P, T, NH, NH])
        rank = sb("rank", [P, T, NH])
        pick = sb("pick", [P, 2, T, NH])
        sel = sb("sel", [P, 2, T])
        hot = sb("hot", [P, 2, T, NX])
        both = sb("both", [P, T * NX], BF16)
        ahead = sb("ahead", [P, T, NX])
        total = sb("total", [P, T, NX])
        run = sb("run", [P, T + 1, NX])
        place = sb("place", [P, 2, T])
        first = sb("first", [P, 2, T])
        prod = sb("prod", [P, 2, T, NX])
        keep = sb("keep", [P, 2, T])
        small = sb("small", [P, 4, NX])
        nb, bend, bstart, one = (small[:, k, :] for k in range(4))
        nb_i = sb("nb_i", [P, NX], I32)
        slot_i, lo_i, hi_i, row_i = (sb(n, [P, 2, T], I32) for n in ("slot_i", "lo_i", "hi_i", "row_i"))
        row, trash = sb("row", [P, 2, T]), sb("trash", [P, 2, T])
        token = sb("token", [P, T], I32)
        iota_blk = sb("iota_blk", [P, NB])
        bmask = sb("bmask", [P, NB, NX])
        bexp = sb("bexp", [P, NB])
        lower, ones = sb("lower", [P, P], BF16), sb("ones", [P, P], BF16)
        empty = sb("empty", [P, NB], I32)
        names = ("weights_in", "consts_made", "pool_own", "dve_own", "var_ready", "rstd_ready", "shift_ready", "xn_ready", "xn_kept", "xn_stored",
                 "xT_ps", "xT_ready", "logit_ps", "taken", "gate", "both_ready", "sums_ready", "emptied", "row_ready", "placed", "tok_in")
        s = {n: sem(n) for n in names}
        block = ctx.enter_context(nc.Block())

        @block.sync
        def _(sp):
            sp.dma_start(hp[:, :, :], v["hp_in"].rearrange("(k p) e -> p k e", p=P)).then_inc(s["weights_in"], 16)
            with sp.Fori(0, T) as t:
                made(sp, s["xn_kept"], t)
                sp.dma_start(v["xn_dram"][bass.ds(t * P, P), :], xn_all[:, bass.ds(t, 1), :].rearrange("p a d -> p (a d)")).then_inc(s["xn_stored"], 16)
            sp.wait_ge(s["placed"], 16 * 2 * T)
            sp.dma_start(tok_idx[:, 0:NB], v["tok_dram"][0:P * NB, :].rearrange("(p b) a -> p (b a)", p=P)).then_inc(s["tok_in"], 16)
            sp.wait_ge(s["tok_in"], 16)
            sp.wait_ge(s["xn_stored"], 16 * T)

        @block.gpsimd
        def _(gp):
            G_ = nc.gpsimd
            own = Chain(gp, s["pool_own"])
            own.step(G_.memset(ones[:, :], 1.0))
            own.step(G_.memset(before[:, :, :], 1.0))
            own.step(G_.memset(empty[:, :], 0))
            G_.memset(tok_idx[:, :], 0).then_inc(s["consts_made"], 1)
            G_.iota(token[:, :], [[P, T]], base=0, channel_multiplier=1).then_inc(s["consts_made"], 1)
            G_.iota(iota_blk[:, :], [[1, NB]], base=0, channel_multiplier=0, allow_small_or_imprecise_dtypes=True).then_inc(s["consts_made"], 1)
            G_.iota(trash[:, :, :], [[N, 2], [P, T]], base=P * NB, channel_multiplier=1, allow_small_or_imprecise_dtypes=True).then_inc(s["consts_made"], 1)
            own.wait()
            G_.affine_select(out=lower[:, :], in_=ones[:, :], compare_op=ALU.is_gt, fill=0.0, base=0,
                             pattern=[[1, P]], channel_multiplier=-1).then_inc(s["consts_made"], 1)
            G_.affine_select(out=before[:, :, :], in_=before[:, :, :], compare_op=ALU.is_gt, fill=0.0, base=0,
                             pattern=[[1, NH], [-1, NH]], channel_multiplier=0).then_inc(s["consts_made"], 1)
            gp.dma_start(v["tok_dram"][0:P * NB, :].rearrange("(p b) a -> p (b a)", p=P), empty[:, :]).then_inc(s["emptied"], 16)
            gp.wait_ge(s["var_ready"], 1)
            G_.tensor_tensor(rstd[:, :], rstd[:, :], neghalf[:, 0:T], ALU.pow).then_inc(s["rstd_ready"], 1)
            gp.wait_ge(s["emptied"], 16)
            gp.wait_ge(s["row_ready"], 1)
            for k in range(2):
                for t in range(T):
                    gp.indirect_dma_start(out=v["tok_dram"], out_offset=bass.IndirectOffsetOnAxis(ap=row_i[:, k, t:t + 1], axis=0),
                                          in_=token[:, t:t + 1], in_offset=None).then_inc(s["placed"], 16)

        @block.vector
        def _(dve):
            V = nc.vector
            own = Chain(dve, s["dve_own"])
            dve.sem_inc(s["xn_kept"], LEAD)
            dve.sem_inc(s["taken"], LEAD)
            norm_stats(nc, own, x, stats, mean, rstd, s["var_ready"], collected=True)
            dve.wait_ge(s["rstd_ready"], 1)
            V.scalar_tensor_tensor(shift[:, :], mean[:, :], -1.0, rstd[:, :], ALU.mult, ALU.mult).then_inc(s["shift_ready"], 1)
            with dve.Fori(0, T // 2) as i:
                own.enter(i, 16)
                for u in two:
                    t = i * 2 + u
                    V.tensor_scalar(xn_all[:, bass.ds(t, 1), :].rearrange("p a d -> p (a d)"), x[:, bass.ds(t, 1), :].rearrange("p a d -> p (a d)"),
                                    mean[:, bass.ds(t, 1)], rstd[:, bass.ds(t, 1)], ALU.subtract, ALU.mult).then_inc(s["xn_kept"], 1)
                for u in two:
                    t = i * 2 + u
                    made(dve, s["logit_ps"], t)
                    dve.sem_inc(s["gate"], 1)
                    for h in range(NH):
                        own.step(V.max(top[u][:, h, :], bank[2 + u][:, h * NX:(h + 1) * NX]))
                    own.wait()
                    dve.sem_inc(s["gate"], 1)
                    for h in range(NH):
                        own.step(V.max_index(top_i[u][:, h, :], top[u][:, h, :], bank[2 + u][:, h * NX:(h + 1) * NX]))
                    own.wait()
                    V.tensor_copy(score[:, bass.ds(t, 1), :].rearrange("p a h -> p (a h)"), top[u][:, :, 0])
                    V.tensor_copy(expert[:, bass.ds(t, 1), :].rearrange("p a h -> p (a h)"), top_i[u][:, :, 0]).then_inc(s["taken"], 1)
                own.leave(T // 2)
            dve.wait_ge(s["taken"], T + LEAD)
            dve.wait_ge(s["consts_made"], 6)
            mine = score[:, :, :].unsqueeze(3).broadcast_to([P, T, NH, NH])
            other = score[:, :, :].unsqueeze(2).broadcast_to([P, T, NH, NH])
            own.step(V.tensor_tensor(beats[:, :, :, :], other, mine, ALU.is_gt))
            own.link(V.tensor_tensor(ties[:, :, :, :], other, mine, ALU.is_equal))
            own.link(V.tensor_tensor(ties[:, :, :, :], ties[:, :, :, :], before[:, :, :].unsqueeze(1).broadcast_to([P, T, NH, NH]), ALU.mult))
            own.link(V.tensor_tensor(beats[:, :, :, :], beats[:, :, :, :], ties[:, :, :, :], ALU.add))
            own.link(V.tensor_reduce(rank[:, :, :], beats[:, :, :, :], AX.X, ALU.add))
            for k in range(2):
                own.step(V.scalar_tensor_tensor(pick[:, k, :, :], rank[:, :, :], float(k), expert[:, :, :], ALU.is_equal, ALU.mult))
            own.wait()
            own.link(V.tensor_reduce(sel[:, :, :], pick[:, :, :, :], AX.X, ALU.add))
            for k in range(2):
                own.step(V.tensor_tensor(hot[:, k, :, :], sel[:, k, :].unsqueeze(2).broadcast_to([P, T, NX]),
                                         iota[:, 0:NX].unsqueeze(1).broadcast_to([P, T, NX]), ALU.is_equal))
            own.wait()
            V.tensor_tensor(both[:, :].rearrange("p (t e) -> p t e", t=T), hot[:, 0, :, :], hot[:, 1, :, :], ALU.add).then_inc(s["both_ready"], 1)
            own.step(V.memset(run[:, 0, :], 0.0))
            own.step(V.memset(one, 1.0))
            dve.wait_ge(s["sums_ready"], 1)
            for k in range(2):
                own.step(V.tensor_copy(ahead[:, 8 * k:8 * k + 8, :].rearrange("p t e -> p (t e)"), bank[4 + k][:, :]))
                own.step(V.tensor_copy(total[:, 8 * k:8 * k + 8, :].rearrange("p t e -> p (t e)"), bank[6 + k][:, :]))
            own.wait()
            for t in range(T):
                own.link(V.tensor_tensor(run[:, t + 1, :], run[:, t, :], total[:, t, :], ALU.add))
            own.step(V.tensor_tensor(ahead[:, :, :], ahead[:, :, :], run[:, 0:T, :], ALU.add))
            own.link(V.tensor_scalar(nb_i[:, :], run[:, T, :], float(CAP), float(P - 1), ALU.min, ALU.add))
            own.link(V.tensor_scalar(nb_i[:, :], nb_i[:, :], P.bit_length() - 1, None, ALU.arith_shift_right))
            own.link(V.tensor_copy(nb, nb_i[:, :]))
            own.link(V.tensor_tensor_scan(bend, one, nb, 0.0, ALU.mult, ALU.add))
            own.link(V.tensor_tensor(bstart, bend, nb, ALU.subtract))
            own.step(V.tensor_tensor(prod[:, 0, :, :], hot[:, 0, :, :], ahead[:, :, :], ALU.mult))
            own.link(V.tensor_tensor(ahead[:, :, :], ahead[:, :, :], hot[:, 0, :, :], ALU.add))
            own.link(V.tensor_tensor(prod[:, 1, :, :], hot[:, 1, :, :], ahead[:, :, :], ALU.mult))
            own.link(V.tensor_reduce(place[:, :, :], prod[:, :, :, :], AX.X, ALU.add))
            for k in range(2):
                own.step(V.tensor_tensor(prod[:, k, :, :], hot[:, k, :, :], bstart.unsqueeze(1).broadcast_to([P, T, NX]), ALU.mult))
            own.wait()
            own.step(V.tensor_reduce(first[:, :, :], prod[:, :, :, :], AX.X, ALU.add))
            own.link(V.tensor_scalar(keep[:, :, :], place[:, :, :], float(CAP), None, ALU.is_lt))
            own.link(V.scalar_tensor_tensor(place[:, :, :], first[:, :, :], float(P), place[:, :, :], ALU.mult, ALU.add))
            own.link(V.tensor_tensor(place[:, :, :], place[:, :, :], keep[:, :, :], ALU.mult))
            own.step(V.tensor_copy(y_idx[:, 0:2 * T].rearrange("p (t k) -> p k t", k=2), place[:, :, :]))
            own.step(V.memset(y_idx[:, 2 * T:], 0))
            own.step(V.tensor_scalar(gain[:, :].rearrange("p (t k) -> p k t", k=2), keep[:, :, :], 0.5, None, ALU.mult))
            own.link(V.tensor_copy(slot_i[:, :, :], place[:, :, :]))
            own.step(V.tensor_scalar(lo_i[:, :, :], slot_i[:, :, :], P - 1, None, ALU.bitwise_and))
            own.link(V.tensor_scalar(hi_i[:, :, :], slot_i[:, :, :], P.bit_length() - 1, None, ALU.arith_shift_right))
            own.link(V.scalar_tensor_tensor(row[:, :, :], lo_i[:, :, :], float(NB), hi_i[:, :, :], ALU.mult, ALU.add))
            own.link(V.tensor_tensor(row[:, :, :], row[:, :, :], trash[:, :, :], ALU.subtract))
            own.link(V.tensor_tensor(row[:, :, :], row[:, :, :], keep[:, :, :], ALU.mult))
            V.tensor_tensor(row_i[:, :, :], row[:, :, :], trash[:, :, :], ALU.add).then_inc(s["row_ready"], 1)
            own.link(V.tensor_tensor(bmask[:, :, :], iota_blk[:, :].unsqueeze(2).broadcast_to([P, NB, NX]),
                                     bend.unsqueeze(1).broadcast_to([P, NB, NX]), ALU.is_ge))
            own.link(V.tensor_reduce(bexp[:, :], bmask[:, :, :], AX.X, ALU.add))
            own.link(V.tensor_scalar(bexp[:, :], bexp[:, :], float(NX - 1), None, ALU.min))
            own.link(V.tensor_copy(block_expert[:, :], bexp[:, :]))

        @block.scalar
        def _(act):
            A = nc.scalar
            act.sem_inc(s["xn_ready"], LEAD)
            act.sem_inc(s["xT_ready"], LEAD)
            act.wait_ge(s["shift_ready"], 1)
            with act.Fori(0, T // 2) as i:
                for u in two:
                    t = i * 2 + u
                    retired(act, s["xT_ps"], t)
                    A.activation(xn[u][:, :], x[:, bass.ds(t, 1), :].rearrange("p a d -> p (a d)"), ACT.Identity,
                                 bias=shift[:, bass.ds(t, 1)], scale=rstd[:, bass.ds(t, 1)]).then_inc(s["xn_ready"], 1)
                for u in two:
                    t = i * 2 + u
                    made(act, s["xT_ps"], t)
                    retired(act, s["logit_ps"], t)
                    A.activation(xT[u][:, :, :].rearrange("p k n -> p (k n)"), bank[u][:, :], ACT.Copy).then_inc(s["xT_ready"], 1)

        @block.tensor
        def _(pe):
            M = nc.tensor
            pe.sem_inc(s["xT_ps"], LEAD)
            pe.sem_inc(s["logit_ps"], LEAD)
            pe.wait_ge(s["weights_in"], 16)
            with pe.Fori(0, T // 2) as i:
                for u in two:
                    t = i * 2 + u
                    made(pe, s["xn_ready"], t)
                    for k in range(K):
                        last = M.transpose(bank[u][:, k * P:(k + 1) * P], xn[u][:, k * P:(k + 1) * P], ident[:, :])
                    last.then_inc(s["xT_ps"], 1)
                for u in two:
                    t = i * 2 + u
                    made(pe, s["xT_ready"], t)
                    retired(pe, s["taken"], t)
                    for k in range(K):
                        last = M.matmul(bank[2 + u][:, 0:NH * NX], xT[u][:, k, :], hp[:, k, :], start=(k == 0), stop=(k == K - 1))
                    last.then_inc(s["logit_ps"], 1)
            pe.wait_ge(s["consts_made"], 6)
            pe.wait_ge(s["both_ready"], 1)
            for k in range(2):
                M.matmul(bank[4 + k][:, :], lower[:, :], both[:, k * 512:(k + 1) * 512], start=True, stop=True)
                last = M.matmul(bank[6 + k][:, :], ones[:, :], both[:, k * 512:(k + 1) * 512], start=True, stop=True)
            last.then_inc(s["sums_ready"], 1)


def layer1_experts(nc, v):
    ident, bank, tok_idx, block_expert = (v[k] for k in ("ident", "bank", "tok_idx", "block_expert"))
    xn_dram, y_dram = v["xn_dram"], v["y_dram"]
    QUADS = 4
    PAIRS = NB // 2
    DH = D // 2
    two = range(2)
    with ExitStack() as ctx:
        sb, sem = allocators(nc, ctx, "experts1")
        rows = [sb(f"rows{q}", [P, 4, D]) for q in range(QUADS)]
        idx = [sb(f"idx{h}", [P, 16], I32) for h in range(2)]
        w = [sb(f"w{r}", [P, K * HX + DH]) for r in range(4)]
        xT = [sb(f"xT{u}", [P, K, P]) for u in two]
        hT = [sb(f"hT{u}", [P, P]) for u in two]
        y = [sb(f"y{q}", [P, 2, D]) for q in two]
        names = ("idx_ready", "gate", "xT_ps", "xT_ready", "h_ps", "h_ready", "y_ps", "y_ready")
        s = {n: sem(n) for n in names}
        gathered = [sem(f"gathered{q}") for q in range(QUADS)]
        w_in = [sem(f"w_in{r}") for r in range(4)]
        y_stored = [sem(f"y_stored{q}") for q in two]
        block = ctx.enter_context(nc.Block())

        @block.sync
        def _(sp):
            def load(i, q):
                m = i * 2 + q
                retired(sp, s["y_ps"], m)
                for u in two:
                    e = sp.value_load(block_expert[0:1, bass.ds(m * 2 + u, 1)], min_val=0, max_val=NX - 1)
                    sp.dma_start(w[2 * q + u][:, :], v["x12_in"][bass.ds(e, 1), :, :].rearrange("a p c -> (a p) c")).then_inc(w_in[2 * q + u], 16)

            def store(i, q):
                m = i * 2 + q
                made(sp, s["y_ready"], m)
                sp.dma_start(y_dram[bass.ds(m * (2 * P), 2 * P), :].rearrange("(t p) d -> p t d", p=P), y[q][:, :, :]).then_inc(y_stored[q], 16)

            for q in two:
                load(0, q)
            with sp.Fori(1, PAIRS // 2) as i:
                for q in two:
                    load(i, q)
                    store(i - 1, q)
            for q in two:
                store(PAIRS // 2 - 1, q)
            for q in two:
                sp.wait_ge(y_stored[q], 16 * PAIRS // 2)

        @block.gpsimd
        def _(gp):
            gather_quads(nc, gp, s, gathered, NB, rows, idx, tok_idx, xn_dram, s["xT_ps"], 4)

        @block.vector
        def _(dve):
            V = nc.vector
            dve.sem_inc(s["xT_ready"], LEAD)
            dve.sem_inc(s["y_ready"], LEAD)

            def turned(i, q):
                for u in two:
                    b = i * 4 + q * 2 + u
                    made(dve, s["xT_ps"], b, lead=4 * QUADS)
                    retired(dve, s["h_ps"], b)
                    V.tensor_copy(xT[u][:, :, :].rearrange("p k n -> p (k n)"), bank[u][:, :]).then_inc(s["xT_ready"], 1)

            def result(i, q, first):
                made(dve, s["y_ps"], i * 2 + q)
                if not first:
                    dve.wait_ge(y_stored[q], i * 16)
                for h in two:
                    last = V.tensor_copy(y[q][:, :, h * DH:(h + 1) * DH], bank[4 + 2 * q + h][:, :].rearrange("p (t c) -> p t c", c=DH))
                last.then_inc(s["y_ready"], 1)

            turned(0, 0)
            turned(0, 1)
            result(0, 0, True)
            turned(1, 0)
            result(0, 1, True)
            with dve.Fori(1, PAIRS // 2 - 1) as i:
                turned(i, 1)
                result(i, 0, False)
                turned(i + 1, 0)
                result(i, 1, False)
            turned(PAIRS // 2 - 1, 1)
            for q in two:
                result(PAIRS // 2 - 1, q, False)

        @block.scalar
        def _(act):
            act.sem_inc(s["h_ready"], LEAD)
            with act.Fori(0, PAIRS // 4) as i:
                for pair, u in ((k, u) for k in range(4) for u in two):
                    b = (i * 4 + pair) * 2 + u
                    made(act, s["h_ps"], b)
                    retired(act, s["y_ps"], i * 4 + pair, ring=1)
                    nc.scalar.activation(hT[u][0:HX, :], bank[2 + u][0:HX, 0:P], ACT.Gelu)
                    nc.scalar.activation(hT[u][HX:, :], bank[2 + u][0:HX, 0:P], ACT.Gelu).then_inc(s["h_ready"], 1)

        @block.tensor
        def _(pe):
            M = nc.tensor
            pe.sem_inc(s["xT_ps"], 4 * QUADS)
            pe.sem_inc(s["h_ps"], LEAD)
            pe.sem_inc(s["y_ps"], LEAD)

            def turn(i, j):
                for u in two:
                    q, r = j // 2, 2 * (j % 2) + u
                    pe.wait_ge(gathered[q], i * 64 + 64)
                    retired(pe, s["xT_ready"], i * 16 + j * 2 + u)
                    for k in range(K):
                        last = M.transpose(bank[u][:, k * P:(k + 1) * P], rows[q][:, r, k:D:K], ident[:, :])
                    last.then_inc(s["xT_ps"], 1)

            def hidden(i, j):
                for u in two:
                    b, r = i * 16 + j * 2 + u, (2 * j + u) % 4
                    made(pe, s["xT_ready"], b)
                    retired(pe, s["h_ready"], b)
                    pe.wait_ge(w_in[r], (i * 4 + (2 * j + u) // 4) * 16 + 16)
                    for k in range(K):
                        last = M.matmul(bank[2 + u][0:HX, 0:P], w[r][:, k * HX:(k + 1) * HX], xT[u][:, k, :], start=(k == 0), stop=(k == K - 1))
                    last.then_inc(s["h_ps"], 1)

            def result(i, j):
                a, b = bank[4 + 2 * (j % 2)], bank[5 + 2 * (j % 2)]
                retired(pe, s["y_ready"], i * 8 + j)
                for u in two:
                    made(pe, s["h_ready"], i * 16 + j * 2 + u)
                    w2 = w[(2 * j + u) % 4][:, K * HX:]
                    M.matmul(a[:, u * DH:(u + 1) * DH], hT[u][0:HX, :], w2[0:HX, :], start=True, stop=True)
                    last = M.matmul(b[:, u * DH:(u + 1) * DH], hT[u][HX:, :], w2[HX:, :], start=True, stop=True)
                last.then_inc(s["y_ps"], 1)

            steps = NB // 16
            turn(0, 0)
            with pe.Fori(0, steps - 1) as i:
                for j in range(8):
                    hidden(i, j)
                    if j < 7:
                        turn(i, j + 1)
                    else:
                        turn(i + 1, 0)
                    result(i, j)
            for j in range(8):
                hidden(steps - 1, j)
                if j < 7:
                    turn(steps - 1, j + 1)
                result(steps - 1, j)


def layer1_combine(nc, v):
    x, y_idx, gain = (v[k] for k in ("x", "y_idx", "gain"))
    QUADS = 4
    with ExitStack() as ctx:
        sb, sem = allocators(nc, ctx, "combine1")
        rows = [sb(f"rows{q}", [P, 4, D]) for q in range(QUADS)]
        idx = [sb(f"idx{h}", [P, 16], I32) for h in range(2)]
        s = {n: sem(n) for n in ("idx_ready", "gate", "added", "out_stored")}
        gathered = [sem(f"gathered{q}") for q in range(QUADS)]
        block = ctx.enter_context(nc.Block())

        @block.gpsimd
        def _(gp):
            gather_quads(nc, gp, s, gathered, 2 * T, rows, idx, y_idx, v["y_dram"], s["added"], 4)

        @block.vector
        def _(dve):
            dve.sem_inc(s["added"], 4 * QUADS)
            with dve.Fori(0, 2 * T // (4 * QUADS)) as i:
                for r in range(4 * QUADS):
                    n = i * (4 * QUADS) + r
                    dve.wait_ge(gathered[r // 4], i * 64 + 64)
                    xt = x[:, bass.ds(i * (2 * QUADS) + r // 2, 1), :].rearrange("p a d -> p (a d)")
                    if r % 2:
                        made(dve, s["added"], n - 1, lead=4 * QUADS)
                    nc.vector.scalar_tensor_tensor(xt, rows[r // 4][:, r % 4, :], gain[:, bass.ds(n, 1)], xt,
                                                   ALU.mult, ALU.add).then_inc(s["added"], 1)

        @block.sync
        def _(sp):
            with sp.Fori(0, T // 2) as i:
                made(sp, s["added"], i * 4 + 3, lead=4 * QUADS)
                sp.dma_start(v["out"][bass.ds(i * 2 * P, 2 * P), :].rearrange("(t p) d -> p t d", p=P),
                             x[:, bass.ds(i * 2, 2), :]).then_inc(s["out_stored"], 16)
            sp.wait_ge(s["out_stored"], 16 * T // 2)


KINDS = [1, 0, 2, 3]


def dram_inputs(inputs):
    f = {k: np.ascontiguousarray(a) for k, a in inputs.items()}
    w, y, a20 = f["edge_weight"], f["edge_attr_4"], f["edge_attr_20"]
    rec = np.zeros((E, REC), w.dtype)
    rec[:, R_W], rec[:, R_Y:R_Y + 4], rec[:, R_F:R_F + 20] = w, y, a20
    def chunks(a):
        return a.reshape(K, P).T

    laid = {
        "x_in": f["x"], "to_in": f["src"], "from_in": f["dst"], "rec_in": rec, "wg_in": f["L0_gnn_weight"].T,
        "wg1_in": f["L0_ffn_Wg1"], "bg1_in": f["L0_ffn_bg1"].reshape(-1, 1),
        "wg2_in": f["L0_ffn_Wg2"], "bg2_in": f["L0_ffn_bg2"].reshape(1, -1),
        "w1_in": f["L0_ffn_W1"].transpose(1, 0, 2).reshape(D, D), "b1_in": f["L0_ffn_b1"].reshape(1, D),
        "gb1_in": np.stack([chunks(f["L0_ffn_g1"]), chunks(f["L0_ffn_be1"])], axis=1),
        "w2_in": f["L0_ffn_W2"], "b2_in": f["L0_ffn_b2"].reshape(1, D),
        "g2_in": f["L0_ffn_g2"].reshape(1, D), "be2_in": f["L0_ffn_be2"].reshape(1, D),
        "w_in_in": np.stack([f["L1_gnn_w_in2f_s"], f["L1_gnn_w_in2f_v"]], axis=1),
        "wr_in": f["L1_gnn_W1"], "br_in": np.tile(f["L1_gnn_b1"], 4).reshape(P, 1),
        "wf_in": f["L1_gnn_W2"].reshape(F, F, 6)[:, :, KINDS].transpose(0, 2, 1).reshape(F, P),
        "bf_in": np.tile(f["L1_gnn_b2"].reshape(F, 6)[:, KINDS].T.reshape(1, P), (1, 4)),
        "w1s_in": f["L1_gnn_w_f2o1_s"], "w1v_in": f["L1_gnn_w_f2o1_v"],
        "w2s_in": f["L1_gnn_w_f2o2_s"], "w2v_in": f["L1_gnn_w_f2o2_v"],
        "hp_in": f["L1_ffn_hash_proj"].transpose(1, 0, 2).reshape(D, NH * NX),
        "x12_in": np.concatenate([f["L1_ffn_W1"].reshape(NX, P, K * HX),
                                  f["L1_ffn_W2"].reshape(NX, HX, 2, D // 2).transpose(0, 2, 1, 3).reshape(NX, P, D // 2)], axis=2),
        "w3_in": f["L0_ffn_W3"].reshape(D, D), "b3_in": f["L0_ffn_b3"],
    }
    return {k: np.ascontiguousarray(a) for k, a in laid.items()}


def kernel(**inputs):
    import concourse.bacc as bacc
    from concourse.bass_utils import run_bass_kernel_spmd

    nc = bacc.Bacc("TRN2", target_bir_lowering=False, num_devices=1)
    arrays, args = {}, {}
    for name, a in dram_inputs(inputs).items():
        arrays[name] = a
        args[name] = nc.dram_tensor(name, a.shape, mybir.dt.from_np(a.dtype), kind="ExternalInput").ap()
    args["out"] = nc.dram_tensor("out", (N, D), FP32, kind="ExternalOutput").ap()
    build(nc, args)
    r = run_bass_kernel_spmd(nc, [arrays], core_ids=[0])
    return r.results[0]["out"]
```
